# Optimizing a Trainium2 kernel written in Bass

```python
import numpy as np
import jax
import jax.numpy as jnp

def _softmax(x, axis=-1):
    return jax.nn.softmax(x, axis=axis)

def _gelu(x):
    return jax.nn.gelu(x, approximate=True)

def _silu(x):
    return jax.nn.silu(x)

def _sigmoid(x):
    return jax.nn.sigmoid(x)

def _layernorm(x, axis=-1, eps=1e-05):
    m = jnp.mean(x, axis=axis, keepdims=True)
    v = jnp.var(x, axis=axis, keepdims=True)
    return (x - m) / jnp.sqrt(v + eps)

def _scatter_add(tgt, idx, src, axis=0):
    return tgt.at[idx].add(src)

def _segment_sum(src, seg, n):
    return jax.ops.segment_sum(src, seg, n)
kernel_name = 'mk_early_fusion_d1_tok_img768_r4_5a510f'

def setup_inputs(seed: int=0):
    np.random.seed(seed)
    _w = jnp.asarray

    def _rec_inputs():
        import jax
        import jax.numpy as jnp
        _rk = jax.random.key(seed)
        x = 7.57192e-06 + 1.00007 * jax.random.normal(jax.random.fold_in(_rk, 1), (32, 3, 96, 96), jnp.float32)
        txt = 0.282054 + 0.588173 * jax.random.normal(jax.random.fold_in(_rk, 2), (32, 77, 192), jnp.float32)
        return (x, txt)
    x, txt = _rec_inputs()

    def _L0_tok_setup():
        import jax, jax.numpy as jnp
        import numpy as np
        PATCH = 16
        EPS = 1e-05

        def _conv_offsets(x, offset_w, offset_b):
            off = jax.lax.conv_general_dilated(x, offset_w, window_strides=(PATCH, PATCH), padding='VALID', dimension_numbers=('NCHW', 'OIHW', 'NCHW'))
            return off + offset_b[None, :, None, None]

        def _deform_conv(x, offset_w, offset_b, dconv_w):
            B, C, H, W = x.shape
            kh = kw = PATCH
            K = kh * kw
            Ho, Wo = (H // PATCH, W // PATCH)
            off = _conv_offsets(x, offset_w, offset_b)
            off = off.reshape(B, K, 2, Ho, Wo)
            dy = off[:, :, 0].transpose(0, 2, 3, 1)
            dx = off[:, :, 1].transpose(0, 2, 3, 1)
            ii, jj = jnp.meshgrid(jnp.arange(kh), jnp.arange(kw), indexing='ij')
            ki = ii.reshape(-1).astype(x.dtype)
            kj = jj.reshape(-1).astype(x.dtype)
            base_y = (jnp.arange(Ho, dtype=x.dtype) * PATCH)[:, None] + ki[None, :]
            base_x = (jnp.arange(Wo, dtype=x.dtype) * PATCH)[:, None] + kj[None, :]
            py = base_y[None, :, None, :] + dy
            px = base_x[None, None, :, :] + dx
            y0 = jnp.floor(py)
            x0 = jnp.floor(px)
            wy1 = py - y0
            wx1 = px - x0
            wy0 = 1.0 - wy1
            wx0 = 1.0 - wx1
            y0i = y0.astype(jnp.int32)
            x0i = x0.astype(jnp.int32)
            y1i = y0i + 1
            x1i = x0i + 1
            xt = x.transpose(0, 2, 3, 1)
            bidx = jnp.arange(B)[:, None, None, None]

            def gather(yi, xi):
                ok = ((yi >= 0) & (yi < H) & (xi >= 0) & (xi < W)).astype(x.dtype)
                v = xt[bidx, jnp.clip(yi, 0, H - 1), jnp.clip(xi, 0, W - 1)]
                return v * ok[..., None]
            sampled = gather(y0i, x0i) * (wy0 * wx0)[..., None] + gather(y0i, x1i) * (wy0 * wx1)[..., None] + gather(y1i, x0i) * (wy1 * wx0)[..., None] + gather(y1i, x1i) * (wy1 * wx1)[..., None]
            Wk = dconv_w.reshape(dconv_w.shape[0], C, K)
            out = jnp.einsum('bhwkc,ock->bohw', sampled, Wk)
            return out
        key = jax.random.key(seed)
        ks = jax.random.split(key, 3)
        B, C, H, W = (64, 3, 224, 224)
        O = 192
        x = jax.random.normal(ks[0], (B, C, H, W), jnp.float32)
        offset_w = jax.random.normal(ks[1], (2 * PATCH * PATCH, C, PATCH, PATCH), jnp.float32) * 0.01
        offset_b = jnp.zeros((2 * PATCH * PATCH,), jnp.float32)
        dconv_w = jax.random.normal(ks[2], (O, C, PATCH, PATCH), jnp.float32) * 0.02
        bn_gamma = jnp.ones((O,), jnp.float32)
        bn_beta = jnp.zeros((O,), jnp.float32)
        return {'x': x, 'offset_w': offset_w, 'offset_b': offset_b, 'dconv_w': dconv_w, 'bn_gamma': bn_gamma, 'bn_beta': bn_beta}
    _L0_tok_all = _L0_tok_setup()
    _L0_tok_in = {k: v for k, v in _L0_tok_all.items() if k in ('offset_w', 'offset_b', 'dconv_w', 'bn_gamma', 'bn_beta')}
    del _L0_tok_all

    def _L0_attn_setup():
        import jax, jax.numpy as jnp
        import numpy as np
        EMBED_DIM = 192
        MAX_LEN = 256
        ALPHA = 0.99
        BATCH = 16

        def _retention_mask(sl, alpha, dtype):
            i = jnp.arange(sl)[:, None]
            j = jnp.arange(sl)[None, :]
            causal = i >= j
            exponent = jnp.where(causal, (i - j).astype(dtype), 0.0)
            decay = jnp.asarray(alpha, dtype) ** exponent
            return jnp.where(causal, decay, jnp.zeros((), dtype))
        key = jax.random.key(seed)
        k1, k2, k3 = jax.random.split(key, 3)
        x = jax.random.normal(k1, (BATCH, MAX_LEN, EMBED_DIM), dtype=jnp.float32)
        scale = 1.0 / np.sqrt(EMBED_DIM)
        W_qkv = jax.random.uniform(k2, (EMBED_DIM, 3 * EMBED_DIM), dtype=jnp.float32, minval=-scale, maxval=scale)
        b_qkv = jax.random.uniform(k3, (3 * EMBED_DIM,), dtype=jnp.float32, minval=-scale, maxval=scale)
        return {'x': x, 'W_qkv': W_qkv, 'b_qkv': b_qkv}
    _L0_attn_all = _L0_attn_setup()
    _L0_attn_in = {k: v for k, v in _L0_attn_all.items() if k in ('W_qkv', 'b_qkv')}
    del _L0_attn_all

    def _L0_ffn_setup():
        import jax, jax.numpy as jnp
        import numpy as np
        EPS_NORM = 1e-05
        RMS_EPS = 1e-05

        def _l2_normalize(v):
            n = jnp.sqrt(jnp.sum(v * v, axis=-1, keepdims=True))
            return v / jnp.maximum(n, EPS_NORM)

        def _rms_norm(x, weight, eps):
            ms = jnp.mean(x * x, axis=-1, keepdims=True)
            return x * jax.lax.rsqrt(ms + eps) * weight
        key = jax.random.key(seed)
        ks = jax.random.split(key, 6)
        B, T, D = (8, 1024, 192)
        S, F = (64, 768)
        x = jax.random.normal(ks[0], (B, T, D), dtype=jnp.float32)
        slots = 0.02 * jax.random.normal(ks[1], (S, D), dtype=jnp.float32)
        scale = jnp.ones((S,), dtype=jnp.float32)
        fc1_weight = 0.02 * jax.random.normal(ks[2], (S, D, F), dtype=jnp.float32)
        fc1_bias = jnp.zeros((S, F), dtype=jnp.float32)
        fc2_weight = 0.02 * jax.random.normal(ks[3], (S, F, D), dtype=jnp.float32)
        fc2_bias = jnp.zeros((S, D), dtype=jnp.float32)
        norm_weight = jnp.ones((D,), dtype=jnp.float32)
        return {'x': x, 'slots': slots, 'scale': scale, 'fc1_weight': fc1_weight, 'fc1_bias': fc1_bias, 'fc2_weight': fc2_weight, 'fc2_bias': fc2_bias, 'norm_weight': norm_weight}
    _L0_ffn_all = _L0_ffn_setup()
    _L0_ffn_in = {k: v for k, v in _L0_ffn_all.items() if k in ('slots', 'scale', 'fc1_weight', 'fc1_bias', 'fc2_weight', 'fc2_bias', 'norm_weight')}
    del _L0_ffn_all
    return {'x': x, 'txt': txt, 'L0_tok_offset_w': _L0_tok_in['offset_w'], 'L0_tok_offset_b': _L0_tok_in['offset_b'], 'L0_tok_dconv_w': _L0_tok_in['dconv_w'], 'L0_tok_bn_gamma': _L0_tok_in['bn_gamma'], 'L0_tok_bn_beta': _L0_tok_in['bn_beta'], 'L0_attn_W_qkv': _L0_attn_in['W_qkv'], 'L0_attn_b_qkv': _L0_attn_in['b_qkv'], 'L0_ffn_slots': _L0_ffn_in['slots'], 'L0_ffn_scale': _L0_ffn_in['scale'], 'L0_ffn_fc1_weight': _L0_ffn_in['fc1_weight'], 'L0_ffn_fc1_bias': _L0_ffn_in['fc1_bias'], 'L0_ffn_fc2_weight': _L0_ffn_in['fc2_weight'], 'L0_ffn_fc2_bias': _L0_ffn_in['fc2_bias'], 'L0_ffn_norm_weight': _L0_ffn_in['norm_weight']}

def reference(x, txt, L0_tok_offset_w, L0_tok_offset_b, L0_tok_dconv_w, L0_tok_bn_gamma, L0_tok_bn_beta, L0_attn_W_qkv, L0_attn_b_qkv, L0_ffn_slots, L0_ffn_scale, L0_ffn_fc1_weight, L0_ffn_fc1_bias, L0_ffn_fc2_weight, L0_ffn_fc2_bias, L0_ffn_norm_weight):
    import jax
    import jax.numpy as jnp

    def _L0_tok_ref(x, offset_w, offset_b, dconv_w, bn_gamma, bn_beta):
        import jax, jax.numpy as jnp
        import numpy as np
        PATCH = 16
        EPS = 1e-05

        def _conv_offsets(x, offset_w, offset_b):
            off = jax.lax.conv_general_dilated(x, offset_w, window_strides=(PATCH, PATCH), padding='VALID', dimension_numbers=('NCHW', 'OIHW', 'NCHW'))
            return off + offset_b[None, :, None, None]

        def _deform_conv(x, offset_w, offset_b, dconv_w):
            B, C, H, W = x.shape
            kh = kw = PATCH
            K = kh * kw
            Ho, Wo = (H // PATCH, W // PATCH)
            off = _conv_offsets(x, offset_w, offset_b)
            off = off.reshape(B, K, 2, Ho, Wo)
            dy = off[:, :, 0].transpose(0, 2, 3, 1)
            dx = off[:, :, 1].transpose(0, 2, 3, 1)
            ii, jj = jnp.meshgrid(jnp.arange(kh), jnp.arange(kw), indexing='ij')
            ki = ii.reshape(-1).astype(x.dtype)
            kj = jj.reshape(-1).astype(x.dtype)
            base_y = (jnp.arange(Ho, dtype=x.dtype) * PATCH)[:, None] + ki[None, :]
            base_x = (jnp.arange(Wo, dtype=x.dtype) * PATCH)[:, None] + kj[None, :]
            py = base_y[None, :, None, :] + dy
            px = base_x[None, None, :, :] + dx
            y0 = jnp.floor(py)
            x0 = jnp.floor(px)
            wy1 = py - y0
            wx1 = px - x0
            wy0 = 1.0 - wy1
            wx0 = 1.0 - wx1
            y0i = y0.astype(jnp.int32)
            x0i = x0.astype(jnp.int32)
            y1i = y0i + 1
            x1i = x0i + 1
            xt = x.transpose(0, 2, 3, 1)
            bidx = jnp.arange(B)[:, None, None, None]

            def gather(yi, xi):
                ok = ((yi >= 0) & (yi < H) & (xi >= 0) & (xi < W)).astype(x.dtype)
                v = xt[bidx, jnp.clip(yi, 0, H - 1), jnp.clip(xi, 0, W - 1)]
                return v * ok[..., None]
            sampled = gather(y0i, x0i) * (wy0 * wx0)[..., None] + gather(y0i, x1i) * (wy0 * wx1)[..., None] + gather(y1i, x0i) * (wy1 * wx0)[..., None] + gather(y1i, x1i) * (wy1 * wx1)[..., None]
            Wk = dconv_w.reshape(dconv_w.shape[0], C, K)
            out = jnp.einsum('bhwkc,ock->bohw', sampled, Wk)
            return out
        B = x.shape[0]
        y = _deform_conv(x, offset_w, offset_b, dconv_w)
        mean = jnp.mean(y, axis=(0, 2, 3), keepdims=True)
        var = jnp.mean((y - mean) ** 2, axis=(0, 2, 3), keepdims=True)
        yn = (y - mean) * jax.lax.rsqrt(var + EPS)
        yn = yn * bn_gamma[None, :, None, None] + bn_beta[None, :, None, None]
        ya = jax.nn.gelu(yn, approximate=False)
        O, Ho, Wo = (ya.shape[1], ya.shape[2], ya.shape[3])
        return ya.reshape(B, O, Ho * Wo).transpose(0, 2, 1)

    def _L0_attn_ref(x, W_qkv, b_qkv):
        import jax, jax.numpy as jnp
        import numpy as np
        EMBED_DIM = 192
        MAX_LEN = 256
        ALPHA = 0.99
        BATCH = 16

        def _retention_mask(sl, alpha, dtype):
            i = jnp.arange(sl)[:, None]
            j = jnp.arange(sl)[None, :]
            causal = i >= j
            exponent = jnp.where(causal, (i - j).astype(dtype), 0.0)
            decay = jnp.asarray(alpha, dtype) ** exponent
            return jnp.where(causal, decay, jnp.zeros((), dtype))
        bs, sl, d = x.shape
        qkv = x @ W_qkv + b_qkv
        q, k, v = jnp.split(qkv, 3, axis=-1)
        M = _retention_mask(sl, ALPHA, x.dtype)
        scores = jnp.einsum('bsd,btd->bst', q, k) / jnp.sqrt(jnp.asarray(d, x.dtype))
        out = jnp.einsum('bst,btd->bsd', scores * M[None, :, :], v)
        return out

    def _L0_ffn_ref(x, slots, scale, fc1_weight, fc1_bias, fc2_weight, fc2_bias, norm_weight):
        import jax, jax.numpy as jnp
        import numpy as np
        EPS_NORM = 1e-05
        RMS_EPS = 1e-05

        def _l2_normalize(v):
            n = jnp.sqrt(jnp.sum(v * v, axis=-1, keepdims=True))
            return v / jnp.maximum(n, EPS_NORM)

        def _rms_norm(x, weight, eps):
            ms = jnp.mean(x * x, axis=-1, keepdims=True)
            return x * jax.lax.rsqrt(ms + eps) * weight
        xn = _rms_norm(x, norm_weight, RMS_EPS)
        tok = _l2_normalize(xn)
        sl = _l2_normalize(slots) * scale[:, None]
        logits = jnp.einsum('sd,btd->bst', sl, tok)
        dispatch_w = jax.nn.softmax(logits, axis=-1)
        combine_w = jax.nn.softmax(logits, axis=-2)
        y = jnp.einsum('btd,bst->bsd', xn, dispatch_w)
        y = jnp.einsum('sio,bsi->bso', fc1_weight, y) + fc1_bias
        y = jax.nn.gelu(y, approximate=False)
        y = jnp.einsum('sio,bsi->bso', fc2_weight, y) + fc2_bias
        out = jnp.einsum('bsd,bst->btd', y, combine_w)
        return out
    h = _L0_tok_ref(x, L0_tok_offset_w, L0_tok_offset_b, L0_tok_dconv_w, L0_tok_bn_gamma, L0_tok_bn_beta)
    h = jnp.concatenate([h, txt], axis=1)
    h = h + _L0_attn_ref(_layernorm(h, axis=-1), L0_attn_W_qkv, L0_attn_b_qkv)
    h = h + _L0_ffn_ref(_layernorm(h, axis=-1), L0_ffn_slots, L0_ffn_scale, L0_ffn_fc1_weight, L0_ffn_fc1_bias, L0_ffn_fc2_weight, L0_ffn_fc2_bias, L0_ffn_norm_weight)
    return h

_drawn_inputs = setup_inputs


def setup_inputs(seed=0):
    import zlib

    import numpy as np

    out = dict(_drawn_inputs(seed))
    spreads = {'L0_tok_offset_b': (0.0, 0.1),
     'L0_tok_bn_gamma': (1.0, 0.2),
     'L0_tok_bn_beta': (0.0, 0.1),
     'L0_ffn_scale': (1.0, 0.6),
     'L0_ffn_fc1_bias': (0.0, 0.8),
     'L0_ffn_fc2_bias': (0.0, 0.8),
     'L0_ffn_norm_weight': (1.0, 0.6)}
    factors = {'L0_ffn_slots': 8.0, 'L0_ffn_fc1_weight': 8.0, 'L0_ffn_fc2_weight': 8.0}
    for name, (base, spread) in spreads.items():
        noise = np.random.default_rng([zlib.crc32(name.encode()), seed]).standard_normal(out[name].shape)
        drawn = base * np.exp(spread * noise) if base else spread * noise
        out[name] = jnp.asarray(drawn.astype(out[name].dtype))
    for name, factor in factors.items():
        out[name] = (out[name] * factor).astype(out[name].dtype)
    return out
```

```python
import numpy as np

import concourse.bass as bass
from concourse import mybir
from contextlib import ExitStack

B, C, IMG, PATCH = 32, 3, 96, 16
D, TXT, SLOTS, FF = 192, 77, 64, 768
PT = 6
HT = PT // 2
TOK = PT * PT + TXT
RAD = 2
WIN = 2 * RAD + 1
QW = HT * PATCH
HALO = QW + 2 * RAD
NPOS = PATCH * QW
KK = PATCH * PATCH
KC = C * KK // 128
TAPS = WIN * WIN
DC = D // 2
NG = B // 2
T2 = 2 * TOK
MS = 4
MG = SLOTS // MS
FT = FF // 128
ALPHA, EPS = 0.99, 1e-5
POOL_TAPS = 8


def fusion_program(nc, x_halo, x_cols, x_flat, w_off, b_off, w_conv, bn_g, bn_b, txt, w_qkv, b_qk, b_v,
                   slots, scale, fc1, fc1_b, fc2, fc2_b, norm_w, ident_in, decay_in, grid_in, corner_in, out):
    f32, i32, u32 = mybir.dt.float32, mybir.dt.int32, mybir.dt.uint32
    ALU, ACT, AX = mybir.AluOpType, mybir.ActivationFunctionType, mybir.AxisListType
    ctx = ExitStack()
    with ctx:
        KEEP, SHARED = 3200, 48896
        arena = ctx.enter_context(nc.sbuf_tensor("arena", [128, KEEP + SHARED], f32))
        place = {"at": 0, "end": KEEP}

        def region(at, end):
            place["at"], place["end"] = at, end

        def carve(parts, *shape):
            n = int(np.prod(shape))
            at = place["at"]
            place["at"] = at + n
            assert place["at"] <= place["end"], (place, shape)
            v = arena[0:parts, at:at + n]
            names = "abcde"[:len(shape)]
            if len(shape) == 1:
                return v
            return v.rearrange("p (" + " ".join(names) + ") -> p " + " ".join(names),
                               **{names[i]: shape[i] for i in range(len(shape))})

        ident = carve(128, 128)
        decay = carve(TOK, TOK)
        wqkv = carve(DC, 2, 3 * D)
        bqk = carve(DC, 4)
        bv = carve(TOK, D)
        normw = carve(TOK, D)
        gam, bet = carve(DC, 2), carve(DC, 2)
        slotv, slotsc = carve(SLOTS, D), carve(SLOTS, 1)
        slot_sq, slot_f = carve(SLOTS, 1), carve(SLOTS, 1)
        slotn = carve(SLOTS, D)
        slotT = carve(DC, 2, SLOTS)
        half_neg = carve(128, 2)
        bn6, bn2 = carve(DC, 2, HT, 6), carve(DC, 2, 2)
        bn_r, bn_s, bn_t = carve(DC, 2), carve(DC, 2), carve(DC, 2)
        off_max, off_all = carve(128, HT), carve(128, HT)
        st6 = carve(TOK, 4, 2, 6)
        mv1, mv2 = carve(TOK, 4, 2, 2), carve(TOK, 16, 2, 2)
        r1 = carve(TOK, 4, 2)
        a2 = carve(TOK, 16, 2)
        ssq, f2 = carve(TOK, 4, 2), carve(TOK, 4, 2)
        tmp2 = carve(TOK, 4, 2)
        nmax1, sum1 = carve(SLOTS, 4, 2), carve(SLOTS, 4, 2)
        nmax2 = carve(TOK, 4, 2)
        sum2, rsum2 = carve(TOK, B), carve(TOK, B)
        rsum1 = carve(SLOTS, 4, 2)

        region(KEEP, KEEP + SHARED)
        xh = carve(128, C, HT, HALO, PATCH + 2 * RAD)
        xc = carve(128, 2, KC, HT, 128)
        woff = carve(128, KC, 2 * KK)
        boff = carve(128, 2 * KK)
        wcv = carve(128, KC, D)
        off = carve(128, 2, 2, HT, KK)
        haty = carve(128, 2, HT, KK)
        hatx = carve(128, WIN, HT, KK)
        hat_t = carve(128, 2, HT, KK)
        prod_v = carve(128, 2, C, HT, KK)
        pool_at = place["at"]
        prod_p = carve(128, 2, C, HT, KK)
        w_p = carve(128, HT, KK)
        gen_more = carve(128, 4, NPOS)
        gen = arena[:, pool_at:pool_at + 11 * NPOS].rearrange("p (a n) -> p a n", n=NPOS)
        outl = carve(128, C, HT, KK)
        corner = carve(128, 12)
        corner_at, corner_idx = carve(128, 12), carve(128, 12)
        corner_val, corner_wv, corner_s = carve(128, C, 4), carve(128, C, 4), carve(128, C, 2)
        samp = carve(128, KC, HT, 128)
        convs = carve(DC, 2, HT, HT * 128)

        region(KEEP, KEEP + SHARED)
        h = carve(TOK, B, D)
        patch_tok = carve(DC, 2, B, PT * PT)
        F2R = 2
        f1w = carve(DC + 1, 2, MS, 2, FF)
        f2w = carve(128, F2R, MS, FT, D)
        yT = carve(DC + 1, 2, SLOTS, B)
        temps_at = place["at"]
        xl = carve(TOK, 2, 2, D)
        xlT = carve(DC, 2, 2, T2)
        qkT = carve(DC, 2, 4, T2)
        vt = carve(TOK, 3, 2, D)
        pt = carve(TOK, 2, 2, TOK)
        z = carve(TOK, 3, 2, D)
        tk = carve(TOK, 2, 2, D)
        tkT = carve(DC, 2, 2, T2)
        e1 = carve(SLOTS, 3, 2, TOK)
        e2 = carve(TOK, 2, 2, SLOTS)
        dT = carve(TOK, 2, 2, SLOTS)
        xn = carve(TOK, 2, 2, D)
        temps_end = place["at"]
        combT = carve(SLOTS, B, TOK)
        region(temps_at, KEEP + SHARED)
        ybuf = carve(SLOTS, B, D)
        g1 = carve(128, 1, FF)
        g1T = carve(128, 1, FT, 128)
        y2 = carve(128, 2, D)
        b2 = carve(128, 2, D)
        assert place["at"] <= temps_end

        psum = ctx.enter_context(nc.psum_tensor("psum", [128, 8 * 512], f32))
        bank = lambda n: psum[:, 512 * n:512 * n + 512]

        acc = psum[:, 0:KC * HT * 128]
        w_v = psum[:, 5 * 512:5 * 512 + HT * KK].rearrange("p (w q) -> p w q", q=KK)
        off_ps = conv_ps = bank(7)
        tok_ps = bank(0)[0:PT * PT, 0:2 * D].rearrange("p (b d) -> p b d", d=D)
        l2_ps = bank(0)[0:TOK, 256:256 + 2 * SLOTS].rearrange("p (b s) -> p b s", s=SLOTS)
        tr_ps = bank(1)[0:DC, 0:2 * T2].rearrange("p (j t) -> p j t", t=T2)
        qk_ps = [bank(2 + m // 2)[0:DC, (m % 2) * T2:(m % 2 + 1) * T2] for m in range(4)]
        v_ps = bank(4)[0:TOK, 0:2 * D].rearrange("p (b d) -> p b d", d=D)
        dT_ps = bank(7)[0:TOK, 0:2 * SLOTS].rearrange("p (b s) -> p b s", s=SLOTS)
        s_ps = bank(5)[0:TOK, 0:T2].rearrange("p (b t) -> p b t", t=TOK)
        y_ps = bank(5)[0:DC, 256:512].rearrange("p (b j s) -> p b j s", b=2, j=2)
        o_ps = bank(6)[0:TOK, 0:2 * D].rearrange("p (b d) -> p b d", d=D)
        l1_ps = bank(0)[0:SLOTS, 0:T2].rearrange("p (b t) -> p b t", t=TOK)
        cT_ps = bank(7)[0:SLOTS, 256:256 + T2].rearrange("p (b t) -> p b t", t=TOK)
        h1_ps = [psum[:, 1024 * q:1024 * q + 1024].rearrange("p (a n) -> p a n", n=512)[:, :, 0:FF // 2] for q in range(2)]
        h1T_ps = psum[:, 2048:2048 + FT * 128]
        y2_ps = bank(6)[:, 0:D]
        fin_ps = [bank(6)[0:TOK, 0:2 * D].rearrange("p (b d) -> p b d", d=D),
                  bank(7)[0:TOK, 0:2 * D].rearrange("p (b d) -> p b d", d=D)]

        def sem(name):
            return ctx.enter_context(nc.semaphore(name))

        ld_x, ld_w, ld_cols, ld_const = sem("ld_x"), sem("ld_w"), [sem("ld_cols0"), sem("ld_cols1")], sem("ld_const")
        ld_txt = sem("ld_txt")
        ld_f1, ld_f2 = [sem(f"ld_f1_{i}") for i in range(2)], [sem(f"ld_f2_{i}") for i in range(F2R)]
        ld_b2 = [sem(f"ld_b2_{i}") for i in range(2)]
        off_done, off_taken, off_maxed, off_checked = sem("off_done"), sem("off_taken"), sem("off_maxed"), sem("off_checked")
        hats, prod_v_done, prod_p_done = sem("hats"), sem("prod_v_done"), sem("prod_p_done")
        prod_v_used, prod_p_used, outl_used = sem("prod_v_used"), sem("prod_p_used"), sem("outl_used")
        samp_done, conv_done, conv_taken = sem("samp_done"), sem("conv_done"), sem("conv_taken")
        bn_var, bn_rstd, bn_affine, patches = sem("bn_var"), sem("bn_rstd"), sem("bn_affine"), sem("patches")
        gathered, grid_in_sb = sem("gathered"), sem("grid_in_sb")
        slot_sqd, slot_fd, slot_nd, slot_td, slot_td2 = sem("slot_sqd"), sem("slot_fd"), sem("slot_nd"), sem("slot_td"), sem("slot_td2")
        consts_made = sem("consts_made")
        v_step, a_step, g_step = sem("v_step"), sem("a_step"), sem("g_step")
        names = ("tokT_done h_patches var1_done rstd1_done xl_done xlT_done xlT_taken qk_done qk_taken "
                 "vproj_done v_taken score_done probs_done attn_done h_done var2_done a2_done z_done ssq_done f2_done "
                 "tok_done tkT_done tkT_taken logits_done max_done exp1_done exp2_done disp_done "
                 "cT_done dT_taken cT_taken xn_done y_done y_taken")
        s = {n: sem(n) for n in names.split()}
        fc1_done, gelu_done, h1T_done, h1T_taken, fc2_done, y2_done = (sem(n) for n in ("fc1_done", "gelu_done", "h1T_done", "h1T_taken", "fc2_done", "y2_done"))
        y_moved = [sem("y_moved0"), sem("y_moved1")]
        fin_done, out_done, stored = sem("fin_done"), sem("out_done"), sem("stored")

        def tap_owner(t):
            return "pool" if t % 3 == 2 and t // 3 < POOL_TAPS else "vector"
        OWN = [tap_owner(t) for t in range(TAPS)]
        V_TAPS = OWN.count("vector")

        def nth(t):
            return OWN[:t].count(OWN[t])

        def hat_count(ck, i, j):
            return ck * 2 * WIN + (max(1, j + 2) if i == 0 else WIN + 1 + i)

        def window(ck, i, j):
            return xh[:, :, :, PATCH * ck + i:PATCH * ck + i + PATCH, j:j + PATCH]

        def bcast_c(w):
            return pixels(w.unsqueeze(1).broadcast_to([128, C, HT, KK]))

        def pixels(v):
            return v.rearrange("p c w (r q) -> p c w r q", q=PATCH)

        def steps(g_of_stage):
            last = max(lag for _, lag in g_of_stage)
            for t in range(NG + last):
                for stage, lag in g_of_stage:
                    if 0 <= t - lag < NG:
                        yield stage, t - lag

        block = ctx.enter_context(nc.Block())

        @block.sync
        def _(sp):
            sp.dma_start(xc[:, 0], x_cols[0]).then_inc(ld_cols[0], 16)
            sp.dma_start(woff, w_off).then_inc(ld_w, 16)
            sp.dma_start(boff, b_off.partition_broadcast(128)).then_inc(ld_w, 16)
            sp.dma_start(ident, ident_in).then_inc(ld_w, 16)
            sp.dma_start(xh.rearrange("p c w r q -> p (c w r q)"), x_halo.rearrange("p c w r q -> p (c w r q)")).then_inc(ld_x, 16)
            sp.dma_start(xc[:, 1], x_cols[1]).then_inc(ld_cols[1], 16)
            sp.dma_start(wcv, w_conv).then_inc(ld_const, 16)
            sp.dma_start(corner, corner_in).then_inc(ld_const, 16)
            sp.dma_start(decay, decay_in).then_inc(ld_const, 16)
            sp.dma_start(wqkv, w_qkv).then_inc(ld_const, 16)
            sp.dma_start(bqk, b_qk).then_inc(ld_const, 16)
            sp.dma_start(bv, b_v.partition_broadcast(TOK)).then_inc(ld_const, 16)
            sp.dma_start(normw, norm_w.partition_broadcast(TOK)).then_inc(ld_const, 16)
            sp.dma_start(gam, bn_g).then_inc(ld_const, 16)
            sp.dma_start(bet, bn_b).then_inc(ld_const, 16)
            sp.dma_start(slotv, slots).then_inc(ld_const, 16)
            sp.dma_start(slotsc, scale).then_inc(ld_const, 16)
            sp.wait_ge(off_done, HT)
            sp.dma_start(xc[:, 0], x_cols[2]).then_inc(ld_cols[0], 16)
            sp.wait_ge(samp_done, HT)
            sp.dma_start(h[PT * PT:TOK, :, :], txt.rearrange("b t d -> t b d")).then_inc(ld_txt, 16)

            sp.wait_ge(conv_taken, 2 * HT)
            for q in range(MG):
                if q >= 2:
                    sp.wait_ge(fc1_done, q - 1)
                sp.dma_start(f1w[0:DC, q % 2], fc1[MS * q:MS * q + MS].rearrange("s p j f -> p s j f")).then_inc(ld_f1[q % 2], 16)
                sp.dma_start(f1w[DC:DC + 1, q % 2, :, 0, :], fc1_b[MS * q:MS * q + MS].unsqueeze(0)).then_inc(ld_f1[q % 2], 16)
                if q >= F2R:
                    sp.wait_ge(fc2_done, q - F2R + 1)
                sp.dma_start(f2w[:, q % F2R], fc2[MS * q:MS * q + MS].rearrange("s p j d -> p s j d")).then_inc(ld_f2[q % F2R], 16)
            sp.wait_ge(stored, 16 * 2 * NG)

        @block.tensor
        def _(pe):
            def offsets(ck):
                pe.wait_ge(ld_cols[ck % 2], 16 * (ck // 2 + 1))
                for wt in range(HT):
                    n = HT * ck + wt
                    if n:
                        pe.wait_ge(off_taken, n)
                    if ck >= 2:
                        pe.wait_ge(conv_taken, 2 * (ck - 1))
                    for k in range(KC):
                        last = nc.tensor.matmul(off_ps, xc[:, ck % 2, k, wt, :], woff[:, k, :], start=(k == 0), stop=(k == KC - 1))
                    last.then_inc(off_done, 1)
                    yield

            def transposed_sum(src, first):
                for n in range(KC * HT):
                    k, wt = n // HT, n % HT
                    c, half = k // 2, k % 2
                    piece = src[:, c, wt, 128 * half:128 * half + 128]
                    last = nc.tensor.matmul(acc[:, 128 * n:128 * n + 128], piece, ident,
                                            start=(first and n % 4 == 0), stop=True, skip_group_check=True)
                return last

            pe.wait_ge(ld_w, 48)
            for _ in offsets(0):
                pass
            for ck in range(HT):
                nxt = offsets(ck + 1) if ck + 1 < HT else None
                if ck:
                    pe.wait_ge(samp_done, ck)
                pe.wait_ge(off_checked, ck + 1)
                transposed_sum(outl, True).then_inc(outl_used, 1)
                for t in range(TAPS):
                    if OWN[t] == "vector":
                        n = V_TAPS * ck + nth(t)
                        pe.wait_ge(prod_v_done, n + 1)
                        last = transposed_sum(prod_v[:, n % 2], False)
                        last.then_inc(prod_v_used, 1)
                    else:
                        n = POOL_TAPS * ck + nth(t)
                        pe.wait_ge(prod_p_done, n + 1)
                        last = transposed_sum(prod_p[:, n % 2], False)
                        last.then_inc(prod_p_used, 1)
                    if nxt is not None and t in (3, 8, 13):
                        next(nxt)
                pe.wait_ge(samp_done, ck + 1)
                if ck == 0:
                    pe.wait_ge(ld_const, 16 * 11)
                pe.wait_ge(off_taken, HT * min(ck + 2, HT))
                for oc in range(2):
                    if 2 * ck + oc:
                        pe.wait_ge(conv_taken, 2 * ck + oc)
                    for k in range(KC):
                        last = nc.tensor.matmul(conv_ps[0:DC, 0:HT * 128], wcv[:, k, DC * oc:DC * oc + DC],
                                                samp[:, k].rearrange("p w n -> p (w n)"), start=(k == 0), stop=(k == KC - 1))
                    last.then_inc(conv_done, 1)

            pe.wait_ge(slot_nd, 1)
            pe.wait_ge(conv_taken, 2 * HT)
            for j in range(2):
                last = nc.tensor.transpose(conv_ps[0:DC, SLOTS * j:SLOTS * j + SLOTS], slotn[:, DC * j:DC * j + DC], ident[0:SLOTS, 0:SLOTS])
            last.then_inc(slot_td, 1)
            pe.wait_ge(slot_td2, 1)
            pe.wait_ge(patches, 1)

            def back_to_tokens(g):
                if g:
                    pe.wait_ge(s["h_patches"], g)
                if g >= 7:
                    pe.wait_ge(s["exp2_done"], g - 6)
                for b in range(2):
                    for j in range(2):
                        last = nc.tensor.transpose(tok_ps[:, b, DC * j:DC * j + DC], patch_tok[:, j, 2 * g + b, :], ident[0:DC, 0:DC])
                last.then_inc(s["tokT_done"], 1)

            def normed_transpose(g):
                pe.wait_ge(s["xl_done"], g + 1)
                if g >= 1:
                    pe.wait_ge(s["xlT_taken"], g)
                if g >= 5:
                    pe.wait_ge(s["tkT_taken"], g - 4)
                for j in range(2):
                    for b in range(2):
                        last = nc.tensor.transpose(tr_ps[:, j, TOK * b:TOK * b + TOK], xl[:, g % 2, b, DC * j:DC * j + DC], ident[0:TOK, 0:TOK])
                last.then_inc(s["xlT_done"], 1)

            def project(g):
                pe.wait_ge(s["xlT_taken"], g + 1)
                if g:
                    pe.wait_ge(s["qk_taken"], g)
                for m in range(4):
                    for j in range(2):
                        last = nc.tensor.matmul(qk_ps[m], wqkv[:, j, DC * m:DC * m + DC], xlT[:, g % 2, j, :], start=(j == 0), stop=(j == 1))
                last.then_inc(s["qk_done"], 1)
                if g:
                    pe.wait_ge(s["v_taken"], g)
                for b in range(2):
                    for j in range(2):
                        last = nc.tensor.matmul(v_ps[:, b, :], xlT[:, g % 2, j, TOK * b:TOK * b + TOK], wqkv[:, j, 2 * D:3 * D], start=(j == 0), stop=(j == 1))
                last.then_inc(s["vproj_done"], 1)

            def scores(g):
                pe.wait_ge(s["qk_taken"], g + 1)
                if g:
                    pe.wait_ge(s["probs_done"], g)
                if g >= 6:
                    pe.wait_ge(s["y_taken"], g - 5)
                for b in range(2):
                    for j in range(2):
                        last = nc.tensor.matmul(s_ps[:, b, :], qkT[:, g % 2, 2 + j, TOK * b:TOK * b + TOK], qkT[:, g % 2, j, TOK * b:TOK * b + TOK], start=(j == 0), stop=(j == 1))
                last.then_inc(s["score_done"], 1)

            def attend(g):
                pe.wait_ge(s["probs_done"], g + 1)
                pe.wait_ge(s["v_taken"], g + 1)
                if g:
                    pe.wait_ge(s["h_done"], g)
                for b in range(2):
                    last = nc.tensor.matmul(o_ps[:, b, :], pt[:, g % 2, b, :], vt[:, g % 3, b, :], start=True, stop=True)
                last.then_inc(s["attn_done"], 1)

            def directions_transpose(g):
                pe.wait_ge(s["tok_done"], g + 1)
                if g >= 1:
                    pe.wait_ge(s["tkT_taken"], g)
                pe.wait_ge(s["xlT_taken"], min(g + 5, NG))
                for j in range(2):
                    for b in range(2):
                        last = nc.tensor.transpose(tr_ps[:, j, TOK * b:TOK * b + TOK], tk[:, g % 2, b, DC * j:DC * j + DC], ident[0:TOK, 0:TOK])
                last.then_inc(s["tkT_done"], 1)

            def logits(g):
                pe.wait_ge(s["tkT_taken"], g + 1)
                if g:
                    pe.wait_ge(s["exp2_done"], g)
                pe.wait_ge(s["h_patches"], min(g + 7, NG))
                for j in range(2):
                    nc.tensor.matmul(l1_ps.rearrange("p b t -> p (b t)"), slotT[:, j, :], tkT[:, g % 2, j, :], start=(j == 0), stop=(j == 1))
                for b in range(2):
                    for j in range(2):
                        last = nc.tensor.matmul(l2_ps[:, b, :], tkT[:, g % 2, j, TOK * b:TOK * b + TOK], slotT[:, j, :], start=(j == 0), stop=(j == 1))
                last.then_inc(s["logits_done"], 1)

            def weights_transpose(g):
                pe.wait_ge(s["disp_done"], g + 1)
                pe.wait_ge(s["exp2_done"], g + 1)
                if g:
                    pe.wait_ge(s["cT_taken"], g)
                for b in range(2):
                    nc.tensor.transpose(dT_ps[:, b, :], e1[:, g % 3, b, :], ident[0:SLOTS, 0:SLOTS])
                for b in range(2):
                    last = nc.tensor.transpose(cT_ps[:, b, :], e2[:, g % 2, b, :], ident[0:TOK, 0:TOK])
                last.then_inc(s["cT_done"], 1)

            def dispatch(g):
                pe.wait_ge(s["dT_taken"], g + 1)
                pe.wait_ge(s["xn_done"], g + 1)
                if g:
                    pe.wait_ge(s["y_taken"], g)
                pe.wait_ge(s["probs_done"], min(g + 6, NG))
                for b in range(2):
                    for j in range(2):
                        last = nc.tensor.matmul(y_ps[:, b, j, :], xn[:, g % 2, b, DC * j:DC * j + DC], dT[:, g % 2, b, :], start=True, stop=True)
                last.then_inc(s["y_done"], 1)

            for stage, g in steps([(dispatch, 9), (weights_transpose, 8), (logits, 7), (directions_transpose, 6), (attend, 4),
                                   (scores, 3), (project, 2), (normed_transpose, 1), (back_to_tokens, 0)]):
                stage(g)

            pe.wait_ge(s["y_taken"], NG)
            pe.wait_ge(s["cT_taken"], NG)
            pe.wait_ge(consts_made, 2)

            def up(q):
                pe.wait_ge(ld_f1[q % 2], 32 * (q // 2 + 1))
                if q >= 2:
                    pe.wait_ge(gelu_done, q - 1)
                for half in range(2):
                    for j in range(2):
                        rows = DC + 1 - j
                        for i in range(MS):
                            last = nc.tensor.matmul(h1_ps[q % 2][32 * i:32 * i + 32, half, :], yT[0:rows, j, MS * q + i, :],
                                                    f1w[0:rows, q % 2, i, j, FF // 2 * half:FF // 2 * half + FF // 2],
                                                    start=(j == 0), stop=(j == 1), tile_position=(0, 32 * i))
                last.then_inc(fc1_done, 1)

            def turn(q):
                pe.wait_ge(gelu_done, q + 1)
                if q:
                    pe.wait_ge(h1T_taken, q)
                for j in range(FT):
                    last = nc.tensor.transpose(h1T_ps[:, 128 * j:128 * j + 128], g1[:, 0, 128 * j:128 * j + 128], ident)
                last.then_inc(h1T_done, 1)

            def down(q):
                pe.wait_ge(h1T_taken, q + 1)
                pe.wait_ge(ld_f2[q % F2R], 16 * (q // F2R + 1))
                if q:
                    pe.wait_ge(y2_done, q)
                for j in range(FT):
                    for i in range(MS):
                        last = nc.tensor.matmul(y2_ps[32 * i:32 * i + 32, :], g1T[:, 0, j, 32 * i:32 * i + 32], f2w[:, q % F2R, i, j, :],
                                                start=(j == 0), stop=(j == FT - 1), tile_position=(0, 32 * i))
                last.then_inc(fc2_done, 1)

            for q in range(MG + 1):
                if q:
                    turn(q - 1)
                if q < MG:
                    up(q)
                if q:
                    down(q - 1)

            pe.wait_ge(y2_done, MG)
            pe.wait_ge(y_moved[0], 16 * MS * MG // 2)
            pe.wait_ge(y_moved[1], 16 * MS * MG // 2)
            for g in range(NG):
                if g >= 2:
                    pe.wait_ge(out_done, g - 1)
                for b in range(2):
                    last = nc.tensor.matmul(fin_ps[g % 2][:, b, :], combT[:, 2 * g + b, :], ybuf[:, 2 * g + b, :], start=True, stop=True)
                last.then_inc(fin_done, 1)

        @block.vector
        def _(ve):
            n_step = [0]

            def then(ins):
                n_step[0] += 1
                ins.then_inc(v_step, 1)
                ve.wait_ge(v_step, n_step[0])

            def take_offsets(ck, wt):
                n = HT * ck + wt
                ve.wait_ge(off_done, n + 1)
                if ck >= 2 and wt == 0:
                    ve.wait_ge(hats, 2 * WIN * (ck - 1))
                nc.vector.tensor_tensor(off[:, ck % 2, :, wt, :], off_ps.rearrange("p (a q) -> p a q", a=2),
                                        boff.rearrange("p (a q) -> p a q", a=2), ALU.add).then_inc(off_taken, 1)

            def max_offset(ck):
                ve.wait_ge(off_taken, HT * (ck + 1))
                nc.vector.tensor_reduce(off_max[:, ck:ck + 1], off[:, ck % 2].rearrange("p a w q -> p (a w q)"), AX.X, ALU.max,
                                        apply_absolute_value=True).then_inc(off_maxed, 1)

            ve.wait_ge(ld_w, 48)
            for wt in range(HT):
                take_offsets(0, wt)
            max_offset(0)
            ve.wait_ge(ld_x, 16)
            for ck in range(HT):
                for t in range(TAPS):
                    if OWN[t] != "vector":
                        continue
                    i, j = t // WIN, t % WIN
                    n = V_TAPS * ck + nth(t)
                    ve.wait_ge(hats, hat_count(ck, i, j))
                    if n:
                        ve.wait_ge(prod_v_done, n)
                    then(nc.vector.tensor_tensor(w_v, haty[:, (WIN * ck + i) % 2], hatx[:, j], ALU.mult))
                    if n >= 2:
                        ve.wait_ge(prod_v_used, n - 1)
                    nc.vector.tensor_tensor(pixels(prod_v[:, n % 2]), window(ck, i, j), bcast_c(w_v), ALU.mult).then_inc(prod_v_done, 1)
                    if ck + 1 < HT and t in (6, 12, 16):
                        take_offsets(ck + 1, (6, 12, 16).index(t))
                    if ck + 1 < HT and t == 18:
                        max_offset(ck + 1)

            for ck in range(HT):
                for oc in range(2):
                    ve.wait_ge(conv_taken, 2 * ck + oc + 1)
                    last = nc.vector.bn_stats(bn6[:, oc, ck, :], convs[:, oc, ck, :])
            then(last)
            for oc in range(2):
                last = nc.vector.bn_aggr(bn2[:, oc, :], bn6[:, oc].rearrange("p a b -> p (a b)"))
            last.then_inc(bn_var, 1)
            ve.wait_ge(bn_rstd, 1)
            then(nc.vector.tensor_tensor(bn_s, bn_r, gam, ALU.mult))
            then(nc.vector.tensor_tensor(bn_t, bn2[:, :, 0], bn_s, ALU.mult))
            nc.vector.tensor_tensor(bn_t, bet, bn_t, ALU.subtract).then_inc(bn_affine, 1)

            def variances(g, mv):
                for b in range(2):
                    last = nc.vector.bn_stats(st6[:, b, 0, :], h[:, 2 * g + b, :])
                then(last)
                for b in range(2):
                    last = nc.vector.bn_aggr(mv[:, b, :], st6[:, b, 0, :])
                return last

            def first_stats(g):
                ve.wait_ge(s["h_patches"], g + 1)
                if g == 0:
                    ve.wait_ge(ld_txt, 16)
                if g >= 4:
                    ve.wait_ge(s["xl_done"], g - 3)
                variances(g, mv1[:, g % 4]).then_inc(s["var1_done"], 1)

            def first_norm(g):
                ve.wait_ge(s["rstd1_done"], g + 1)
                if g >= 2:
                    ve.wait_ge(s["xlT_done"], g - 1)
                for b in range(2):
                    last = nc.vector.tensor_scalar(xl[:, g % 2, b, :], h[:, 2 * g + b, :], mv1[:, g % 4, b, 0:1], r1[:, g % 4, b:b + 1], ALU.subtract, ALU.mult)
                last.then_inc(s["xl_done"], 1)

            def values(g):
                ve.wait_ge(s["vproj_done"], g + 1)
                if g >= 3:
                    ve.wait_ge(s["attn_done"], g - 2)
                nc.vector.tensor_tensor(vt[:, g % 3], v_ps, bv.unsqueeze(1).broadcast_to([TOK, 2, D]), ALU.add).then_inc(s["v_taken"], 1)

            def decayed(g):
                ve.wait_ge(s["score_done"], g + 1)
                if g >= 2:
                    ve.wait_ge(s["attn_done"], g - 1)
                nc.vector.tensor_tensor(pt[:, g % 2], s_ps, decay.unsqueeze(1).broadcast_to([TOK, 2, TOK]), ALU.mult).then_inc(s["probs_done"], 1)

            def residual(g):
                ve.wait_ge(s["attn_done"], g + 1)
                ve.wait_ge(s["xl_done"], g + 1)
                last = nc.vector.tensor_tensor(h[:, 2 * g:2 * g + 2, :], o_ps, h[:, 2 * g:2 * g + 2, :], ALU.add)
                last.then_inc(s["h_done"], 1)
                ve.wait_ge(s["h_done"], g + 1)
                variances(g, mv2[:, g]).then_inc(s["var2_done"], 1)

            def weighted(g):
                ve.wait_ge(s["var2_done"], g + 1)
                if g >= 3:
                    ve.wait_ge(s["tok_done"], g - 2)
                for b in range(2):
                    last = nc.vector.scalar_tensor_tensor(z[:, g % 3, b, :], h[:, 2 * g + b, :], mv2[:, g, b, 0:1], normw, ALU.subtract, ALU.mult)
                last.then_inc(s["z_done"], 1)

            def unit(g):
                ve.wait_ge(s["f2_done"], g + 1)
                ve.wait_ge(s["z_done"], g + 1)
                if g >= 2:
                    ve.wait_ge(s["tkT_done"], g - 1)
                for b in range(2):
                    last = nc.vector.tensor_scalar(tk[:, g % 2, b, :], z[:, g % 3, b, :], f2[:, g % 4, b:b + 1], None, ALU.mult)
                last.then_inc(s["tok_done"], 1)

            def maxima(g):
                ve.wait_ge(s["logits_done"], g + 1)
                if g >= 4:
                    ve.wait_ge(s["exp1_done"], g - 3)
                nc.vector.tensor_reduce(nmax1[:, g % 4, :], l1_ps, AX.X, ALU.max, negate=True)
                if g >= 4:
                    ve.wait_ge(s["exp2_done"], g - 3)
                nc.vector.tensor_reduce(nmax2[:, g % 4, :], l2_ps, AX.X, ALU.max, negate=True).then_inc(s["max_done"], 1)

            def normed_dispatch(g):
                ve.wait_ge(s["exp1_done"], g + 1)
                then(nc.vector.reciprocal(rsum1[:, g % 4, :], sum1[:, g % 4, :]))
                for b in range(2):
                    last = nc.vector.tensor_scalar(e1[:, g % 3, b, :], e1[:, g % 3, b, :], rsum1[:, g % 4, b:b + 1], None, ALU.mult)
                last.then_inc(s["disp_done"], 1)

            def normed_tokens(g):
                if g >= 2:
                    ve.wait_ge(s["y_done"], g - 1)
                for b in range(2):
                    last = nc.vector.scalar_tensor_tensor(xn[:, g % 2, b, :], h[:, 2 * g + b, :], mv2[:, g, b, 0:1], normw, ALU.subtract, ALU.mult)
                last.then_inc(s["xn_done"], 1)

            for stage, g in steps([(weighted, 5), (unit, 6), (maxima, 7), (normed_tokens, 8), (residual, 4), (decayed, 3),
                                   (normed_dispatch, 7), (values, 2), (first_norm, 1), (first_stats, 0)]):
                stage(g)

            ve.wait_ge(s["exp2_done"], NG)
            then(nc.vector.reciprocal(rsum2, sum2))
            for q in range(MG):
                ve.wait_ge(h1T_done, q + 1)
                if q:
                    ve.wait_ge(fc2_done, q)
                else:
                    ve.wait_ge(s["y_done"], NG)
                nc.vector.tensor_copy(g1T[:, 0].rearrange("p a b -> p (a b)"), h1T_ps).then_inc(h1T_taken, 1)
                ve.wait_ge(fc2_done, q + 1)
                ve.wait_ge(ld_b2[q % 2], 16 * (q // 2 + 1))
                if q >= 2:
                    ve.wait_ge(y_moved[q % 2], 16 * MS * (q // 2))
                nc.vector.tensor_tensor(y2[:, q % 2, :], y2_ps, b2[:, q % 2, :], ALU.add).then_inc(y2_done, 1)
            for g in range(NG):
                ve.wait_ge(fin_done, g + 1)
                for b in range(2):
                    n = 2 * g + b
                    last = nc.vector.scalar_tensor_tensor(h[:, n, :], fin_ps[g % 2][:, b, :], rsum2[:, n:n + 1], h[:, n, :], ALU.mult, ALU.add)
                last.then_inc(out_done, 1)

        @block.scalar
        def _(ac):
            n_step = [0]

            def then(ins):
                n_step[0] += 1
                ins.then_inc(a_step, 1)
                ac.wait_ge(a_step, n_step[0])

            ac.wait_ge(ld_const, 16 * 11)
            nc.scalar.activation(slotn, slotv, ACT.Square, accum_out=slot_sq).then_inc(slot_sqd, 1)

            n_hat = [0]

            def hat(dst, src, center):
                n = n_hat[0]
                n_hat[0] += 1
                t = hat_t[:, n % 2]
                if n >= 2:
                    ac.wait_ge(hats, n - 1)
                then(nc.scalar.activation(t, src, ACT.Abs, bias=-float(center)))
                nc.scalar.activation(dst, t, ACT.Relu, bias=1.0, scale=-1.0).then_inc(hats, 1)

            def last_use(ck, i, j):
                t = WIN * i + j
                v = V_TAPS * ck + OWN[:t + 1].count("vector")
                p = POOL_TAPS * ck + OWN[:t + 1].count("pool")
                if v:
                    ac.wait_ge(prod_v_done, v)
                if p:
                    ac.wait_ge(prod_p_done, p)

            for ck in range(HT):
                ac.wait_ge(off_checked, ck + 1)
                for i in range(WIN):
                    r = WIN * ck + i
                    if r >= 2:
                        last_use((r - 2) // WIN, (r - 2) % WIN, WIN - 1)
                    hat(haty[:, (WIN * ck + i) % 2], off[:, ck % 2, 0], i - RAD)
                    if i == 0:
                        for j in range(WIN):
                            if ck:
                                last_use(ck - 1, WIN - 1, j)
                            hat(hatx[:, j], off[:, ck % 2, 1], j - RAD)
                ac.wait_ge(prod_v_used, V_TAPS * (ck + 1))
                ac.wait_ge(prod_p_used, POOL_TAPS * (ck + 1))
                if ck:
                    ac.wait_ge(conv_done, 2 * ck)
                nc.scalar.activation(samp.rearrange("p k w n -> p (k w n)"), acc, ACT.Copy).then_inc(samp_done, 1)
                for oc in range(2):
                    ac.wait_ge(conv_done, 2 * ck + oc + 1)
                    nc.scalar.activation(convs[:, oc, ck, :], conv_ps[0:DC, 0:HT * 128], ACT.Copy).then_inc(conv_taken, 1)

            ac.wait_ge(slot_td, 1)
            nc.scalar.activation(slotT.rearrange("p j s -> p (j s)"), conv_ps[0:DC, 0:2 * SLOTS], ACT.Copy).then_inc(slot_td2, 1)
            ac.wait_ge(bn_affine, 1)
            for oc in range(2):
                for hot in range(HT):
                    for hop in range(2):
                        src = convs[:, oc, hot, :].rearrange("p (wt hp wp b) -> p hp wt wp b", wt=HT, hp=2, wp=2)[:, hop]
                        dst = patch_tok[:, oc].rearrange("p b (hp ht wp wt) -> p hp ht wt wp b", hp=2, ht=HT, wp=2)[:, hop, hot]
                        last = nc.scalar.activation(dst, src, ACT.Gelu, bias=bn_t[:, oc:oc + 1], scale=bn_s[:, oc:oc + 1])
            last.then_inc(patches, 1)

            def take_patches(g):
                ac.wait_ge(s["tokT_done"], g + 1)
                nc.scalar.activation(h[0:PT * PT, 2 * g:2 * g + 2, :], tok_ps, ACT.Copy).then_inc(s["h_patches"], 1)

            def take_normed(g):
                ac.wait_ge(s["xlT_done"], g + 1)
                if g >= 2:
                    ac.wait_ge(s["vproj_done"], g - 1)
                nc.scalar.activation(xlT[:, g % 2], tr_ps, ACT.Copy).then_inc(s["xlT_taken"], 1)

            def take_qk(g):
                ac.wait_ge(s["qk_done"], g + 1)
                if g >= 2:
                    ac.wait_ge(s["score_done"], g - 1)
                for m in range(4):
                    last = nc.scalar.activation(qkT[:, g % 2, m, :], qk_ps[m], ACT.Identity, bias=bqk[:, m:m + 1])
                last.then_inc(s["qk_taken"], 1)

            def squares(g):
                ac.wait_ge(s["z_done"], g + 1)
                if g >= 4:
                    ac.wait_ge(s["f2_done"], g - 3)
                if g >= 2:
                    ac.wait_ge(s["tkT_done"], g - 1)
                for b in range(2):
                    last = nc.scalar.activation(tk[:, g % 2, b, :], z[:, g % 3, b, :], ACT.Square, accum_out=ssq[:, g % 4, b:b + 1])
                last.then_inc(s["ssq_done"], 1)

            def take_directions(g):
                ac.wait_ge(s["tkT_done"], g + 1)
                if g >= 2:
                    ac.wait_ge(s["logits_done"], g - 1)
                nc.scalar.activation(tkT[:, g % 2], tr_ps, ACT.Copy).then_inc(s["tkT_taken"], 1)

            def exps(g):
                ac.wait_ge(s["max_done"], g + 1)
                if g >= 3:
                    ac.wait_ge(s["cT_done"], g - 2)
                for b in range(2):
                    last = nc.scalar.activation(e1[:, g % 3, b, :], l1_ps[:, b, :], ACT.Exp, bias=nmax1[:, g % 4, b:b + 1], accum_out=sum1[:, g % 4, b:b + 1])
                last.then_inc(s["exp1_done"], 1)
                if g >= 2:
                    ac.wait_ge(s["cT_done"], g - 1)
                for b in range(2):
                    last = nc.scalar.activation(e2[:, g % 2, b, :], l2_ps[:, b, :], ACT.Exp, bias=nmax2[:, g % 4, b:b + 1], accum_out=sum2[:, 2 * g + b:2 * g + b + 1])
                last.then_inc(s["exp2_done"], 1)

            def take_weights(g):
                ac.wait_ge(s["cT_done"], g + 1)
                if g >= 2:
                    ac.wait_ge(s["y_done"], g - 1)
                for b in range(2):
                    last = nc.scalar.activation(dT[:, g % 2, b, :], dT_ps[:, b, :], ACT.Copy, scale=a2[:, g, b:b + 1])
                last.then_inc(s["dT_taken"], 1)
                nc.scalar.activation(combT[:, 2 * g:2 * g + 2, :], cT_ps, ACT.Copy).then_inc(s["cT_taken"], 1)

            def take_dispatched(g):
                ac.wait_ge(s["y_done"], g + 1)
                nc.scalar.activation(yT[0:DC, :, :, 2 * g:2 * g + 2].rearrange("p j s b -> p b j s"), y_ps, ACT.Copy).then_inc(s["y_taken"], 1)

            for stage, g in steps([(take_dispatched, 9), (take_weights, 8), (squares, 5), (exps, 7), (take_directions, 6),
                                   (take_qk, 2), (take_normed, 1), (take_patches, 0)]):
                stage(g)

            for q in range(MG + 1):
                if q < MG:
                    if q == 0:
                        ac.wait_ge(s["y_done"], NG)
                    if q < 2:
                        ac.dma_start(b2[:, q % 2, :], fc2_b[q]).then_inc(ld_b2[q % 2], 16)
                    ac.wait_ge(fc1_done, q + 1)
                    if q:
                        ac.wait_ge(h1T_done, q)
                    nc.scalar.activation(g1[:, 0].rearrange("p (a n) -> p a n", a=2), h1_ps[q % 2], ACT.Gelu).then_inc(gelu_done, 1)
                if q:
                    p = q - 1
                    ac.wait_ge(y2_done, p + 1)
                    for i in range(MS):
                        n = MS * p + i
                        ac.dma_start(ybuf[n:n + 1, :, :], y2[32 * i:32 * i + 32, p % 2, :]).then_inc(y_moved[p % 2], 16)
                    if p + 2 < MG:
                        ac.dma_start(b2[:, p % 2, :], fc2_b[p + 2]).then_inc(ld_b2[p % 2], 16)

            for g in range(NG):
                ac.wait_ge(out_done, g + 1)
                o = out[2 * g:2 * g + 2].rearrange("b t d -> t b d")
                ac.dma_start(o[0:TOK - 1], h[0:TOK - 1, 2 * g:2 * g + 2, :]).then_inc(stored, 16)
                ac.dma_start(o[TOK - 1:TOK], h[TOK - 1:TOK, 2 * g:2 * g + 2, :]).then_inc(stored, 16)
            ac.wait_ge(stored, 16 * 2 * NG)

        @block.gpsimd
        def _(gp):
            n_step = [0]

            def then(ins):
                n_step[0] += 1
                ins.then_inc(g_step, 1)
                gp.wait_ge(g_step, n_step[0])

            nc.gpsimd.memset(half_neg, -0.5)
            nc.gpsimd.memset(outl, 0.0).then_inc(consts_made, 1)
            gp.wait_ge(ld_const, 16 * 11)
            gp.wait_ge(consts_made, 1)

            gp.wait_ge(slot_sqd, 1)
            then(nc.gpsimd.tensor_scalar(slot_f, slot_sq, EPS * EPS, None, ALU.max))
            then(nc.gpsimd.tensor_tensor(slot_f, slot_f, half_neg[0:SLOTS, 0:1], ALU.pow))
            then(nc.gpsimd.tensor_tensor(slot_f, slot_f, slotsc, ALU.mult))
            nc.gpsimd.tensor_tensor(slotn, slotv, slot_f.broadcast_to([SLOTS, D]), ALU.mult).then_inc(slot_nd, 1)

            def gather_outliers(ck):
                py, px, ry, rx, ti, w0, w1, w2, w3, mask, t = (gen[:, n] for n in range(11))
                dy, dx = off[:, ck % 2, 0].rearrange("p w q -> p (w q)"), off[:, ck % 2, 1].rearrange("p w q -> p (w q)")
                done = sem(f"exact_{ck}")
                count = [0]

                def run(ins):
                    count[0] += 1
                    ins.then_inc(done, 1)
                    gp.wait_ge(done, count[0])

                if pool_made[0]:
                    gp.wait_ge(prod_p_used, pool_made[0])
                gp.dma_start(gen[:, 0:2], grid_in[ck]).then_inc(grid_in_sb, 16)
                gp.wait_ge(grid_in_sb, 16)
                gp.sem_clear(grid_in_sb)
                ts, tt = nc.gpsimd.tensor_scalar, nc.gpsimd.tensor_tensor
                run(tt(py, py, dy, ALU.add))
                run(tt(px, px, dx, ALU.add))
                run(tt(mask, dy, dy, ALU.mult))
                run(ts(mask, mask, float(RAD * RAD), None, ALU.is_gt))
                run(tt(t, dx, dx, ALU.mult))
                run(ts(t, t, float(RAD * RAD), None, ALU.is_gt))
                run(tt(mask, mask, t, ALU.add))
                run(ts(mask, mask, 1.0, None, ALU.min))
                for pos, low in ((py, ry), (px, rx)):
                    run(ts(low, pos, 0.0, float(IMG - 2), ALU.max, ALU.min))
                    run(nc.gpsimd.tensor_copy(ti.bitcast(i32), low))
                    run(nc.gpsimd.tensor_copy(t, ti.bitcast(i32)))
                    run(tt(low, t, low, ALU.subtract))
                    run(ts(low, low, 0.0, None, ALU.is_gt))
                    run(tt(low, t, low, ALU.subtract))

                def pair(pos, low, near, far):
                    run(tt(pos, pos, low, ALU.subtract))
                    for dst, shift in ((near, 0.0), (far, 1.0)):
                        run(ts(dst, pos, -1.0, 1.0 + shift, ALU.mult, ALU.add))
                        run(ts(dst, dst, 0.0, 1.0, ALU.max, ALU.min))
                        run(ts(t, pos, 1.0 - shift, None, ALU.add))
                        run(ts(t, t, 0.0, 1.0, ALU.max, ALU.min))
                        run(tt(dst, dst, t, ALU.mult))

                pair(py, ry, w0, w2)
                pair(px, rx, w1, w3)
                run(tt(w0, w0, mask, ALU.mult))
                run(tt(w2, w2, mask, ALU.mult))
                run(tt(ti, w0, w1, ALU.mult))
                run(tt(py, w0, w3, ALU.mult))
                run(tt(px, w2, w1, ALU.mult))
                run(tt(w3, w2, w3, ALU.mult))
                run(nc.gpsimd.tensor_copy(w0, ti))
                run(nc.gpsimd.tensor_copy(w1, py))
                run(nc.gpsimd.tensor_copy(w2, px))
                run(ts(ry, ry, float(IMG), None, ALU.mult))
                run(tt(ry, ry, rx, ALU.add))
                run(ts(dy, dy, -3.0, 3.0, ALU.max, ALU.min))
                run(ts(mask, mask, 1e6, None, ALU.mult))
                run(tt(dy, dy, mask, ALU.add))
                quad = gen[:, 5:9]
                flat = outl.rearrange("p c w q -> p c (w q)")
                with gp.Fori(0, NPOS) as pos:
                    nc.gpsimd.tensor_tensor(corner_at, ry[:, bass.ds(pos, 1)].broadcast_to([128, 12]), corner, ALU.add)
                    gp.drain()
                    nc.gpsimd.tensor_copy(corner_idx.bitcast(i32), corner_at)
                    gp.drain()
                    for n in range(12):
                        gp.indirect_dma_start(corner_val.rearrange("p c q -> p (c q)")[:, n:n + 1], None, x_flat,
                                              bass.IndirectOffsetOnAxis(ap=corner_idx.bitcast(u32)[:, n:n + 1], axis=0)).then_inc(gathered, 16)
                    gp.wait_ge(gathered, 16 * 12)
                    gp.sem_clear(gathered)
                    nc.gpsimd.tensor_tensor(corner_wv, corner_val, quad[:, :, bass.ds(pos, 1)].rearrange("p q o -> p o q").broadcast_to([128, C, 4]), ALU.mult)
                    gp.drain()
                    nc.gpsimd.tensor_tensor(corner_s, corner_wv[:, :, 0:2], corner_wv[:, :, 2:4], ALU.add)
                    gp.drain()
                    nc.gpsimd.tensor_tensor(flat[:, :, bass.ds(pos, 1)], corner_s[:, :, 0:1], corner_s[:, :, 1:2], ALU.add)
                    gp.drain()

            pool_made = [0]

            def check_offsets(ck):
                gp.wait_ge(off_maxed, ck + 1)
                if ck:
                    gp.wait_ge(outl_used, ck)
                    then(nc.gpsimd.memset(outl, 0.0))
                then(nc.gpsimd.partition_all_reduce(off_all[:, ck:ck + 1], off_max[:, ck:ck + 1], 128, bass.bass_isa.ReduceOp.max))
                far = gp.value_load(off_all[0:1, ck:ck + 1].bitcast(i32))
                with gp.If(far > int(np.float32(RAD).view(np.int32))):
                    gather_outliers(ck)
                nc.gpsimd.nop().then_inc(off_checked, 1)

            check_offsets(0)
            gp.wait_ge(ld_x, 16)
            for ck in range(HT):
                for t in range(TAPS):
                    if OWN[t] != "pool":
                        continue
                    i, j = t // WIN, t % WIN
                    n = POOL_TAPS * ck + nth(t)
                    gp.wait_ge(hats, hat_count(ck, i, j))
                    if n:
                        gp.wait_ge(prod_p_done, n)
                    then(nc.gpsimd.tensor_tensor(w_p, haty[:, (WIN * ck + i) % 2], hatx[:, j], ALU.mult))
                    if n >= 2:
                        gp.wait_ge(prod_p_used, n - 1)
                    nc.gpsimd.tensor_tensor(pixels(prod_p[:, n % 2]), window(ck, i, j), bcast_c(w_p), ALU.mult).then_inc(prod_p_done, 1)
                    pool_made[0] = n + 1
                    if ck + 1 < HT and nth(t) == 6:
                        check_offsets(ck + 1)

            gp.wait_ge(bn_var, 1)
            then(nc.gpsimd.tensor_scalar(bn_r, bn2[:, :, 1], EPS, None, ALU.add))
            nc.gpsimd.tensor_tensor(bn_r, bn_r, half_neg[0:DC, 0:2], ALU.pow).then_inc(bn_rstd, 1)
            gp.wait_ge(samp_done, HT)
            nc.gpsimd.memset(yT[DC:DC + 1, 0], 1.0).then_inc(consts_made, 1)
            gp.wait_ge(consts_made, 2)

            def first_rstd(g):
                gp.wait_ge(s["var1_done"], g + 1)
                if g >= 4:
                    gp.wait_ge(s["xl_done"], g - 3)
                then(nc.gpsimd.tensor_scalar(r1[:, g % 4, :], mv1[:, g % 4, :, 1], EPS, None, ALU.add))
                nc.gpsimd.tensor_tensor(r1[:, g % 4, :], r1[:, g % 4, :], half_neg[0:TOK, 0:2], ALU.pow).then_inc(s["rstd1_done"], 1)

            def second_factor(g):
                gp.wait_ge(s["var2_done"], g + 1)
                then(nc.gpsimd.tensor_scalar(a2[:, g, :], mv2[:, g, :, 1], 1.0 + EPS, EPS * EPS, ALU.mult, ALU.add))
                nc.gpsimd.tensor_tensor(a2[:, g, :], a2[:, g, :], half_neg[0:TOK, 0:2], ALU.pow).then_inc(s["a2_done"], 1)

            def unit_factor(g):
                gp.wait_ge(s["ssq_done"], g + 1)
                if g >= 4:
                    gp.wait_ge(s["tok_done"], g - 3)
                gp.wait_ge(s["a2_done"], g + 1)
                then(nc.gpsimd.tensor_tensor(tmp2[:, g % 4, :], a2[:, g, :], a2[:, g, :], ALU.mult))
                then(nc.gpsimd.tensor_tensor(tmp2[:, g % 4, :], tmp2[:, g % 4, :], ssq[:, g % 4, :], ALU.mult))
                then(nc.gpsimd.tensor_scalar(tmp2[:, g % 4, :], tmp2[:, g % 4, :], EPS * EPS, None, ALU.max))
                then(nc.gpsimd.tensor_tensor(tmp2[:, g % 4, :], tmp2[:, g % 4, :], half_neg[0:TOK, 0:2], ALU.pow))
                nc.gpsimd.tensor_tensor(f2[:, g % 4, :], tmp2[:, g % 4, :], a2[:, g, :], ALU.mult).then_inc(s["f2_done"], 1)

            for stage, g in steps([(unit_factor, 5), (second_factor, 4), (first_rstd, 0)]):
                stage(g)


_OUT = (B, TOK, D)


def kernel(x, txt, L0_tok_offset_w, L0_tok_offset_b, L0_tok_dconv_w, L0_tok_bn_gamma, L0_tok_bn_beta, L0_attn_W_qkv,
           L0_attn_b_qkv, L0_ffn_slots, L0_ffn_scale, L0_ffn_fc1_weight, L0_ffn_fc1_bias, L0_ffn_fc2_weight,
           L0_ffn_fc2_bias, L0_ffn_norm_weight):
    import concourse.bacc as bacc
    from concourse.bass_utils import run_bass_kernel_spmd

    x = np.asarray(x)
    halves = 2
    padded = np.zeros((B, C, IMG + 2 * RAD, IMG + 2 * RAD), x.dtype)
    padded[:, :, RAD:RAD + IMG, RAD:RAD + IMG] = x
    wide = PATCH + 2 * RAD
    halo = np.stack([np.stack([padded[:, :, QW * hp:QW * hp + HALO, QW * wp + PATCH * wt:QW * wp + PATCH * wt + wide] for wt in range(HT)], axis=2)
                     for hp in range(2) for wp in range(2)])
    cols = x.reshape(B, C, 2, HT, halves, 8, 2, HT, PATCH).transpose(3, 5, 8, 1, 4, 7, 2, 6, 0)
    w_off = np.asarray(L0_tok_offset_w).reshape(KK, 2, C, halves, 128).transpose(4, 2, 3, 1, 0)
    w_conv = np.asarray(L0_tok_dconv_w).reshape(D, C, halves, 128).transpose(3, 1, 2, 0)
    w_qkv, b_qkv = np.asarray(L0_attn_W_qkv), np.asarray(L0_attn_b_qkv)
    i = np.arange(TOK)
    gap = i[None, :] - i[:, None]
    decay = np.where(gap >= 0, np.float32(ALPHA) ** np.maximum(gap, 0).astype(np.float32), 0) / np.sqrt(np.float32(D))
    p = np.arange(128)
    hop, wop, b = p // 64, p // 32 % 2, p % 32
    r = np.arange(PATCH)
    wt = np.arange(HT)[None, :, None, None]
    grid = np.zeros((HT, 128, 2, HT, PATCH, PATCH), np.float32)
    for ck in range(HT):
        grid[ck, :, 0] = QW * hop[:, None, None, None] + PATCH * ck + r[None, None, :, None]
        grid[ck, :, 1] = QW * wop[:, None, None, None] + PATCH * wt + r[None, None, None, :]
    corner = (b[:, None, None] * C + np.arange(C)[None, :, None]) * IMG * IMG + np.array([0, 1, IMG, IMG + 1])[None, None, :]
    arrays = {
        "x_halo": halo.reshape(128, C, HT, HALO, wide),
        "x_cols": cols.reshape(HT, 128, KC, HT, 128),
        "x_flat": x.reshape(-1, 1),
        "w_off": w_off.reshape(128, KC, 2 * KK),
        "b_off": np.asarray(L0_tok_offset_b).reshape(KK, 2).T.reshape(2 * KK),
        "w_conv": w_conv.reshape(128, KC, D),
        "bn_g": np.asarray(L0_tok_bn_gamma).reshape(2, DC).T,
        "bn_b": np.asarray(L0_tok_bn_beta).reshape(2, DC).T,
        "txt": np.asarray(txt),
        "w_qkv": w_qkv.reshape(2, DC, 3 * D).transpose(1, 0, 2),
        "b_qk": b_qkv[:2 * D].reshape(4, DC).T,
        "b_v": b_qkv[2 * D:],
        "slots": np.asarray(L0_ffn_slots),
        "scale": np.asarray(L0_ffn_scale).reshape(SLOTS, 1),
        "fc1": np.asarray(L0_ffn_fc1_weight).reshape(SLOTS, 2, DC, FF).transpose(0, 2, 1, 3),
        "fc1_b": np.asarray(L0_ffn_fc1_bias),
        "fc2": np.asarray(L0_ffn_fc2_weight).reshape(SLOTS, FT, 128, D).transpose(0, 2, 1, 3),
        "fc2_b": np.repeat(np.asarray(L0_ffn_fc2_bias), B, axis=0).reshape(MG, MS * B, D),
        "norm_w": np.asarray(L0_ffn_norm_weight),
        "ident_in": np.eye(128, dtype=np.float32),
        "decay_in": decay.astype(np.float32),
        "grid_in": grid.reshape(HT, 128, 2, NPOS),
        "corner_in": corner.reshape(128, 12).astype(np.float32),
    }
    arrays = {n: np.ascontiguousarray(a) for n, a in arrays.items()}
    nc = bacc.Bacc("TRN2", target_bir_lowering=False, num_devices=1)
    args = [nc.dram_tensor(n, a.shape, mybir.dt.from_np(a.dtype), kind="ExternalInput").ap() for n, a in arrays.items()]
    out = nc.dram_tensor("out", _OUT, mybir.dt.float32, kind="ExternalOutput").ap()
    fusion_program(nc, *args, out)
    return run_bass_kernel_spmd(nc, [arrays], core_ids=[0]).results[0]["out"]
```

```python
import numpy as np

import concourse.bass as bass
from concourse import mybir
from contextlib import ExitStack

B, C, IMG, PATCH = 32, 3, 96, 16
D, TXT, SLOTS, FF = 192, 77, 64, 768
PT = 6
HT = PT // 2
TOK = PT * PT + TXT
RAD = 2
WIN = 2 * RAD + 1
QW = HT * PATCH
HALO = QW + 2 * RAD
NPOS = PATCH * QW
KK = PATCH * PATCH
KC = C * KK // 128
TAPS = WIN * WIN
DC = D // 2
NG = B // 2
T2 = 2 * TOK
MS = 4
MG = SLOTS // MS
FT = FF // 128
ALPHA, EPS = 0.99, 1e-5
POOL_TAPS = 8
OFF_AT = (6, 10, 14)
TAKE_AT = (9, 13, 18)
SAMP_HALF = 12
CONSTS = 8
STORE = 4


def fusion_program(nc, x_halo, x_cols, x_flat, w_off, b_off, w_conv, bn_g, bn_b, txt, wq_t, wk_t, b_q, w_v, b_v,
                   slots, scale, fc1, fc1_b, fc2, fc2_b, norm_w, ident_in, decay_in, grid_in, corner_in, out):
    f32, i32, u32 = mybir.dt.float32, mybir.dt.int32, mybir.dt.uint32
    ALU, ACT, AX = mybir.AluOpType, mybir.ActivationFunctionType, mybir.AxisListType
    ctx = ExitStack()
    with ctx:
        KEEP, SHARED = 3200, 48896
        arena = ctx.enter_context(nc.sbuf_tensor("arena", [128, KEEP + SHARED], f32))
        place = {"at": 0, "end": KEEP}

        def region(at, end):
            place["at"], place["end"] = at, end

        def carve(parts, *shape):
            n = int(np.prod(shape))
            at = place["at"]
            place["at"] = at + n
            assert place["at"] <= place["end"], (place, shape)
            v = arena[0:parts, at:at + n]
            names = "abcde"[:len(shape)]
            if len(shape) == 1:
                return v
            return v.rearrange("p (" + " ".join(names) + ") -> p " + " ".join(names),
                               **{names[i]: shape[i] for i in range(len(shape))})

        ident = carve(128, 128)
        decay = carve(TOK, TOK)
        wv = carve(DC, 2, D)
        gram = carve(DC, 2, D + 1)
        gram0 = carve(DC + 1, 2)
        bv = carve(TOK, D)
        normw = carve(TOK, D)
        gam, bet = carve(DC, 2), carve(DC, 2)
        slotv, slotsc = carve(SLOTS, D), carve(SLOTS, 1)
        slot_sq, slot_f = carve(SLOTS, 1), carve(SLOTS, 1)
        slotn = carve(SLOTS, D)
        slotT = carve(DC, 2, SLOTS)
        half_neg = carve(128, 2)
        bn6, bn2 = carve(DC, 2, HT, 6), carve(DC, 2, 2)
        bn_r, bn_s, bn_t = carve(DC, 2), carve(DC, 2), carve(DC, 2)
        off_max, off_all = carve(128, HT), carve(128, HT)
        st6 = carve(TOK, 4, 2, 6)
        mv1, mv2 = carve(TOK, 4, 2, 2), carve(TOK, 16, 2, 2)
        r1 = carve(TOK, 4, 2)
        a2 = carve(TOK, 16, 2)
        ssq, f2 = carve(TOK, 4, 2), carve(TOK, 4, 2)
        tmp2 = carve(TOK, 4, 2)
        nmax1, sum1 = carve(SLOTS, 4, 2), carve(SLOTS, 4, 2)
        nmax2 = carve(TOK, 4, 2)
        sum2, rsum2 = carve(TOK, B), carve(TOK, B)
        rsum1 = carve(SLOTS, 4, 2)

        region(KEEP, KEEP + SHARED)
        xh = carve(128, C, HT, HALO, PATCH + 2 * RAD)
        xc = carve(128, 2, KC, HT, 128)
        woff = carve(128, KC, 2 * KK)
        boff = carve(128, 2 * KK)
        wcv = carve(128, KC, D)
        off = carve(128, 2, 2, HT, KK)
        haty = carve(128, 2, HT, KK)
        hatx = carve(128, WIN, HT, KK)
        hat_t = carve(128, 2, HT, KK)
        prod_v = carve(128, 2, C, HT, KK)
        pool_at = place["at"]
        prod_p = carve(128, 2, C, HT, KK)
        w_p = carve(128, HT, KK)
        gen_more = carve(128, 4, NPOS)
        gen = arena[:, pool_at:pool_at + 11 * NPOS].rearrange("p (a n) -> p a n", n=NPOS)
        outl = carve(128, C, HT, KK)
        corner = carve(128, 12)
        corner_at, corner_idx = carve(128, 12), carve(128, 12)
        corner_val, corner_wv, corner_s = carve(128, C, 4), carve(128, C, 4), carve(128, C, 2)
        samp = carve(128, KC, HT, 128)
        convs = carve(DC, 2, HT, HT * 128)
        early = samp.rearrange("p k w n -> p (k w n)")[0:DC]
        wqT = early[:, 0:2 * D].rearrange("p (c n) -> p c n", c=2)
        wkT = early[:, 2 * D:4 * D + 2].rearrange("p (c n) -> p c n", c=2)
        bq = early[:, 4 * D + 2:4 * D + 4]

        region(KEEP, KEEP + SHARED)
        h = carve(TOK, B, D)
        patch_tok = carve(DC, 2, B, PT * PT)
        F2R = 2
        f1w = carve(DC + 1, 2, MS, 2, FF)
        f2w = carve(128, F2R, MS, FT, D)
        yT = carve(DC + 1, 2, SLOTS, B)
        temps_at = place["at"]
        xl = carve(TOK, 2, 2, D)
        xlT = carve(DC + 1, 3, 2, T2)
        uT = carve(DC + 1, 2, 2, T2)
        vt = carve(TOK, 3, 2, D)
        pt = carve(TOK, 2, 2, TOK)
        z = carve(TOK, 3, 2, D)
        tk = carve(TOK, 2, 2, D)
        tkT = carve(DC, 2, 2, T2)
        e1 = carve(SLOTS, 3, 2, TOK)
        e2 = carve(TOK, 2, 2, SLOTS)
        dT = carve(TOK, 2, 2, SLOTS)
        xn = carve(TOK, 2, 2, D)
        temps_end = place["at"]
        combT = carve(SLOTS, B, TOK)
        region(temps_at, KEEP + SHARED)
        ybuf = carve(SLOTS, B, D)
        g1 = carve(128, 1, FF)
        g1T = carve(128, 1, FT, 128)
        y2 = carve(128, 2, D)
        b2 = carve(128, 2, D)
        assert place["at"] <= temps_end

        psum = ctx.enter_context(nc.psum_tensor("psum", [128, 8 * 512], f32))
        bank = lambda n: psum[:, 512 * n:512 * n + 512]

        acc = psum[:, 0:KC * HT * 128]
        tap_w = psum[:, 5 * 512:5 * 512 + HT * KK].rearrange("p (w q) -> p w q", q=KK)
        off_ps = conv_ps = bank(7)
        tok_ps = bank(3)[0:PT * PT, 0:2 * D].rearrange("p (b d) -> p b d", d=D)
        l2_ps = bank(0)[0:TOK, 256:256 + 2 * SLOTS].rearrange("p (b s) -> p b s", s=SLOTS)
        tr_ps = bank(1)[0:DC, 0:2 * T2].rearrange("p (j t) -> p j t", t=T2)
        u_ps = bank(2)[0:DC + 1, 0:2 * T2].rearrange("p (j t) -> p j t", t=T2)
        v_ps = bank(4)[0:TOK, 0:2 * D].rearrange("p (b d) -> p b d", d=D)
        dT_ps = bank(7)[0:TOK, 0:2 * SLOTS].rearrange("p (b s) -> p b s", s=SLOTS)
        s_ps = bank(5)[0:TOK, 0:T2].rearrange("p (b t) -> p b t", t=TOK)
        y_ps = bank(5)[0:DC, 256:512].rearrange("p (b j s) -> p b j s", b=2, j=2)
        o_ps = bank(6)[0:TOK, 0:2 * D].rearrange("p (b d) -> p b d", d=D)
        l1_ps = bank(0)[0:SLOTS, 0:T2].rearrange("p (b t) -> p b t", t=TOK)
        cT_ps = bank(7)[0:SLOTS, 256:256 + T2].rearrange("p (b t) -> p b t", t=TOK)
        h1_ps = [psum[:, 1024 * q:1024 * q + 1024].rearrange("p (a n) -> p a n", n=512)[:, :, 0:FF // 2] for q in range(2)]
        h1T_ps = psum[:, 2048:2048 + FT * 128]
        y2_ps = bank(6)[:, 0:D]
        fin_ps = [bank(6)[0:TOK, 0:2 * D].rearrange("p (b d) -> p b d", d=D),
                  bank(7)[0:TOK, 0:2 * D].rearrange("p (b d) -> p b d", d=D)]

        def sem(name):
            return ctx.enter_context(nc.semaphore(name))

        ld_x, ld_first, ld_w, ld_qk, ld_cols, ld_const = [sem(f"ld_x{ck}") for ck in range(HT)], [sem(f"ld_first{k}") for k in range(KC)], sem("ld_w"), sem("ld_qk"), [sem("ld_cols2"), sem("ld_cols1")], sem("ld_const")
        ld_txt, ld_slots = sem("ld_txt"), sem("ld_slots")
        ld_f1, ld_f2 = [sem(f"ld_f1_{i}") for i in range(2)], [sem(f"ld_f2_{i}") for i in range(F2R)]
        ld_b2 = [sem(f"ld_b2_{i}") for i in range(2)]
        off_done, off_taken, off_maxed, off_checked = sem("off_done"), sem("off_taken"), sem("off_maxed"), sem("off_checked")
        hats, prod_v_done, prod_p_done = sem("hats"), sem("prod_v_done"), sem("prod_p_done")
        prod_v_used, prod_p_used, outl_used = sem("prod_v_used"), sem("prod_p_used"), sem("outl_used")
        samp_done, conv_done, conv_taken = sem("samp_done"), sem("conv_done"), sem("conv_taken")
        bn_var, bn_rstd, bn_affine, patches = sem("bn_var"), sem("bn_rstd"), sem("bn_affine"), sem("patches")
        grid_in_sb, exact_step = ([sem(f"{n}_{ck}") for ck in range(HT)] for n in ("grid_in_sb", "exact_step"))
        gathered = [sem(f"gathered_{n}") for n in range(HT * HT)]
        slot_sqd, slot_fd, slot_nd, slot_td, slot_td2 = sem("slot_sqd"), sem("slot_fd"), sem("slot_nd"), sem("slot_td"), sem("slot_td2")
        consts_made, gram_done, gram_taken = sem("consts_made"), sem("gram_done"), sem("gram_taken")
        v_step, a_step, g_step = sem("v_step"), sem("a_step"), sem("g_step")
        names = ("tokT_done h_patches var1_done rstd1_done xl_done xlT_done xlT_taken u_done u_taken "
                 "vproj_done v_taken score_done probs_done attn_done h_done var2_done a2_done z_done ssq_done f2_done "
                 "tok_done tkT_done tkT_taken logits_done max_done exp1_done exp2_done disp_done "
                 "cT_done dT_taken cT_taken xn_done y_done y_taken")
        s = {n: sem(n) for n in names.split()}
        fc1_done, gelu_done, h1T_done, h1T_taken, fc2_done, y2_done = (sem(n) for n in ("fc1_done", "gelu_done", "h1T_done", "h1T_taken", "fc2_done", "y2_done"))
        y_moved = [sem("y_moved0"), sem("y_moved1")]
        fin_done, out_done, stored = sem("fin_done"), sem("out_done"), sem("stored")

        def tap_owner(t):
            return "pool" if t % 3 == 2 and t // 3 < POOL_TAPS else "vector"
        OWN = [tap_owner(t) for t in range(TAPS)]
        V_TAPS = OWN.count("vector")

        def nth(t):
            return OWN[:t].count(OWN[t])

        def hat_count(ck, i, j):
            return ck * 2 * WIN + (max(1, j + 2) if i == 0 else WIN + 1 + i)

        def window(ck, i, j):
            return xh[:, :, :, PATCH * ck + i:PATCH * ck + i + PATCH, j:j + PATCH]

        def bcast_c(w):
            return pixels(w.unsqueeze(1).broadcast_to([128, C, HT, KK]))

        def pixels(v):
            return v.rearrange("p c w (r q) -> p c w r q", q=PATCH)

        def steps(g_of_stage):
            last = max(lag for _, lag in g_of_stage)
            for t in range(NG + last):
                for stage, lag in g_of_stage:
                    if 0 <= t - lag < NG:
                        yield stage, t - lag

        block = ctx.enter_context(nc.Block())

        @block.sync
        def _(sp):
            for k in range(KC):
                sp.dma_start(xc[:, 0, k], x_cols[0, :, k]).then_inc(ld_first[k], 16)
                sp.dma_start(woff[:, k, :], w_off[:, k, :]).then_inc(ld_first[k], 16)
            sp.dma_start(boff, b_off.partition_broadcast(128)).then_inc(ld_w, 16)
            sp.dma_start(ident, ident_in).then_inc(ld_w, 16)
            for dst, src in ((wqT, wq_t), (wkT, wk_t), (bq, b_q)):
                sp.dma_start(dst, src).then_inc(ld_qk, 16)
            for ck in range(HT):
                rows = slice(PATCH * ck + (2 * RAD if ck else 0), PATCH * (ck + 1) + 2 * RAD)
                sp.dma_start(xh.rearrange("p c w r q -> p (c w) r q")[:, :, rows, :],
                             x_halo.rearrange("p c w r q -> p (c w) r q")[:, :, rows, :]).then_inc(ld_x[ck], 16)
                if ck == 0:
                    sp.dma_start(xc[:, 1], x_cols[1]).then_inc(ld_cols[1], 16)
            for dst, src in ((wcv, w_conv), (decay, decay_in), (wv, w_v), (bv, b_v.partition_broadcast(TOK)),
                             (normw, norm_w.partition_broadcast(TOK)), (gam, bn_g), (bet, bn_b), (corner, corner_in)):
                sp.dma_start(dst, src).then_inc(ld_const, 16)
            sp.dma_start(slotv, slots).then_inc(ld_slots, 16)
            sp.dma_start(slotsc, scale).then_inc(ld_slots, 16)
            sp.wait_ge(off_done, HT)
            sp.dma_start(xc[:, 0], x_cols[2]).then_inc(ld_cols[0], 16)
            sp.wait_ge(samp_done, 2 * HT)
            sp.dma_start(h[PT * PT:TOK, :, :], txt.rearrange("b t d -> t b d")).then_inc(ld_txt, 16)

            sp.wait_ge(conv_taken, 2 * HT)
            for q in range(MG + 1):
                if q < MG:
                    if q >= 2:
                        sp.wait_ge(fc1_done, q - 1)
                    sp.dma_start(f1w[0:DC, q % 2], fc1[MS * q:MS * q + MS].rearrange("s p j f -> p s j f")).then_inc(ld_f1[q % 2], 16)
                    sp.dma_start(f1w[DC:DC + 1, q % 2, :, 0, :], fc1_b[MS * q:MS * q + MS].unsqueeze(0)).then_inc(ld_f1[q % 2], 16)
                r = q - 1
                if r >= 0:
                    if r >= F2R:
                        sp.wait_ge(fc2_done, r - F2R + 1)
                    sp.dma_start(f2w[:, r % F2R], fc2[MS * r:MS * r + MS].rearrange("s p j d -> p s j d")).then_inc(ld_f2[r % F2R], 16)
            sp.wait_ge(stored, 16 * (B // STORE + 1))

        @block.tensor
        def _(pe):
            def offsets(ck, wt):
                pe.wait_ge(ld_cols[ck % 2], 16)
                n = HT * ck + wt
                if n:
                    pe.wait_ge(off_taken, n)
                if ck >= 2 and wt == 0:
                    pe.wait_ge(conv_taken, 2 * (ck - 1))
                for k in range(KC):
                    last = nc.tensor.matmul(off_ps, xc[:, ck % 2, k, wt, :], woff[:, k, :], start=(k == 0), stop=(k == KC - 1))
                last.then_inc(off_done, 1)

            def transposed_sum(src, ck=0, first=False):
                for n in range(KC * HT):
                    k, wt = n // HT, n % HT
                    c, half = k // 2, k % 2
                    piece = src[:, c, wt, 128 * half:128 * half + 128]
                    if first and ck and n in (0, SAMP_HALF):
                        pe.wait_ge(samp_done, 2 * ck - 1 + (n > 0))
                    last = nc.tensor.matmul(acc[:, 128 * n:128 * n + 128], piece, ident, is_transpose=True,
                                            start=(first and n % 4 == 0), stop=True, skip_group_check=True)
                return last

            def convolve(ck):
                if ck == 0:
                    pe.wait_ge(ld_const, 16 * CONSTS)
                pe.wait_ge(samp_done, 2 * ck + 2)
                pe.wait_ge(off_taken, HT * min(ck + 2, HT))
                for oc in range(2):
                    if 2 * ck + oc:
                        pe.wait_ge(conv_taken, 2 * ck + oc)
                    for k in range(KC):
                        last = nc.tensor.matmul(conv_ps[0:DC, 0:HT * 128], wcv[:, k, DC * oc:DC * oc + DC],
                                                samp[:, k].rearrange("p w n -> p (w n)"), start=(k == 0), stop=(k == KC - 1))
                    last.then_inc(conv_done, 1)

            for k in range(KC):
                pe.wait_ge(ld_first[k], 32)
                for wt in range(HT):
                    last = nc.tensor.matmul(bank(wt), xc[:, 0, k, wt, :], woff[:, k, :], start=(k == 0), stop=(k == KC - 1))
                    if k == KC - 1:
                        last.then_inc(off_done, 1)
            pe.wait_ge(ld_qk, 48)
            for i in range(2):
                for c in range(2):
                    nc.tensor.matmul(bank(3 + i)[0:DC, 0:D + 1], wqT[:, c, DC * i:DC * i + DC], wkT[:, c, :], start=(c == 0), stop=(c == 1))
            for j in range(2):
                for c in range(2):
                    last = nc.tensor.matmul(bank(5)[0:DC + j, j:j + 1], wkT[:, c, DC * j:DC * j + DC + j], bq[:, c:c + 1], start=(c == 0), stop=(c == 1))
            last.then_inc(gram_done, 1)
            pe.wait_ge(gram_taken, 1)
            pe.wait_ge(ld_w, 32)
            for ck in range(HT):
                pe.wait_ge(off_checked, ck + 1)
                transposed_sum(outl, ck, True).then_inc(outl_used, 1)
                for t in range(TAPS):
                    if OWN[t] == "vector":
                        n = V_TAPS * ck + nth(t)
                        pe.wait_ge(prod_v_done, n + 1)
                        transposed_sum(prod_v[:, n % 2]).then_inc(prod_v_used, 1)
                    else:
                        n = POOL_TAPS * ck + nth(t)
                        pe.wait_ge(prod_p_done, n + 1)
                        transposed_sum(prod_p[:, n % 2]).then_inc(prod_p_used, 1)
                    if ck and t == 3:
                        convolve(ck - 1)
                    if ck + 1 < HT and t in OFF_AT:
                        offsets(ck + 1, OFF_AT.index(t))
            convolve(HT - 1)

            pe.wait_ge(slot_nd, 1)
            pe.wait_ge(conv_taken, 2 * HT)
            for j in range(2):
                last = nc.tensor.transpose(conv_ps[0:DC, SLOTS * j:SLOTS * j + SLOTS], slotn[:, DC * j:DC * j + DC], ident[0:SLOTS, 0:SLOTS])
            last.then_inc(slot_td, 1)
            pe.wait_ge(slot_td2, 1)
            pe.wait_ge(patches, 1)
            pe.wait_ge(consts_made, 2)

            def back_to_tokens(g):
                if g:
                    pe.wait_ge(s["h_patches"], g)
                for b in range(2):
                    for j in range(2):
                        last = nc.tensor.transpose(tok_ps[:, b, DC * j:DC * j + DC], patch_tok[:, j, 2 * g + b, :], ident[0:DC, 0:DC])
                last.then_inc(s["tokT_done"], 1)

            def normed_transpose(g):
                pe.wait_ge(s["xl_done"], g + 1)
                if g >= 1:
                    pe.wait_ge(s["xlT_taken"], g)
                if g >= 5:
                    pe.wait_ge(s["tkT_taken"], g - 4)
                for j in range(2):
                    for b in range(2):
                        last = nc.tensor.transpose(tr_ps[:, j, TOK * b:TOK * b + TOK], xl[:, g % 2, b, DC * j:DC * j + DC], ident[0:TOK, 0:TOK])
                last.then_inc(s["xlT_done"], 1)

            def project(g):
                pe.wait_ge(s["xlT_taken"], g + 1)
                if g:
                    pe.wait_ge(s["u_taken"], g)
                for j in range(2):
                    for i in range(2):
                        last = nc.tensor.matmul(u_ps[0:DC + j, j, :], gram[:, i, DC * j:DC * j + DC + j], xlT[0:DC, g % 3, i, :], start=(i == 0), stop=(i == 1))
                last.then_inc(s["u_done"], 1)
                if g:
                    pe.wait_ge(s["v_taken"], g)
                for b in range(2):
                    for j in range(2):
                        last = nc.tensor.matmul(v_ps[:, b, :], xlT[0:DC, g % 3, j, TOK * b:TOK * b + TOK], wv[:, j, :], start=(j == 0), stop=(j == 1))
                last.then_inc(s["vproj_done"], 1)

            def scores(g):
                pe.wait_ge(s["u_taken"], g + 1)
                if g:
                    pe.wait_ge(s["probs_done"], g)
                if g >= 6:
                    pe.wait_ge(s["y_taken"], g - 5)
                for b in range(2):
                    for j in range(2):
                        last = nc.tensor.matmul(s_ps[:, b, :], xlT[0:DC + j, g % 3, j, TOK * b:TOK * b + TOK], uT[0:DC + j, g % 2, j, TOK * b:TOK * b + TOK], start=(j == 0), stop=(j == 1))
                last.then_inc(s["score_done"], 1)

            def attend(g):
                pe.wait_ge(s["probs_done"], g + 1)
                pe.wait_ge(s["v_taken"], g + 1)
                if g:
                    pe.wait_ge(s["h_done"], g)
                for b in range(2):
                    last = nc.tensor.matmul(o_ps[:, b, :], pt[:, g % 2, b, :], vt[:, g % 3, b, :], start=True, stop=True)
                last.then_inc(s["attn_done"], 1)

            def directions_transpose(g):
                pe.wait_ge(s["tok_done"], g + 1)
                if g >= 1:
                    pe.wait_ge(s["tkT_taken"], g)
                pe.wait_ge(s["xlT_taken"], min(g + 5, NG))
                for j in range(2):
                    for b in range(2):
                        last = nc.tensor.transpose(tr_ps[:, j, TOK * b:TOK * b + TOK], tk[:, g % 2, b, DC * j:DC * j + DC], ident[0:TOK, 0:TOK])
                last.then_inc(s["tkT_done"], 1)

            def logits(g):
                pe.wait_ge(s["tkT_taken"], g + 1)
                if g:
                    pe.wait_ge(s["exp2_done"], g)
                for j in range(2):
                    nc.tensor.matmul(l1_ps.rearrange("p b t -> p (b t)"), slotT[:, j, :], tkT[:, g % 2, j, :], start=(j == 0), stop=(j == 1))
                for b in range(2):
                    for j in range(2):
                        last = nc.tensor.matmul(l2_ps[:, b, :], tkT[:, g % 2, j, TOK * b:TOK * b + TOK], slotT[:, j, :], start=(j == 0), stop=(j == 1))
                last.then_inc(s["logits_done"], 1)

            def weights_transpose(g):
                pe.wait_ge(s["disp_done"], g + 1)
                pe.wait_ge(s["exp2_done"], g + 1)
                if g:
                    pe.wait_ge(s["cT_taken"], g)
                for b in range(2):
                    nc.tensor.transpose(dT_ps[:, b, :], e1[:, g % 3, b, :], ident[0:SLOTS, 0:SLOTS])
                for b in range(2):
                    last = nc.tensor.transpose(cT_ps[:, b, :], e2[:, g % 2, b, :], ident[0:TOK, 0:TOK])
                last.then_inc(s["cT_done"], 1)

            def dispatch(g):
                pe.wait_ge(s["dT_taken"], g + 1)
                pe.wait_ge(s["xn_done"], g + 1)
                if g:
                    pe.wait_ge(s["y_taken"], g)
                pe.wait_ge(s["probs_done"], min(g + 6, NG))
                for b in range(2):
                    for j in range(2):
                        last = nc.tensor.matmul(y_ps[:, b, j, :], xn[:, g % 2, b, DC * j:DC * j + DC], dT[:, g % 2, b, :], start=True, stop=True)
                last.then_inc(s["y_done"], 1)

            for stage, g in steps([(dispatch, 10), (weights_transpose, 9), (logits, 8), (directions_transpose, 7), (attend, 5),
                                   (scores, 4), (project, 3), (normed_transpose, 2), (back_to_tokens, 0)]):
                stage(g)

            pe.wait_ge(s["y_taken"], NG)
            pe.wait_ge(s["cT_taken"], NG)

            def up(q):
                pe.wait_ge(ld_f1[q % 2], 32 * (q // 2 + 1))
                if q >= 2:
                    pe.wait_ge(gelu_done, q - 1)
                for half in range(2):
                    for j in range(2):
                        rows = DC + 1 - j
                        for i in range(MS):
                            last = nc.tensor.matmul(h1_ps[q % 2][32 * i:32 * i + 32, half, :], yT[0:rows, j, MS * q + i, :],
                                                    f1w[0:rows, q % 2, i, j, FF // 2 * half:FF // 2 * half + FF // 2],
                                                    start=(j == 0), stop=(j == 1), tile_position=(0, 32 * i))
                last.then_inc(fc1_done, 1)

            def turn(q):
                pe.wait_ge(gelu_done, q + 1)
                if q:
                    pe.wait_ge(h1T_taken, q)
                for j in range(FT):
                    last = nc.tensor.transpose(h1T_ps[:, 128 * j:128 * j + 128], g1[:, 0, 128 * j:128 * j + 128], ident)
                last.then_inc(h1T_done, 1)

            def down(q):
                pe.wait_ge(h1T_taken, q + 1)
                pe.wait_ge(ld_f2[q % F2R], 16 * (q // F2R + 1))
                if q:
                    pe.wait_ge(y2_done, q)
                for j in range(FT):
                    for i in range(MS):
                        last = nc.tensor.matmul(y2_ps[32 * i:32 * i + 32, :], g1T[:, 0, j, 32 * i:32 * i + 32], f2w[:, q % F2R, i, j, :],
                                                start=(j == 0), stop=(j == FT - 1), tile_position=(0, 32 * i))
                last.then_inc(fc2_done, 1)

            for q in range(MG + 1):
                if q:
                    turn(q - 1)
                if q < MG:
                    up(q)
                if q:
                    down(q - 1)

            pe.wait_ge(y2_done, MG)
            pe.wait_ge(y_moved[0], 16 * MS * MG // 2)
            pe.wait_ge(y_moved[1], 16 * MS * MG // 2)
            for g in range(NG):
                if g >= 2:
                    pe.wait_ge(out_done, g - 1)
                for b in range(2):
                    last = nc.tensor.matmul(fin_ps[g % 2][:, b, :], combT[:, 2 * g + b, :], ybuf[:, 2 * g + b, :], start=True, stop=True)
                last.then_inc(fin_done, 1)

        @block.vector
        def _(ve):
            n_step = [0]

            def then(ins):
                n_step[0] += 1
                ins.then_inc(v_step, 1)
                ve.wait_ge(v_step, n_step[0])

            def take_offsets(ck, wt):
                n = HT * ck + wt
                ve.wait_ge(off_done, n + 1)
                if ck >= 2 and wt == 0:
                    ve.wait_ge(hats, 2 * WIN * (ck - 1))
                nc.vector.tensor_tensor(off[:, ck % 2, :, wt, :], (bank(wt) if ck == 0 else off_ps).rearrange("p (a q) -> p a q", a=2),
                                        boff.rearrange("p (a q) -> p a q", a=2), ALU.add).then_inc(off_taken, 1)

            def max_offset(ck):
                ve.wait_ge(off_taken, HT * (ck + 1))
                nc.vector.tensor_reduce(off_max[:, ck:ck + 1], off[:, ck % 2].rearrange("p a w q -> p (a w q)"), AX.X, ALU.max,
                                        apply_absolute_value=True).then_inc(off_maxed, 1)

            ve.wait_ge(ld_w, 32)
            for wt in range(HT):
                take_offsets(0, wt)
            max_offset(0)
            for ck in range(HT):
                ve.wait_ge(ld_x[ck], 16)
                for t in range(TAPS):
                    if OWN[t] != "vector":
                        continue
                    i, j = t // WIN, t % WIN
                    n = V_TAPS * ck + nth(t)
                    ve.wait_ge(hats, hat_count(ck, i, j))
                    if n:
                        ve.wait_ge(prod_v_done, n)
                    then(nc.vector.tensor_tensor(tap_w, haty[:, (WIN * ck + i) % 2], hatx[:, j], ALU.mult))
                    if n >= 2:
                        ve.wait_ge(prod_v_used, n - 1)
                    nc.vector.tensor_tensor(pixels(prod_v[:, n % 2]), window(ck, i, j), bcast_c(tap_w), ALU.mult).then_inc(prod_v_done, 1)
                    if ck + 1 < HT and t in TAKE_AT:
                        take_offsets(ck + 1, TAKE_AT.index(t))
                    if ck + 1 < HT and t == TAKE_AT[-1]:
                        max_offset(ck + 1)

            for oc in range(2):
                for ck in range(HT):
                    ve.wait_ge(conv_taken, 2 * ck + oc + 1)
                    last = nc.vector.bn_stats(bn6[:, oc, ck, :], convs[:, oc, ck, :])
                then(last)
                nc.vector.bn_aggr(bn2[:, oc, :], bn6[:, oc].rearrange("p a b -> p (a b)")).then_inc(bn_var, 1)
            for oc in range(2):
                ve.wait_ge(bn_rstd, oc + 1)
                then(nc.vector.tensor_tensor(bn_s[:, oc:oc + 1], bn_r[:, oc:oc + 1], gam[:, oc:oc + 1], ALU.mult))
                then(nc.vector.tensor_tensor(bn_t[:, oc:oc + 1], bn2[:, oc, 0:1], bn_s[:, oc:oc + 1], ALU.mult))
                nc.vector.tensor_tensor(bn_t[:, oc:oc + 1], bet[:, oc:oc + 1], bn_t[:, oc:oc + 1], ALU.subtract).then_inc(bn_affine, 1)

            def variances(g, mv):
                for b in range(2):
                    last = nc.vector.bn_stats(st6[:, b, 0, :], h[:, 2 * g + b, :])
                then(last)
                for b in range(2):
                    last = nc.vector.bn_aggr(mv[:, b, :], st6[:, b, 0, :])
                return last

            def first_stats(g):
                ve.wait_ge(s["h_patches"], g + 1)
                if g == 0:
                    ve.wait_ge(ld_txt, 16)
                if g >= 4:
                    ve.wait_ge(s["xl_done"], g - 3)
                variances(g, mv1[:, g % 4]).then_inc(s["var1_done"], 1)

            def first_norm(g):
                ve.wait_ge(s["rstd1_done"], g + 1)
                if g >= 2:
                    ve.wait_ge(s["xlT_done"], g - 1)
                for b in range(2):
                    last = nc.vector.tensor_scalar(xl[:, g % 2, b, :], h[:, 2 * g + b, :], mv1[:, g % 4, b, 0:1], r1[:, g % 4, b:b + 1], ALU.subtract, ALU.mult)
                last.then_inc(s["xl_done"], 1)

            def values(g):
                ve.wait_ge(s["vproj_done"], g + 1)
                if g >= 3:
                    ve.wait_ge(s["attn_done"], g - 2)
                nc.vector.tensor_tensor(vt[:, g % 3], v_ps, bv.unsqueeze(1).broadcast_to([TOK, 2, D]), ALU.add).then_inc(s["v_taken"], 1)

            def decayed(g):
                ve.wait_ge(s["score_done"], g + 1)
                if g >= 2:
                    ve.wait_ge(s["attn_done"], g - 1)
                nc.vector.tensor_tensor(pt[:, g % 2], s_ps, decay.unsqueeze(1).broadcast_to([TOK, 2, TOK]), ALU.mult).then_inc(s["probs_done"], 1)

            def residual(g):
                ve.wait_ge(s["attn_done"], g + 1)
                ve.wait_ge(s["xl_done"], g + 1)
                last = nc.vector.tensor_tensor(h[:, 2 * g:2 * g + 2, :], o_ps, h[:, 2 * g:2 * g + 2, :], ALU.add)
                last.then_inc(s["h_done"], 1)
                ve.wait_ge(s["h_done"], g + 1)
                variances(g, mv2[:, g]).then_inc(s["var2_done"], 1)

            def weighted(g):
                ve.wait_ge(s["var2_done"], g + 1)
                if g >= 3:
                    ve.wait_ge(s["tok_done"], g - 2)
                for b in range(2):
                    last = nc.vector.scalar_tensor_tensor(z[:, g % 3, b, :], h[:, 2 * g + b, :], mv2[:, g, b, 0:1], normw, ALU.subtract, ALU.mult)
                last.then_inc(s["z_done"], 1)

            def unit(g):
                ve.wait_ge(s["f2_done"], g + 1)
                ve.wait_ge(s["z_done"], g + 1)
                if g >= 2:
                    ve.wait_ge(s["tkT_done"], g - 1)
                for b in range(2):
                    last = nc.vector.tensor_scalar(tk[:, g % 2, b, :], z[:, g % 3, b, :], f2[:, g % 4, b:b + 1], None, ALU.mult)
                last.then_inc(s["tok_done"], 1)

            def maxima(g):
                ve.wait_ge(s["logits_done"], g + 1)
                if g >= 4:
                    ve.wait_ge(s["exp1_done"], g - 3)
                nc.vector.tensor_reduce(nmax1[:, g % 4, :], l1_ps, AX.X, ALU.max, negate=True)
                if g >= 4:
                    ve.wait_ge(s["exp2_done"], g - 3)
                nc.vector.tensor_reduce(nmax2[:, g % 4, :], l2_ps, AX.X, ALU.max, negate=True).then_inc(s["max_done"], 1)

            def normed_dispatch(g):
                ve.wait_ge(s["exp1_done"], g + 1)
                then(nc.vector.reciprocal(rsum1[:, g % 4, :], sum1[:, g % 4, :]))
                for b in range(2):
                    last = nc.vector.tensor_scalar(e1[:, g % 3, b, :], e1[:, g % 3, b, :], rsum1[:, g % 4, b:b + 1], None, ALU.mult)
                last.then_inc(s["disp_done"], 1)

            def normed_tokens(g):
                if g >= 2:
                    ve.wait_ge(s["y_done"], g - 1)
                for b in range(2):
                    last = nc.vector.scalar_tensor_tensor(xn[:, g % 2, b, :], h[:, 2 * g + b, :], mv2[:, g, b, 0:1], normw, ALU.subtract, ALU.mult)
                last.then_inc(s["xn_done"], 1)

            for stage, g in steps([(weighted, 6), (unit, 7), (first_stats, 1), (maxima, 8), (normed_tokens, 9), (residual, 5), (decayed, 4),
                                   (values, 3), (first_norm, 1), (normed_dispatch, 8)]):
                stage(g)

            ve.wait_ge(s["exp2_done"], NG)
            then(nc.vector.reciprocal(rsum2, sum2))
            for q in range(MG):
                ve.wait_ge(h1T_done, q + 1)
                if q:
                    ve.wait_ge(fc2_done, q)
                else:
                    ve.wait_ge(s["y_done"], NG)
                nc.vector.tensor_copy(g1T[:, 0].rearrange("p a b -> p (a b)"), h1T_ps).then_inc(h1T_taken, 1)
                ve.wait_ge(fc2_done, q + 1)
                ve.wait_ge(ld_b2[q % 2], 16 * (q // 2 + 1))
                if q >= 2:
                    ve.wait_ge(y_moved[q % 2], 16 * MS * (q // 2))
                nc.vector.tensor_tensor(y2[:, q % 2, :], y2_ps, b2[:, q % 2, :], ALU.add).then_inc(y2_done, 1)
            for g in range(NG):
                ve.wait_ge(fin_done, g + 1)
                for b in range(2):
                    n = 2 * g + b
                    last = nc.vector.scalar_tensor_tensor(h[:, n, :], fin_ps[g % 2][:, b, :], rsum2[:, n:n + 1], h[:, n, :], ALU.mult, ALU.add)
                last.then_inc(out_done, 1)

        @block.scalar
        def _(ac):
            n_step = [0]

            def then(ins):
                n_step[0] += 1
                ins.then_inc(a_step, 1)
                ac.wait_ge(a_step, n_step[0])

            n_hat = [0]

            def hat(dst, src, center):
                n = n_hat[0]
                n_hat[0] += 1
                t = hat_t[:, n % 2]
                if n >= 2:
                    ac.wait_ge(hats, n - 1)
                then(nc.scalar.activation(t, src, ACT.Abs, bias=-float(center)))
                nc.scalar.activation(dst, t, ACT.Relu, bias=1.0, scale=-1.0).then_inc(hats, 1)

            def last_use(ck, i, j):
                t = WIN * i + j
                v = V_TAPS * ck + OWN[:t + 1].count("vector")
                p = POOL_TAPS * ck + OWN[:t + 1].count("pool")
                if v:
                    ac.wait_ge(prod_v_done, v)
                if p:
                    ac.wait_ge(prod_p_done, p)

            def hat_row(ck, i):
                r = WIN * ck + i
                if r >= 2:
                    last_use((r - 2) // WIN, (r - 2) % WIN, WIN - 1)
                hat(haty[:, r % 2], off[:, ck % 2, 0], i - RAD)

            def first_hats(ck):
                ac.wait_ge(off_checked, ck + 1)
                hat_row(ck, 0)
                for j in range(WIN):
                    if ck:
                        last_use(ck - 1, WIN - 1, j)
                    hat(hatx[:, j], off[:, ck % 2, 1], j - RAD)
                hat_row(ck, 1)

            ac.wait_ge(gram_done, 1)
            for i in range(2):
                nc.scalar.activation(gram[:, i, :], bank(3 + i)[0:DC, 0:D + 1], ACT.Copy)
            nc.scalar.activation(gram0[0:DC, 0:1], bank(5)[0:DC, 0:1], ACT.Copy)
            nc.scalar.activation(gram0[:, 1:2], bank(5)[0:DC + 1, 1:2], ACT.Copy).then_inc(gram_taken, 1)
            ac.wait_ge(ld_slots, 32)
            nc.scalar.activation(slotn, slotv, ACT.Square, accum_out=slot_sq).then_inc(slot_sqd, 1)
            first_hats(0)
            for ck in range(HT):
                for i in range(2, WIN):
                    hat_row(ck, i)
                if ck + 1 < HT:
                    first_hats(ck + 1)
                ac.wait_ge(prod_v_used, V_TAPS * (ck + 1))
                ac.wait_ge(prod_p_used, POOL_TAPS * (ck + 1))
                if ck:
                    ac.wait_ge(conv_done, 2 * ck)
                flat_samp = samp.rearrange("p k w n -> p (k w n)")
                nc.scalar.activation(flat_samp[:, 0:128 * SAMP_HALF], acc[:, 0:128 * SAMP_HALF], ACT.Copy).then_inc(samp_done, 1)
                nc.scalar.activation(flat_samp[:, 128 * SAMP_HALF:], acc[:, 128 * SAMP_HALF:], ACT.Copy).then_inc(samp_done, 1)
                for oc in range(2):
                    ac.wait_ge(conv_done, 2 * ck + oc + 1)
                    nc.scalar.activation(convs[:, oc, ck, :], conv_ps[0:DC, 0:HT * 128], ACT.Copy).then_inc(conv_taken, 1)

            ac.wait_ge(slot_td, 1)
            nc.scalar.activation(slotT.rearrange("p j s -> p (j s)"), conv_ps[0:DC, 0:2 * SLOTS], ACT.Copy).then_inc(slot_td2, 1)
            for oc in range(2):
                ac.wait_ge(bn_affine, oc + 1)
                for hot in range(HT):
                    for hop in range(2):
                        src = convs[:, oc, hot, :].rearrange("p (wt hp wp b) -> p hp wt wp b", wt=HT, hp=2, wp=2)[:, hop]
                        dst = patch_tok[:, oc].rearrange("p b (hp ht wp wt) -> p hp ht wt wp b", hp=2, ht=HT, wp=2)[:, hop, hot]
                        last = nc.scalar.activation(dst, src, ACT.Gelu, bias=bn_t[:, oc:oc + 1], scale=bn_s[:, oc:oc + 1])
            last.then_inc(patches, 1)

            def take_patches(g):
                ac.wait_ge(s["tokT_done"], g + 1)
                nc.scalar.activation(h[0:PT * PT, 2 * g:2 * g + 2, :], tok_ps, ACT.Copy).then_inc(s["h_patches"], 1)

            def take_normed(g):
                ac.wait_ge(s["xlT_done"], g + 1)
                if g >= 3:
                    ac.wait_ge(s["score_done"], g - 2)
                nc.scalar.activation(xlT[0:DC, g % 3], tr_ps, ACT.Copy).then_inc(s["xlT_taken"], 1)

            def take_queries(g):
                ac.wait_ge(s["u_done"], g + 1)
                if g >= 2:
                    ac.wait_ge(s["score_done"], g - 1)
                for j in range(2):
                    last = nc.scalar.activation(uT[0:DC + j, g % 2, j, :], u_ps[0:DC + j, j, :], ACT.Identity, bias=gram0[0:DC + j, j:j + 1])
                last.then_inc(s["u_taken"], 1)

            def squares(g):
                ac.wait_ge(s["z_done"], g + 1)
                if g >= 4:
                    ac.wait_ge(s["f2_done"], g - 3)
                if g >= 2:
                    ac.wait_ge(s["tkT_done"], g - 1)
                for b in range(2):
                    last = nc.scalar.activation(tk[:, g % 2, b, :], z[:, g % 3, b, :], ACT.Square, accum_out=ssq[:, g % 4, b:b + 1])
                last.then_inc(s["ssq_done"], 1)

            def take_directions(g):
                ac.wait_ge(s["tkT_done"], g + 1)
                if g >= 2:
                    ac.wait_ge(s["logits_done"], g - 1)
                nc.scalar.activation(tkT[:, g % 2], tr_ps, ACT.Copy).then_inc(s["tkT_taken"], 1)

            def exps(g):
                ac.wait_ge(s["max_done"], g + 1)
                if g >= 3:
                    ac.wait_ge(s["cT_done"], g - 2)
                for b in range(2):
                    last = nc.scalar.activation(e1[:, g % 3, b, :], l1_ps[:, b, :], ACT.Exp, bias=nmax1[:, g % 4, b:b + 1], accum_out=sum1[:, g % 4, b:b + 1])
                last.then_inc(s["exp1_done"], 1)
                if g >= 2:
                    ac.wait_ge(s["cT_done"], g - 1)
                for b in range(2):
                    last = nc.scalar.activation(e2[:, g % 2, b, :], l2_ps[:, b, :], ACT.Exp, bias=nmax2[:, g % 4, b:b + 1], accum_out=sum2[:, 2 * g + b:2 * g + b + 1])
                last.then_inc(s["exp2_done"], 1)

            def take_weights(g):
                ac.wait_ge(s["cT_done"], g + 1)
                if g >= 2:
                    ac.wait_ge(s["y_done"], g - 1)
                for b in range(2):
                    last = nc.scalar.activation(dT[:, g % 2, b, :], dT_ps[:, b, :], ACT.Copy, scale=a2[:, g, b:b + 1])
                last.then_inc(s["dT_taken"], 1)
                nc.scalar.activation(combT[:, 2 * g:2 * g + 2, :], cT_ps, ACT.Copy).then_inc(s["cT_taken"], 1)

            def take_dispatched(g):
                ac.wait_ge(s["y_done"], g + 1)
                nc.scalar.activation(yT[0:DC, :, :, 2 * g:2 * g + 2].rearrange("p j s b -> p b j s"), y_ps, ACT.Copy).then_inc(s["y_taken"], 1)

            for stage, g in steps([(take_dispatched, 10), (take_weights, 9), (take_directions, 7), (squares, 6), (exps, 8),
                                   (take_queries, 3), (take_normed, 2), (take_patches, 0)]):
                stage(g)

            for q in range(MG + 1):
                if q < MG:
                    if q == 0:
                        ac.wait_ge(s["y_done"], NG)
                    if q < 2:
                        ac.dma_start(b2[:, q % 2, :], fc2_b[q]).then_inc(ld_b2[q % 2], 16)
                    ac.wait_ge(fc1_done, q + 1)
                    if q:
                        ac.wait_ge(h1T_done, q)
                    nc.scalar.activation(g1[:, 0].rearrange("p (a n) -> p a n", a=2), h1_ps[q % 2], ACT.Gelu).then_inc(gelu_done, 1)
                if q:
                    p = q - 1
                    ac.wait_ge(y2_done, p + 1)
                    for i in range(MS):
                        n = MS * p + i
                        ac.dma_start(ybuf[n:n + 1, :, :], y2[32 * i:32 * i + 32, p % 2, :]).then_inc(y_moved[p % 2], 16)
                    if p + 2 < MG:
                        ac.dma_start(b2[:, p % 2, :], fc2_b[p + 2]).then_inc(ld_b2[p % 2], 16)

            for n in range(0, B, STORE):
                ac.wait_ge(out_done, (n + STORE) // 2)
                ac.dma_start(out[n:n + STORE, 0:TOK - 1].rearrange("b t d -> t b d"), h[0:TOK - 1, n:n + STORE, :]).then_inc(stored, 16)
            ac.dma_start(out[:, TOK - 1:TOK].rearrange("b t d -> t b d"), h[TOK - 1:TOK]).then_inc(stored, 16)
            ac.wait_ge(stored, 16 * (B // STORE + 1))

        @block.gpsimd
        def _(gp):
            n_step = [0]

            def then(ins):
                n_step[0] += 1
                ins.then_inc(g_step, 1)
                gp.wait_ge(g_step, n_step[0])

            nc.gpsimd.memset(half_neg, -0.5)
            nc.gpsimd.memset(outl, 0.0).then_inc(consts_made, 1)
            gp.wait_ge(ld_const, 16 * CONSTS)
            gp.wait_ge(consts_made, 1)

            def gather_outliers(ck):
                py, px, ry, rx, ti, w0, w1, w2, w3, mask, t = (gen[:, n] for n in range(11))
                dy, dx = off[:, ck % 2, 0].rearrange("p w q -> p (w q)"), off[:, ck % 2, 1].rearrange("p w q -> p (w q)")
                count = [0]

                def run(ins):
                    count[0] += 1
                    ins.then_inc(exact_step[ck], 1)
                    gp.wait_ge(exact_step[ck], count[0])

                if pool_made[0]:
                    gp.wait_ge(prod_p_used, pool_made[0])
                gp.dma_start(gen[:, 0:2], grid_in[ck]).then_inc(grid_in_sb[ck], 16)
                gp.wait_ge(grid_in_sb[ck], 16)
                ts, tt = nc.gpsimd.tensor_scalar, nc.gpsimd.tensor_tensor
                run(tt(py, py, dy, ALU.add))
                run(tt(px, px, dx, ALU.add))
                run(tt(mask, dy, dy, ALU.mult))
                run(ts(mask, mask, float(RAD * RAD), None, ALU.is_gt))
                run(tt(t, dx, dx, ALU.mult))
                run(ts(t, t, float(RAD * RAD), None, ALU.is_gt))
                run(tt(mask, mask, t, ALU.add))
                run(ts(mask, mask, 1.0, None, ALU.min))
                for pos, low in ((py, ry), (px, rx)):
                    run(ts(low, pos, 0.0, float(IMG - 2), ALU.max, ALU.min))
                    run(nc.gpsimd.tensor_copy(ti.bitcast(i32), low))
                    run(nc.gpsimd.tensor_copy(t, ti.bitcast(i32)))
                    run(tt(low, t, low, ALU.subtract))
                    run(ts(low, low, 0.0, None, ALU.is_gt))
                    run(tt(low, t, low, ALU.subtract))

                def pair(pos, low, near, far):
                    run(tt(pos, pos, low, ALU.subtract))
                    for dst, shift in ((near, 0.0), (far, 1.0)):
                        run(ts(dst, pos, -1.0, 1.0 + shift, ALU.mult, ALU.add))
                        run(ts(dst, dst, 0.0, 1.0, ALU.max, ALU.min))
                        run(ts(t, pos, 1.0 - shift, None, ALU.add))
                        run(ts(t, t, 0.0, 1.0, ALU.max, ALU.min))
                        run(tt(dst, dst, t, ALU.mult))

                pair(py, ry, w0, w2)
                pair(px, rx, w1, w3)
                run(tt(w0, w0, mask, ALU.mult))
                run(tt(w2, w2, mask, ALU.mult))
                run(tt(ti, w0, w1, ALU.mult))
                run(tt(py, w0, w3, ALU.mult))
                run(tt(px, w2, w1, ALU.mult))
                run(tt(w3, w2, w3, ALU.mult))
                run(nc.gpsimd.tensor_copy(w0, ti))
                run(nc.gpsimd.tensor_copy(w1, py))
                run(nc.gpsimd.tensor_copy(w2, px))
                run(ts(ry, ry, float(IMG), None, ALU.mult))
                run(tt(ry, ry, rx, ALU.add))
                run(ts(dy, dy, -3.0, 3.0, ALU.max, ALU.min))
                run(ts(mask, mask, 1e6, None, ALU.mult))
                run(tt(dy, dy, mask, ALU.add))
                quad = gen[:, 5:9].rearrange("p k (w q) -> p k w q", q=KK)
                place_in = ry.rearrange("p (w q) -> p w q", q=KK)
                for wt in range(HT):
                    tile_gathered = gathered[HT * ck + wt]
                    with gp.Fori(0, KK) as q:
                        nc.gpsimd.tensor_tensor(corner_at, place_in[:, wt, bass.ds(q, 1)].broadcast_to([128, 12]), corner, ALU.add)
                        gp.drain()
                        nc.gpsimd.tensor_copy(corner_idx.bitcast(i32), corner_at)
                        gp.drain()
                        for n in range(12):
                            gp.indirect_dma_start(corner_val.rearrange("p c k -> p (c k)")[:, n:n + 1], None, x_flat,
                                                  bass.IndirectOffsetOnAxis(ap=corner_idx.bitcast(u32)[:, n:n + 1], axis=0)).then_inc(tile_gathered, 16)
                        gp.wait_ge(tile_gathered, (q + 1) * (16 * 12))
                        nc.gpsimd.tensor_tensor(corner_wv, corner_val, quad[:, :, wt, bass.ds(q, 1)].rearrange("p k o -> p o k").broadcast_to([128, C, 4]), ALU.mult)
                        gp.drain()
                        nc.gpsimd.tensor_tensor(corner_s, corner_wv[:, :, 0:2], corner_wv[:, :, 2:4], ALU.add)
                        gp.drain()
                        nc.gpsimd.tensor_tensor(outl[:, :, wt, bass.ds(q, 1)], corner_s[:, :, 0:1], corner_s[:, :, 1:2], ALU.add)
                        gp.drain()

            pool_made = [0]

            def check_offsets(ck):
                gp.wait_ge(off_maxed, ck + 1)
                if ck:
                    gp.wait_ge(outl_used, ck)
                    then(nc.gpsimd.memset(outl, 0.0))
                then(nc.gpsimd.partition_all_reduce(off_all[:, ck:ck + 1], off_max[:, ck:ck + 1], 128, bass.bass_isa.ReduceOp.max))
                far = gp.value_load(off_all[0:1, ck:ck + 1].bitcast(i32))
                with gp.If(far > int(np.float32(RAD).view(np.int32))):
                    gather_outliers(ck)
                nc.gpsimd.nop().then_inc(off_checked, 1)

            check_offsets(0)
            gp.wait_ge(slot_sqd, 1)
            then(nc.gpsimd.tensor_scalar(slot_f, slot_sq, EPS * EPS, None, ALU.max))
            then(nc.gpsimd.tensor_tensor(slot_f, slot_f, half_neg[0:SLOTS, 0:1], ALU.pow))
            then(nc.gpsimd.tensor_tensor(slot_f, slot_f, slotsc, ALU.mult))
            nc.gpsimd.tensor_tensor(slotn, slotv, slot_f.broadcast_to([SLOTS, D]), ALU.mult).then_inc(slot_nd, 1)

            for ck in range(HT):
                gp.wait_ge(ld_x[ck], 16)
                for t in range(TAPS):
                    if OWN[t] != "pool":
                        continue
                    i, j = t // WIN, t % WIN
                    n = POOL_TAPS * ck + nth(t)
                    gp.wait_ge(hats, hat_count(ck, i, j))
                    if n:
                        gp.wait_ge(prod_p_done, n)
                    then(nc.gpsimd.tensor_tensor(w_p, haty[:, (WIN * ck + i) % 2], hatx[:, j], ALU.mult))
                    if n >= 2:
                        gp.wait_ge(prod_p_used, n - 1)
                    nc.gpsimd.tensor_tensor(pixels(prod_p[:, n % 2]), window(ck, i, j), bcast_c(w_p), ALU.mult).then_inc(prod_p_done, 1)
                    pool_made[0] = n + 1
                    if ck + 1 < HT and nth(t) == 6:
                        check_offsets(ck + 1)

            for oc in range(2):
                gp.wait_ge(bn_var, oc + 1)
                then(nc.gpsimd.tensor_scalar(bn_r[:, oc:oc + 1], bn2[:, oc, 1:2], EPS, None, ALU.add))
                nc.gpsimd.tensor_tensor(bn_r[:, oc:oc + 1], bn_r[:, oc:oc + 1], half_neg[0:DC, 0:1], ALU.pow).then_inc(bn_rstd, 1)
            gp.wait_ge(samp_done, 2 * HT)
            nc.gpsimd.memset(xlT[DC:DC + 1, :, 1, :], 1.0)
            nc.gpsimd.memset(yT[DC:DC + 1, 0], 1.0).then_inc(consts_made, 1)
            gp.wait_ge(consts_made, 2)

            def first_rstd(g):
                gp.wait_ge(s["var1_done"], g + 1)
                if g >= 4:
                    gp.wait_ge(s["xl_done"], g - 3)
                then(nc.gpsimd.tensor_scalar(r1[:, g % 4, :], mv1[:, g % 4, :, 1], EPS, None, ALU.add))
                nc.gpsimd.tensor_tensor(r1[:, g % 4, :], r1[:, g % 4, :], half_neg[0:TOK, 0:2], ALU.pow).then_inc(s["rstd1_done"], 1)

            def second_factor(g):
                gp.wait_ge(s["var2_done"], g + 1)
                then(nc.gpsimd.tensor_scalar(a2[:, g, :], mv2[:, g, :, 1], 1.0 + EPS, EPS * EPS, ALU.mult, ALU.add))
                nc.gpsimd.tensor_tensor(a2[:, g, :], a2[:, g, :], half_neg[0:TOK, 0:2], ALU.pow).then_inc(s["a2_done"], 1)

            def unit_factor(g):
                gp.wait_ge(s["ssq_done"], g + 1)
                if g >= 4:
                    gp.wait_ge(s["tok_done"], g - 3)
                gp.wait_ge(s["a2_done"], g + 1)
                then(nc.gpsimd.tensor_tensor(tmp2[:, g % 4, :], a2[:, g, :], a2[:, g, :], ALU.mult))
                then(nc.gpsimd.tensor_tensor(tmp2[:, g % 4, :], tmp2[:, g % 4, :], ssq[:, g % 4, :], ALU.mult))
                then(nc.gpsimd.tensor_scalar(tmp2[:, g % 4, :], tmp2[:, g % 4, :], EPS * EPS, None, ALU.max))
                then(nc.gpsimd.tensor_tensor(tmp2[:, g % 4, :], tmp2[:, g % 4, :], half_neg[0:TOK, 0:2], ALU.pow))
                nc.gpsimd.tensor_tensor(f2[:, g % 4, :], tmp2[:, g % 4, :], a2[:, g, :], ALU.mult).then_inc(s["f2_done"], 1)

            for stage, g in steps([(unit_factor, 5), (second_factor, 4), (first_rstd, 0)]):
                stage(g)


_OUT = (B, TOK, D)


def kernel(x, txt, L0_tok_offset_w, L0_tok_offset_b, L0_tok_dconv_w, L0_tok_bn_gamma, L0_tok_bn_beta, L0_attn_W_qkv,
           L0_attn_b_qkv, L0_ffn_slots, L0_ffn_scale, L0_ffn_fc1_weight, L0_ffn_fc1_bias, L0_ffn_fc2_weight,
           L0_ffn_fc2_bias, L0_ffn_norm_weight):
    import concourse.bacc as bacc
    from concourse.bass_utils import run_bass_kernel_spmd

    x = np.asarray(x)
    halves = 2
    padded = np.zeros((B, C, IMG + 2 * RAD, IMG + 2 * RAD), x.dtype)
    padded[:, :, RAD:RAD + IMG, RAD:RAD + IMG] = x
    wide = PATCH + 2 * RAD
    halo = np.stack([np.stack([padded[:, :, QW * hp:QW * hp + HALO, QW * wp + PATCH * wt:QW * wp + PATCH * wt + wide] for wt in range(HT)], axis=2)
                     for hp in range(2) for wp in range(2)])
    cols = x.reshape(B, C, 2, HT, halves, 8, 2, HT, PATCH).transpose(3, 5, 8, 1, 4, 7, 2, 6, 0)
    w_off = np.asarray(L0_tok_offset_w).reshape(KK, 2, C, halves, 128).transpose(4, 2, 3, 1, 0)
    w_conv = np.asarray(L0_tok_dconv_w).reshape(D, C, halves, 128).transpose(3, 1, 2, 0)
    w_qkv, b_qkv = np.asarray(L0_attn_W_qkv), np.asarray(L0_attn_b_qkv)
    i = np.arange(TOK)
    gap = i[None, :] - i[:, None]
    decay = np.where(gap >= 0, np.float32(ALPHA) ** np.maximum(gap, 0).astype(np.float32), 0) / np.sqrt(np.float32(D))
    p = np.arange(128)
    hop, wop, b = p // 64, p // 32 % 2, p % 32
    r = np.arange(PATCH)
    wt = np.arange(HT)[None, :, None, None]
    grid = np.zeros((HT, 128, 2, HT, PATCH, PATCH), np.float32)
    for ck in range(HT):
        grid[ck, :, 0] = QW * hop[:, None, None, None] + PATCH * ck + r[None, None, :, None]
        grid[ck, :, 1] = QW * wop[:, None, None, None] + PATCH * wt + r[None, None, None, :]
    corner = (b[:, None, None] * C + np.arange(C)[None, :, None]) * IMG * IMG + np.array([0, 1, IMG, IMG + 1])[None, None, :]
    arrays = {
        "x_halo": halo.reshape(128, C, HT, HALO, wide),
        "x_cols": cols.reshape(HT, 128, KC, HT, 128),
        "x_flat": x.reshape(-1, 1),
        "w_off": w_off.reshape(128, KC, 2 * KK),
        "b_off": np.asarray(L0_tok_offset_b).reshape(KK, 2).T.reshape(2 * KK),
        "w_conv": w_conv.reshape(128, KC, D),
        "bn_g": np.asarray(L0_tok_bn_gamma).reshape(2, DC).T,
        "bn_b": np.asarray(L0_tok_bn_beta).reshape(2, DC).T,
        "txt": np.asarray(txt),
        "wq_t": w_qkv[:, 0:D].T.reshape(2, DC, D).transpose(1, 0, 2),
        "wk_t": np.concatenate([w_qkv[:, D:2 * D].T, b_qkv[D:2 * D, None]], axis=1).reshape(2, DC, D + 1).transpose(1, 0, 2),
        "b_q": b_qkv[:D].reshape(2, DC).T,
        "w_v": w_qkv[:, 2 * D:].reshape(2, DC, D).transpose(1, 0, 2),
        "b_v": b_qkv[2 * D:],
        "slots": np.asarray(L0_ffn_slots),
        "scale": np.asarray(L0_ffn_scale).reshape(SLOTS, 1),
        "fc1": np.asarray(L0_ffn_fc1_weight).reshape(SLOTS, 2, DC, FF).transpose(0, 2, 1, 3),
        "fc1_b": np.asarray(L0_ffn_fc1_bias),
        "fc2": np.asarray(L0_ffn_fc2_weight).reshape(SLOTS, FT, 128, D).transpose(0, 2, 1, 3),
        "fc2_b": np.repeat(np.asarray(L0_ffn_fc2_bias), B, axis=0).reshape(MG, MS * B, D),
        "norm_w": np.asarray(L0_ffn_norm_weight),
        "ident_in": np.eye(128, dtype=np.float32),
        "decay_in": decay.astype(np.float32),
        "grid_in": grid.reshape(HT, 128, 2, NPOS),
        "corner_in": corner.reshape(128, 12).astype(np.float32),
    }
    arrays = {n: np.ascontiguousarray(a) for n, a in arrays.items()}
    nc = bacc.Bacc("TRN2", target_bir_lowering=False, num_devices=1)
    args = [nc.dram_tensor(n, a.shape, mybir.dt.from_np(a.dtype), kind="ExternalInput").ap() for n, a in arrays.items()]
    out = nc.dram_tensor("out", _OUT, mybir.dt.float32, kind="ExternalOutput").ap()
    fusion_program(nc, *args, out)
    return run_bass_kernel_spmd(nc, [arrays], core_ids=[0]).results[0]["out"]
```

```python
import numpy as np

import concourse.bass as bass
from concourse import mybir
from contextlib import ExitStack

B, C, IMG, PATCH = 32, 3, 96, 16
D, TXT, SLOTS, FF = 192, 77, 64, 768
PT = 6
HT = PT // 2
TOK = PT * PT + TXT
RAD = 1
WIN = 2 * RAD + 1
QW = HT * PATCH
HALO = QW + 2 * RAD
NPOS = PATCH * QW
KK = PATCH * PATCH
KC = C * KK // 128
TAPS = WIN * WIN
DC = D // 2
NG = B // 2
T2 = 2 * TOK
MS = 4
MG = SLOTS // MS
FT = FF // 128
ALPHA, EPS = 0.99, 1e-5
BEST = 8
PRODS = 3
FAR = BEST - 1
CORN = 4 * C
OFF_AT = (2, 4, 6)
TAKE_AT = (4, 6, 8)
MASK_AT = (5, 3)
SAMP_CUT = (0, 4, 8, 12, KC * HT)
PIECES = len(SAMP_CUT) - 1
CONSTS = 7
STORE = 4
R1, R2 = 8, 17
HB = B // 2


def fusion_program(nc, x_halo, x_cols, x_quads, w_off, b_off, w_conv, bn_g, bn_b, txt, wq_t, wk_t, b_q, w_v, b_v,
                   slots, scale, fc1, fc1_b, fc2, fc2_b, norm_w, ident_in, decay_in, grid_in, base_in, off_d, far_d, out):
    f32, i32, u32 = mybir.dt.float32, mybir.dt.int32, mybir.dt.uint32
    ALU, ACT, AX = mybir.AluOpType, mybir.ActivationFunctionType, mybir.AxisListType
    ctx = ExitStack()
    with ctx:
        KEEP, SHARED = 2304, 49792
        arena = ctx.enter_context(nc.sbuf_tensor("arena", [128, KEEP + SHARED], f32))
        place = {"at": 0, "end": KEEP}

        def region(at, end):
            place["at"], place["end"] = at, end

        def carve(parts, *shape):
            n = int(np.prod(shape))
            at = place["at"]
            place["at"] = at + n
            assert place["at"] <= place["end"], (place, shape)
            v = arena[0:parts, at:at + n]
            names = "abcde"[:len(shape)]
            if len(shape) == 1:
                return v
            return v.rearrange("p (" + " ".join(names) + ") -> p " + " ".join(names),
                               **{names[i]: shape[i] for i in range(len(shape))})

        ident = carve(128, 128)
        decay = carve(TOK, TOK)
        wv = carve(DC, 2, D)
        gram = carve(DC, 2, D + 1)
        gram0 = carve(DC + 1, 2)
        bv = carve(TOK, D)
        normw = carve(TOK, D)
        gam, bet = carve(DC, 2), carve(DC, 2)
        slotv, slotsc = carve(SLOTS, D), carve(SLOTS, 1)
        slot_sq, slot_f = carve(SLOTS, 1), carve(SLOTS, 1)
        slotn = carve(SLOTS, D)
        slotT = carve(DC, 2, SLOTS)
        half_neg = carve(128, 2)
        bn6, bn2 = carve(DC, 2, HT, 6), carve(DC, 2, 2)
        bn_r, bn_s, bn_t = carve(DC, 2), carve(DC, 2), carve(DC, 2)
        off_all = carve(128, HT)
        st6 = carve(TOK, 4, 2, 6)
        mv1, mv2 = carve(TOK, 4, 2, 2), carve(TOK, 16, 2, 2)
        r1 = carve(TOK, 4, 2)
        a2 = carve(TOK, 16, 2)
        ssq, f2 = carve(TOK, 4, 2), carve(TOK, 4, 2)
        tmp2 = carve(TOK, 4, 2)
        nmax1, sum1 = carve(SLOTS, 4, 2), carve(SLOTS, 4, 2)
        nmax2 = carve(TOK, 4, 2)
        sum2, rsum2 = carve(TOK, B), carve(TOK, B)
        rsum1 = carve(SLOTS, 4, 2)

        region(KEEP, KEEP + SHARED)
        xh = carve(128, C, HT, HALO, PATCH + 2 * RAD)
        xc = carve(128, 2, KC, HT, 128)
        woff = carve(128, KC, 2 * KK)
        boff = carve(128, 2 * KK)
        wcv = carve(128, KC, D)
        off = carve(128, HT, HT, KK, 2)
        off_in = carve(128, 2, HT, KK)
        off_abs = carve(128, HT, KK)
        haty = carve(128, 2, WIN, HT, KK)
        hatx = carve(128, 2, WIN, HT, KK)
        prod_v = carve(128, PRODS, C, HT, KK)
        gen = xc.rearrange("p a k w n -> p (a k w n)")[:, 0:13 * KK].rearrange("p (a n) -> p a n", n=KK)
        outl = carve(128, HT, KK, C)
        zeros = carve(128, NPOS)
        base = carve(128, 2 + 2 * HT)
        far_val, far_idx = carve(128, HT, BEST), carve(128, HT, BEST)
        far_off, far_row, far_at, far_pix = carve(128, 2, FAR, 2), carve(128, 2, FAR), carve(128, 2, FAR), carve(128, FAR)
        far_gen = carve(128, 2, 13, FAR)
        far_quad, far_wv = carve(128, FAR, CORN), carve(128, FAR, C, 4)
        far_s, far_sum = carve(128, FAR, C, 2), carve(128, FAR, C)
        quad_at = carve(128, 1)
        quad_val, quad_wv, quad_s = carve(128, CORN), carve(128, C, 4), carve(128, C, 2)
        samp = carve(128, KC, HT, 128)
        convs = carve(DC, 2, HT, HT * 128)
        early = samp.rearrange("p k w n -> p (k w n)")[0:DC]
        wqT = early[:, 0:2 * D].rearrange("p (c n) -> p c n", c=2)
        wkT = early[:, 2 * D:4 * D + 2].rearrange("p (c n) -> p c n", c=2)
        bq = early[:, 4 * D + 2:4 * D + 4]

        region(KEEP, KEEP + SHARED)
        h = carve(TOK, B, D)
        patch_at = place["at"]
        patch_tok = carve(DC, 2, B, PT * PT)
        F2N = FT * D
        f2_main = 11
        f2_at = [place["at"] + F2N * r for r in range(f2_main)]
        carve(128, f2_main, FT, D)
        f2_patch = 2 * B * PT * PT // F2N
        f2_at += [patch_at + F2N * r for r in range(f2_patch)]
        f1w = carve(DC + 1, R1, 2, FF)
        yT = carve(DC + 1, 2, SLOTS, B)
        combT = carve(2 * SLOTS, HB, TOK)
        temps_at = place["at"]
        ZR = 5
        xl = carve(TOK, 2, 2, D)
        xlT = carve(DC + 1, 3, 2, T2)
        uT = carve(DC + 1, 2, 2, T2)
        vt = carve(TOK, 3, 2, D)
        pt = carve(TOK, 2, 2, TOK)
        f2_at += [temps_at + F2N * r for r in range((place["at"] - temps_at) // F2N)]
        assert len(f2_at) == R2
        f2w = [arena[:, at:at + F2N].rearrange("p (j d) -> p j d", d=D) for at in f2_at]
        z = carve(TOK, ZR, 2, D)
        tk = carve(TOK, 2, 2, D)
        tkT = carve(DC, 2, 2, T2)
        e1 = carve(SLOTS, 3, 2, TOK)
        e2 = carve(TOK, 2, 2, SLOTS)
        dT = carve(TOK, 2, 2, SLOTS)
        region(f2_at[-1] + F2N, KEEP + SHARED)
        ybuf = carve(2 * SLOTS, HB, D)
        g1 = carve(128, 1, FF)
        g1T = carve(128, 1, FT, 128)
        y2 = carve(128, 2, D)
        b2 = carve(128, 2, D)

        psum = ctx.enter_context(nc.psum_tensor("psum", [128, 8 * 512], f32))
        bank = lambda n: psum[:, 512 * n:512 * n + 512]

        acc = psum[:, 0:KC * HT * 128]
        tap_w = psum[:, 5 * 512:5 * 512 + HT * KK].rearrange("p (w q) -> p w q", q=KK)
        off_ps = conv_ps = bank(7)
        tok_ps = bank(3)[0:PT * PT, 0:2 * D].rearrange("p (b d) -> p b d", d=D)
        l2_ps = bank(0)[0:TOK, 256:256 + 2 * SLOTS].rearrange("p (b s) -> p b s", s=SLOTS)
        tr_ps = bank(1)[0:DC, 0:2 * T2].rearrange("p (j t) -> p j t", t=T2)
        u_ps = bank(2)[0:DC + 1, 0:2 * T2].rearrange("p (j t) -> p j t", t=T2)
        v_ps = bank(4)[0:TOK, 0:2 * D].rearrange("p (b d) -> p b d", d=D)
        dT_ps = bank(7)[0:TOK, 0:2 * SLOTS].rearrange("p (b s) -> p b s", s=SLOTS)
        s_ps = bank(5)[0:TOK, 0:T2].rearrange("p (b t) -> p b t", t=TOK)
        y_ps = bank(5)[0:DC, 256:512].rearrange("p (b j s) -> p b j s", b=2, j=2)
        o_ps = bank(6)[0:TOK, 0:2 * D].rearrange("p (b d) -> p b d", d=D)
        l1_ps = bank(0)[0:SLOTS, 0:T2].rearrange("p (b t) -> p b t", t=TOK)
        cT_ps = bank(7)[0:SLOTS, 256:256 + T2].rearrange("p (b t) -> p b t", t=TOK)
        h1_ps = [psum[:, 1024 * q:1024 * q + 1024].rearrange("p (a n) -> p a n", n=512)[:, :, 0:FF // 2] for q in range(2)]
        h1T_ps = psum[:, 2048:2048 + FT * 128]
        y2_ps = bank(6)[:, 0:D]
        fin_ps = [(bank(6)[0:TOK, 0:D], bank(0)[0:TOK, 0:D]), (bank(7)[0:TOK, 0:D], bank(1)[0:TOK, 0:D])]

        def sem(name):
            return ctx.enter_context(nc.semaphore(name))

        ld_x, ld_first = [sem(f"ld_x{ck}") for ck in range(HT)], [sem(f"ld_first{k}") for k in range(KC)]
        ld_w, ld_qk, ld_cols, ld_const = sem("ld_w"), sem("ld_qk"), [sem("ld_cols2"), sem("ld_cols1")], sem("ld_const")
        ld_txt, ld_slots = sem("ld_txt"), sem("ld_slots")
        ld_f1, ld_f2 = [sem(f"ld_f1_{i}") for i in range(R1)], [sem(f"ld_f2_{i}") for i in range(R2)]
        ld_b2 = [sem(f"ld_b2_{i}") for i in range(2)]
        off_done, off_taken, off_masked, off_checked = sem("off_done"), sem("off_taken"), sem("off_masked"), sem("off_checked")
        hats, prod_v_done = sem("hats"), sem("prod_v_done")
        prod_v_used, outl_used = sem("prod_v_used"), sem("outl_used")
        samp_done, conv_done, conv_taken = sem("samp_done"), sem("conv_done"), sem("conv_taken")
        bn_var, bn_rstd, bn_affine, patches = sem("bn_var"), sem("bn_rstd"), sem("bn_affine"), sem("patches")
        grid_in_sb, exact_step = ([sem(f"{n}_{ck}") for ck in range(HT)] for n in ("grid_in_sb", "exact_step"))
        off_stored, far_found, far_cleared, ld_base = [sem(f"off_stored{ck}") for ck in range(HT)], sem("far_found"), [sem(f"far_cleared{ck}") for ck in range(HT)], sem("ld_base")
        far_off_in, far_quad_in, far_out, outl_in = ([sem(f"{n}_{ck}") for ck in range(HT)] for n in ("far_off_in", "far_quad_in", "far_out", "outl_in"))
        gathered = [sem(f"gathered_{n}") for n in range(HT * HT)]
        slot_sqd, slot_nd, slot_td, slot_td2 = sem("slot_sqd"), sem("slot_nd"), sem("slot_td"), sem("slot_td2")
        consts_made, gram_done, gram_taken = sem("consts_made"), sem("gram_done"), sem("gram_taken")
        v_step, a_step, g_step = sem("v_step"), sem("a_step"), sem("g_step")
        names = ("tokT_done h_patches var1_done rstd1_done xl_done xlT_done xlT_taken u_done u_taken "
                 "vproj_done v_taken score_done probs_done attn_done h_done var2_done a2_done z_done ssq_done f2_done "
                 "tok_done tkT_done tkT_taken logits_done max_done exp1_done exp2_done disp_done "
                 "cT_done dT_taken cT_taken y_done y_taken")
        s = {n: sem(n) for n in names.split()}
        fc1_done, gelu_done, h1T_done, h1T_taken, fc2_done, y2_done = (sem(n) for n in ("fc1_done", "gelu_done", "h1T_done", "h1T_taken", "fc2_done", "y2_done"))
        y_moved = [sem("y_moved0"), sem("y_moved1")]
        fin_done, out_done, stored = sem("fin_done"), sem("out_done"), sem("stored")
        rsum2_done, out_scaled, out_added = sem("rsum2_done"), sem("out_scaled"), sem("out_added")

        def hat_count(ck, i, j):
            return ck * 2 * WIN + (j + 2 if i == 0 else WIN + 1 + i)

        def window(ck, i, j):
            return xh[:, :, :, PATCH * ck + i:PATCH * ck + i + PATCH, j:j + PATCH]

        def bcast_c(w):
            return pixels(w.unsqueeze(1).broadcast_to([128, C, HT, KK]))

        def pixels(v):
            return v.rearrange("p c w (r q) -> p c w r q", q=PATCH)

        def half_of(n):
            return slice(SLOTS * (n // HB), SLOTS * (n // HB) + SLOTS)

        def steps(g_of_stage):
            last = max(lag for _, lag in g_of_stage)
            for t in range(NG + last):
                for stage, lag in g_of_stage:
                    if 0 <= t - lag < NG:
                        yield stage, t - lag

        block = ctx.enter_context(nc.Block())

        @block.sync
        def _(sp):
            for k in range(KC):
                sp.dma_start(xc[:, 0, k], x_cols[0, :, k]).then_inc(ld_first[k], 16)
                sp.dma_start(woff[:, k, :], w_off[:, k, :]).then_inc(ld_first[k], 16)
            sp.dma_start(boff, b_off.partition_broadcast(128)).then_inc(ld_w, 16)
            sp.dma_start(ident, ident_in).then_inc(ld_w, 16)
            for dst, src in ((wqT, wq_t), (wkT, wk_t), (bq, b_q)):
                sp.dma_start(dst, src).then_inc(ld_qk, 16)
            sp.dma_start(xc[:, 1], x_cols[1]).then_inc(ld_cols[1], 16)
            def load_rows(ck):
                rows = slice(PATCH * ck + (2 * RAD if ck else 0), PATCH * (ck + 1) + 2 * RAD)
                sp.dma_start(xh.rearrange("p c w r q -> p (c w) r q")[:, :, rows, :],
                             x_halo.rearrange("p c w r q -> p (c w) r q")[:, :, rows, :]).then_inc(ld_x[ck], 16)

            def store_offsets(ck):
                sp.wait_ge(off_taken, HT * (ck + 1))
                sp.dma_start(off_d[ck], off[:, ck].rearrange("p w q a -> p (w q a)")).then_inc(off_stored[ck], 16)

            def clear_samples(ck):
                sp.dma_start(far_d[ck].rearrange("p (c n) -> p c n", c=C), zeros.unsqueeze(1).broadcast_to([128, C, NPOS])).then_inc(far_cleared[ck], 16)

            def read_samples(ck):
                sp.wait_ge(far_out[ck], 16 * FAR)
                if ck:
                    sp.wait_ge(outl_used, ck)
                sp.dma_start(outl.rearrange("p w q c -> p (w q c)"), far_d[ck]).then_inc(outl_in[ck], 16)

            load_rows(0)
            sp.dma_start(base, base_in).then_inc(ld_base, 16)
            sp.wait_ge(consts_made, 1)
            clear_samples(0)
            store_offsets(0)
            sp.wait_ge(off_done, HT)
            sp.dma_start(xc[:, 0], x_cols[2]).then_inc(ld_cols[0], 16)
            load_rows(1)
            store_offsets(1)
            read_samples(0)
            for dst, src in ((wcv, w_conv), (decay, decay_in), (wv, w_v), (bv, b_v.partition_broadcast(TOK)),
                             (normw, norm_w.partition_broadcast(TOK)), (gam, bn_g), (bet, bn_b)):
                sp.dma_start(dst, src).then_inc(ld_const, 16)
            sp.dma_start(slotv, slots).then_inc(ld_slots, 16)
            sp.dma_start(slotsc, scale).then_inc(ld_slots, 16)
            clear_samples(1)
            clear_samples(2)
            load_rows(2)
            store_offsets(2)
            read_samples(1)
            read_samples(2)
            sp.wait_ge(samp_done, PIECES * HT)
            sp.dma_start(h[PT * PT:TOK, :, :], txt.rearrange("b t d -> t b d")).then_inc(ld_txt, 16)

            def load_first(n):
                r = n % R1
                if n >= R1:
                    sp.wait_ge(fc1_done, (n - R1) // MS + 1)
                sp.dma_start(f1w[0:DC, r], fc1[n]).then_inc(ld_f1[r], 16)
                sp.dma_start(f1w[DC:DC + 1, r, 0, :], fc1_b[n:n + 1]).then_inc(ld_f1[r], 16)

            def load_second(n):
                r = n % R2
                if n == f2_main:
                    sp.wait_ge(s["tokT_done"], NG)
                if n == f2_main + f2_patch:
                    sp.wait_ge(s["attn_done"], NG)
                if n >= R2:
                    sp.wait_ge(fc2_done, (n - R2) // MS + 1)
                sp.dma_start(f2w[r], fc2[n]).then_inc(ld_f2[r], 16)

            sp.wait_ge(conv_taken, 2 * HT)
            for n in range(R1):
                load_first(n)
            for n in range(R2):
                load_second(n)
            for q in range(R1 // MS, MG + 1):
                for n in range(MS * q, MS * q + MS):
                    if n < SLOTS:
                        load_first(n)
                for n in range(MS * q - MS, MS * q):
                    if n >= R2:
                        load_second(n)
            for n in range(0, B, STORE):
                sp.wait_ge(out_done, (n + STORE) // 2)
                sp.wait_ge(out_added, (n + STORE) // 2)
                sp.dma_start(out[n:n + STORE, 0:TOK - 1].rearrange("b t d -> t b d"), h[0:TOK - 1, n:n + STORE, :]).then_inc(stored, 16)
            sp.dma_start(out[:, TOK - 1:TOK].rearrange("b t d -> t b d"), h[TOK - 1:TOK]).then_inc(stored, 16)
            sp.wait_ge(stored, 16 * (B // STORE + 1))

        @block.tensor
        def _(pe):
            def offsets(ck, wt, dst):
                pe.wait_ge(ld_cols[ck % 2], 16)
                for k in range(KC):
                    last = nc.tensor.matmul(dst, xc[:, ck % 2, k, wt, :], woff[:, k, :], start=(k == 0), stop=(k == KC - 1))
                last.then_inc(off_done, 1)

            def transposed_sum(piece, ck=0, first=False):
                for n in range(KC * HT):
                    k, wt = n // HT, n % HT
                    c, half = k // 2, k % 2
                    if first and ck and n in SAMP_CUT:
                        pe.wait_ge(samp_done, PIECES * (ck - 1) + SAMP_CUT.index(n) + 1)
                    last = nc.tensor.matmul(acc[:, 128 * n:128 * n + 128], piece(c, wt, slice(128 * half, 128 * half + 128)), ident, is_transpose=True,
                                            start=(first and n % 4 == 0), stop=True, skip_group_check=True)
                return last

            def convolve(ck):
                if ck == 0:
                    pe.wait_ge(ld_const, 16 * CONSTS)
                pe.wait_ge(off_taken, HT * HT)
                for oc in range(2):
                    if 2 * ck + oc:
                        pe.wait_ge(conv_taken, 2 * ck + oc)
                    for k in range(KC):
                        if oc == 0:
                            pe.wait_ge(samp_done, PIECES * ck + min(PIECES, (HT * k + HT - 1) // 4 + 1))
                        last = nc.tensor.matmul(conv_ps[0:DC, 0:HT * 128], wcv[:, k, DC * oc:DC * oc + DC],
                                                samp[:, k].rearrange("p w n -> p (w n)"), start=(k == 0), stop=(k == KC - 1))
                    last.then_inc(conv_done, 1)

            for k in range(KC):
                pe.wait_ge(ld_first[k], 32)
                for wt in range(HT):
                    last = nc.tensor.matmul(bank(wt), xc[:, 0, k, wt, :], woff[:, k, :], start=(k == 0), stop=(k == KC - 1))
                    if k == KC - 1:
                        last.then_inc(off_done, 1)
            pe.wait_ge(ld_qk, 48)
            for i in range(2):
                for c in range(2):
                    nc.tensor.matmul(bank(3 + i)[0:DC, 0:D + 1], wqT[:, c, DC * i:DC * i + DC], wkT[:, c, :], start=(c == 0), stop=(c == 1))
            for j in range(2):
                for c in range(2):
                    last = nc.tensor.matmul(bank(5)[0:DC + j, j:j + 1], wkT[:, c, DC * j:DC * j + DC + j], bq[:, c:c + 1], start=(c == 0), stop=(c == 1))
            last.then_inc(gram_done, 1)
            pe.wait_ge(gram_taken, 1)
            pe.wait_ge(ld_w, 32)
            for wt in range(HT):
                offsets(1, wt, (bank(3), bank(4), off_ps)[wt])
            pe.wait_ge(off_taken, 2 * HT - 1)
            for ck in range(HT):
                for t in range(TAPS):
                    n = TAPS * ck + t
                    pe.wait_ge(prod_v_done, n + 1)
                    transposed_sum(lambda c, wt, q: prod_v[:, n % PRODS, c, wt, q], ck, t == 0).then_inc(prod_v_used, 1)
                    if ck and t == 3:
                        convolve(ck - 1)
                    if ck == 0 and t in OFF_AT:
                        wt = OFF_AT.index(t)
                        pe.wait_ge(off_taken, 2 * HT + wt)
                        offsets(2, wt, off_ps)
                pe.wait_ge(outl_in[ck], 16)
                pe.wait_ge(off_checked, ck + 1)
                transposed_sum(lambda c, wt, q: outl[:, wt, q, c]).then_inc(outl_used, 1)
            convolve(HT - 1)

            pe.wait_ge(slot_nd, 1)
            pe.wait_ge(conv_taken, 2 * HT)
            for j in range(2):
                last = nc.tensor.transpose(conv_ps[0:DC, SLOTS * j:SLOTS * j + SLOTS], slotn[:, DC * j:DC * j + DC], ident[0:SLOTS, 0:SLOTS])
            last.then_inc(slot_td, 1)
            pe.wait_ge(slot_td2, 1)
            pe.wait_ge(patches, 1)
            pe.wait_ge(consts_made, 2)

            def back_to_tokens(g):
                if g:
                    pe.wait_ge(s["h_patches"], g)
                for b in range(2):
                    for j in range(2):
                        last = nc.tensor.transpose(tok_ps[:, b, DC * j:DC * j + DC], patch_tok[:, j, 2 * g + b, :], ident[0:DC, 0:DC])
                last.then_inc(s["tokT_done"], 1)

            def normed_transpose(g):
                pe.wait_ge(s["xl_done"], g + 1)
                if g >= 1:
                    pe.wait_ge(s["xlT_taken"], g)
                if g >= 5:
                    pe.wait_ge(s["tkT_taken"], g - 4)
                for j in range(2):
                    for b in range(2):
                        last = nc.tensor.transpose(tr_ps[:, j, TOK * b:TOK * b + TOK], xl[:, g % 2, b, DC * j:DC * j + DC], ident[0:TOK, 0:TOK])
                last.then_inc(s["xlT_done"], 1)

            def project(g):
                pe.wait_ge(s["xlT_taken"], g + 1)
                if g:
                    pe.wait_ge(s["u_taken"], g)
                for j in range(2):
                    for i in range(2):
                        last = nc.tensor.matmul(u_ps[0:DC + j, j, :], gram[:, i, DC * j:DC * j + DC + j], xlT[0:DC, g % 3, i, :], start=(i == 0), stop=(i == 1))
                last.then_inc(s["u_done"], 1)
                if g:
                    pe.wait_ge(s["v_taken"], g)
                for b in range(2):
                    for j in range(2):
                        last = nc.tensor.matmul(v_ps[:, b, :], xlT[0:DC, g % 3, j, TOK * b:TOK * b + TOK], wv[:, j, :], start=(j == 0), stop=(j == 1))
                last.then_inc(s["vproj_done"], 1)

            def scores(g):
                pe.wait_ge(s["u_taken"], g + 1)
                if g:
                    pe.wait_ge(s["probs_done"], g)
                if g >= 6:
                    pe.wait_ge(s["y_taken"], g - 5)
                for b in range(2):
                    for j in range(2):
                        last = nc.tensor.matmul(s_ps[:, b, :], xlT[0:DC + j, g % 3, j, TOK * b:TOK * b + TOK], uT[0:DC + j, g % 2, j, TOK * b:TOK * b + TOK], start=(j == 0), stop=(j == 1))
                last.then_inc(s["score_done"], 1)

            def attend(g):
                pe.wait_ge(s["probs_done"], g + 1)
                pe.wait_ge(s["v_taken"], g + 1)
                if g:
                    pe.wait_ge(s["h_done"], g)
                for b in range(2):
                    last = nc.tensor.matmul(o_ps[:, b, :], pt[:, g % 2, b, :], vt[:, g % 3, b, :], start=True, stop=True)
                last.then_inc(s["attn_done"], 1)

            def directions_transpose(g):
                pe.wait_ge(s["tok_done"], g + 1)
                if g >= 1:
                    pe.wait_ge(s["tkT_taken"], g)
                pe.wait_ge(s["xlT_taken"], min(g + 5, NG))
                for j in range(2):
                    for b in range(2):
                        last = nc.tensor.transpose(tr_ps[:, j, TOK * b:TOK * b + TOK], tk[:, g % 2, b, DC * j:DC * j + DC], ident[0:TOK, 0:TOK])
                last.then_inc(s["tkT_done"], 1)

            def logits(g):
                pe.wait_ge(s["tkT_taken"], g + 1)
                if g:
                    pe.wait_ge(s["exp2_done"], g)
                for j in range(2):
                    nc.tensor.matmul(l1_ps.rearrange("p b t -> p (b t)"), slotT[:, j, :], tkT[:, g % 2, j, :], start=(j == 0), stop=(j == 1))
                for b in range(2):
                    for j in range(2):
                        last = nc.tensor.matmul(l2_ps[:, b, :], tkT[:, g % 2, j, TOK * b:TOK * b + TOK], slotT[:, j, :], start=(j == 0), stop=(j == 1))
                last.then_inc(s["logits_done"], 1)

            def weights_transpose(g):
                pe.wait_ge(s["disp_done"], g + 1)
                pe.wait_ge(s["exp2_done"], g + 1)
                if g:
                    pe.wait_ge(s["cT_taken"], g)
                for b in range(2):
                    nc.tensor.transpose(dT_ps[:, b, :], e1[:, g % 3, b, :], ident[0:SLOTS, 0:SLOTS])
                for b in range(2):
                    last = nc.tensor.transpose(cT_ps[:, b, :], e2[:, g % 2, b, :], ident[0:TOK, 0:TOK])
                last.then_inc(s["cT_done"], 1)

            def dispatch(g):
                pe.wait_ge(s["dT_taken"], g + 1)
                pe.wait_ge(s["z_done"], g + 1)
                if g:
                    pe.wait_ge(s["y_taken"], g)
                pe.wait_ge(s["probs_done"], min(g + 6, NG))
                for b in range(2):
                    for j in range(2):
                        last = nc.tensor.matmul(y_ps[:, b, j, :], z[:, g % ZR, b, DC * j:DC * j + DC], dT[:, g % 2, b, :], start=True, stop=True)
                last.then_inc(s["y_done"], 1)

            for stage, g in steps([(dispatch, 10), (logits, 8), (weights_transpose, 9), (directions_transpose, 7), (attend, 5),
                                   (scores, 4), (project, 3), (normed_transpose, 2), (back_to_tokens, 0)]):
                stage(g)

            pe.wait_ge(s["y_taken"], NG)
            pe.wait_ge(s["cT_taken"], NG)

            def up(q):
                for n in range(MS * q, MS * q + MS):
                    pe.wait_ge(ld_f1[n % R1], 32 * (n // R1 + 1))
                if q >= 2:
                    pe.wait_ge(gelu_done, q - 1)
                for part in range(2):
                    for j in range(2):
                        rows = DC + 1 - j
                        for i in range(MS):
                            last = nc.tensor.matmul(h1_ps[q % 2][32 * i:32 * i + 32, part, :], yT[0:rows, j, MS * q + i, :],
                                                    f1w[0:rows, (MS * q + i) % R1, j, FF // 2 * part:FF // 2 * part + FF // 2],
                                                    start=(j == 0), stop=(j == 1), tile_position=(0, 32 * i))
                last.then_inc(fc1_done, 1)

            def turn(q):
                pe.wait_ge(gelu_done, q + 1)
                if q:
                    pe.wait_ge(h1T_taken, q)
                for j in range(FT):
                    last = nc.tensor.transpose(h1T_ps[:, 128 * j:128 * j + 128], g1[:, 0, 128 * j:128 * j + 128], ident)
                last.then_inc(h1T_done, 1)

            def down(q):
                pe.wait_ge(h1T_taken, q + 1)
                for n in range(MS * q, MS * q + MS):
                    pe.wait_ge(ld_f2[n % R2], 16 * (n // R2 + 1))
                if q:
                    pe.wait_ge(y2_done, q)
                for j in range(FT):
                    for i in range(MS):
                        last = nc.tensor.matmul(y2_ps[32 * i:32 * i + 32, :], g1T[:, 0, j, 32 * i:32 * i + 32], f2w[(MS * q + i) % R2][:, j, :],
                                                start=(j == 0), stop=(j == FT - 1), tile_position=(0, 32 * i))
                last.then_inc(fc2_done, 1)

            for q in range(MG + 1):
                if q:
                    turn(q - 1)
                if q < MG:
                    up(q)
                if q:
                    down(q - 1)

            for _ in range(2 * FT * MS):
                nc.tensor.transpose(h1T_ps[:, 0:128], g1[:, 0, 0:128], ident)
            pe.wait_ge(y2_done, MG)
            pe.wait_ge(y_moved[0], 16 * MS * MG // 2)
            pe.wait_ge(y_moved[1], 16 * MS * MG // 2)
            for g in range(NG):
                if g >= 2:
                    pe.wait_ge(out_done, g - 1)
                    pe.wait_ge(out_scaled, g - 1)
                for b in range(2):
                    last = nc.tensor.matmul(fin_ps[g % 2][b], combT[half_of(2 * g), (2 * g + b) % HB, :], ybuf[half_of(2 * g), (2 * g + b) % HB, :], start=True, stop=True)
                last.then_inc(fin_done, 1)

        @block.vector
        def _(ve):
            n_step = [0]

            def then(ins):
                n_step[0] += 1
                ins.then_inc(v_step, 1)
                ve.wait_ge(v_step, n_step[0])

            def take_offsets(ck, wt, src):
                ve.wait_ge(off_done, HT * ck + wt + 1)
                nc.vector.tensor_tensor(off[:, ck, wt].rearrange("p q a -> p a q"), src.rearrange("p (a q) -> p a q", a=2),
                                        boff.rearrange("p (a q) -> p a q", a=2), ALU.add).then_inc(off_taken, 1)

            def mask_offsets(ck):
                ve.wait_ge(off_taken, HT * (ck + 1))
                dy, dx = off[:, ck, :, :, 0], off[:, ck, :, :, 1]
                if ck:
                    ve.wait_ge(far_found, ck)
                if ck >= 2:
                    ve.wait_ge(hats, 2 * WIN * (ck - 1))
                then(nc.vector.scalar_tensor_tensor(off_abs, dy, -1.0, dy, ALU.mult, ALU.max))
                then(nc.vector.scalar_tensor_tensor(off_abs, dx, -1.0, off_abs, ALU.mult, ALU.max))
                then(nc.vector.tensor_tensor(off_abs, off_abs, dx, ALU.max))
                flat = off_abs.rearrange("p w q -> p (w q)")
                then(nc.vector.max(far_val[:, ck], flat))
                nc.vector.max_index(far_idx[:, ck].bitcast(u32), far_val[:, ck], flat).then_inc(far_found, 1)
                then(nc.vector.scalar_tensor_tensor(off_in[:, ck % 2], off_abs, float(RAD), off_abs, ALU.is_gt, ALU.mult))
                nc.vector.scalar_tensor_tensor(off_in[:, ck % 2], off_in[:, ck % 2], 4.0, dy, ALU.mult, ALU.add).then_inc(off_masked, 1)

            ve.wait_ge(ld_w, 32)
            for wt in range(HT):
                take_offsets(0, wt, bank(wt))
            mask_offsets(0)
            for ck in range(HT):
                ve.wait_ge(ld_x[ck], 16)
                for t in range(TAPS):
                    i, j = t // WIN, t % WIN
                    n = TAPS * ck + t
                    ve.wait_ge(hats, hat_count(ck, i, j))
                    if n:
                        ve.wait_ge(prod_v_done, n)
                    then(nc.vector.tensor_tensor(tap_w, haty[:, ck % 2, i], hatx[:, ck % 2, j], ALU.mult))
                    if n >= PRODS:
                        ve.wait_ge(prod_v_used, n - PRODS + 1)
                    nc.vector.tensor_tensor(pixels(prod_v[:, n % PRODS]), window(ck, i, j), bcast_c(tap_w), ALU.mult).then_inc(prod_v_done, 1)
                    if ck == 0 and t == 1:
                        for wt in range(HT):
                            take_offsets(1, wt, (bank(3), bank(4), off_ps)[wt])
                    if ck + 1 < HT and t == MASK_AT[ck]:
                        mask_offsets(ck + 1)
                    if ck == 0 and t in TAKE_AT:
                        take_offsets(2, TAKE_AT.index(t), off_ps)

            for oc in range(2):
                for ck in range(HT):
                    ve.wait_ge(conv_taken, 2 * ck + oc + 1)
                    last = nc.vector.bn_stats(bn6[:, oc, ck, :], convs[:, oc, ck, :])
                then(last)
                nc.vector.bn_aggr(bn2[:, oc, :], bn6[:, oc].rearrange("p a b -> p (a b)")).then_inc(bn_var, 1)
            for oc in range(2):
                ve.wait_ge(bn_rstd, oc + 1)
                then(nc.vector.tensor_tensor(bn_s[:, oc:oc + 1], bn_r[:, oc:oc + 1], gam[:, oc:oc + 1], ALU.mult))
                then(nc.vector.tensor_tensor(bn_t[:, oc:oc + 1], bn2[:, oc, 0:1], bn_s[:, oc:oc + 1], ALU.mult))
                nc.vector.tensor_tensor(bn_t[:, oc:oc + 1], bet[:, oc:oc + 1], bn_t[:, oc:oc + 1], ALU.subtract).then_inc(bn_affine, 1)

            def variances(g, mv):
                for b in range(2):
                    last = nc.vector.bn_stats(st6[:, b, 0, :], h[:, 2 * g + b, :])
                then(last)
                for b in range(2):
                    last = nc.vector.bn_aggr(mv[:, b, :], st6[:, b, 0, :])
                return last

            def first_stats(g):
                ve.wait_ge(s["h_patches"], g + 1)
                if g == 0:
                    ve.wait_ge(ld_txt, 16)
                if g >= 4:
                    ve.wait_ge(s["xl_done"], g - 3)
                variances(g, mv1[:, g % 4]).then_inc(s["var1_done"], 1)

            def first_norm(g):
                ve.wait_ge(s["rstd1_done"], g + 1)
                if g >= 2:
                    ve.wait_ge(s["xlT_done"], g - 1)
                for b in range(2):
                    last = nc.vector.tensor_scalar(xl[:, g % 2, b, :], h[:, 2 * g + b, :], mv1[:, g % 4, b, 0:1], r1[:, g % 4, b:b + 1], ALU.subtract, ALU.mult)
                last.then_inc(s["xl_done"], 1)

            def values(g):
                ve.wait_ge(s["vproj_done"], g + 1)
                if g >= 3:
                    ve.wait_ge(s["attn_done"], g - 2)
                nc.vector.tensor_tensor(vt[:, g % 3], v_ps, bv.unsqueeze(1).broadcast_to([TOK, 2, D]), ALU.add).then_inc(s["v_taken"], 1)

            def decayed(g):
                ve.wait_ge(s["score_done"], g + 1)
                if g >= 2:
                    ve.wait_ge(s["attn_done"], g - 1)
                nc.vector.tensor_tensor(pt[:, g % 2], s_ps, decay.unsqueeze(1).broadcast_to([TOK, 2, TOK]), ALU.mult).then_inc(s["probs_done"], 1)

            def residual(g):
                ve.wait_ge(s["attn_done"], g + 1)
                ve.wait_ge(s["xl_done"], g + 1)
                last = nc.vector.tensor_tensor(h[:, 2 * g:2 * g + 2, :], o_ps, h[:, 2 * g:2 * g + 2, :], ALU.add)
                last.then_inc(s["h_done"], 1)
                ve.wait_ge(s["h_done"], g + 1)
                variances(g, mv2[:, g]).then_inc(s["var2_done"], 1)

            def weighted(g):
                ve.wait_ge(s["var2_done"], g + 1)
                if g >= ZR:
                    ve.wait_ge(s["y_done"], g - ZR + 1)
                for b in range(2):
                    last = nc.vector.scalar_tensor_tensor(z[:, g % ZR, b, :], h[:, 2 * g + b, :], mv2[:, g, b, 0:1], normw, ALU.subtract, ALU.mult)
                last.then_inc(s["z_done"], 1)

            def unit(g):
                ve.wait_ge(s["f2_done"], g + 1)
                ve.wait_ge(s["z_done"], g + 1)
                if g >= 2:
                    ve.wait_ge(s["tkT_done"], g - 1)
                for b in range(2):
                    last = nc.vector.tensor_scalar(tk[:, g % 2, b, :], z[:, g % ZR, b, :], f2[:, g % 4, b:b + 1], None, ALU.mult)
                last.then_inc(s["tok_done"], 1)

            def maxima(g):
                ve.wait_ge(s["logits_done"], g + 1)
                if g >= 4:
                    ve.wait_ge(s["exp1_done"], g - 3)
                nc.vector.tensor_reduce(nmax1[:, g % 4, :], l1_ps, AX.X, ALU.max, negate=True)
                if g >= 4:
                    ve.wait_ge(s["exp2_done"], g - 3)
                nc.vector.tensor_reduce(nmax2[:, g % 4, :], l2_ps, AX.X, ALU.max, negate=True).then_inc(s["max_done"], 1)

            def normed_dispatch(g):
                ve.wait_ge(s["exp1_done"], g + 1)
                then(nc.vector.reciprocal(rsum1[:, g % 4, :], sum1[:, g % 4, :]))
                for b in range(2):
                    last = nc.vector.tensor_scalar(e1[:, g % 3, b, :], e1[:, g % 3, b, :], rsum1[:, g % 4, b:b + 1], None, ALU.mult)
                last.then_inc(s["disp_done"], 1)

            for stage, g in steps([(unit, 7), (weighted, 6), (first_stats, 1), (maxima, 8), (residual, 5), (decayed, 4),
                                   (values, 3), (normed_dispatch, 8), (first_norm, 1)]):
                stage(g)

            ve.wait_ge(s["exp2_done"], NG)
            nc.vector.reciprocal(rsum2, sum2).then_inc(rsum2_done, 1)
            ve.wait_ge(rsum2_done, 1)
            for q in range(MG):
                ve.wait_ge(h1T_done, q + 1)
                if q:
                    ve.wait_ge(fc2_done, q)
                else:
                    ve.wait_ge(s["y_done"], NG)
                nc.vector.tensor_copy(g1T[:, 0].rearrange("p a b -> p (a b)"), h1T_ps).then_inc(h1T_taken, 1)
                ve.wait_ge(fc2_done, q + 1)
                ve.wait_ge(ld_b2[q % 2], 16 * (q // 2 + 1))
                if q >= 2:
                    ve.wait_ge(y_moved[q % 2], 16 * MS * (q // 2))
                nc.vector.tensor_tensor(y2[:, q % 2, :], y2_ps, b2[:, q % 2, :], ALU.add).then_inc(y2_done, 1)
            for g in range(NG):
                ve.wait_ge(fin_done, g + 1)
                n = 2 * g
                nc.vector.scalar_tensor_tensor(h[:, n, :], fin_ps[g % 2][0], rsum2[:, n:n + 1], h[:, n, :], ALU.mult, ALU.add).then_inc(out_done, 1)

        @block.scalar
        def _(ac):
            n_step = [0]

            def then(ins):
                n_step[0] += 1
                ins.then_inc(a_step, 1)
                ac.wait_ge(a_step, n_step[0])

            def hat(dst, src, center):
                then(nc.scalar.activation(dst, src, ACT.Abs, bias=-float(center)))
                nc.scalar.activation(dst, dst, ACT.Relu, bias=1.0, scale=-1.0).then_inc(hats, 1)

            def all_hats(ck):
                ac.wait_ge(off_masked, ck + 1)
                if ck >= 2:
                    ac.wait_ge(prod_v_done, TAPS * (ck - 1))
                hat(haty[:, ck % 2, 0], off_in[:, ck % 2], -RAD)
                for j in range(WIN):
                    hat(hatx[:, ck % 2, j], off[:, ck, :, :, 1], j - RAD)
                for i in range(1, WIN):
                    hat(haty[:, ck % 2, i], off_in[:, ck % 2], i - RAD)

            ac.wait_ge(gram_done, 1)
            for i in range(2):
                nc.scalar.activation(gram[:, i, :], bank(3 + i)[0:DC, 0:D + 1], ACT.Copy)
            nc.scalar.activation(gram0[0:DC, 0:1], bank(5)[0:DC, 0:1], ACT.Copy)
            nc.scalar.activation(gram0[:, 1:2], bank(5)[0:DC + 1, 1:2], ACT.Copy).then_inc(gram_taken, 1)
            all_hats(0)
            all_hats(1)
            for ck in range(HT):
                ac.wait_ge(prod_v_used, TAPS * (ck + 1))
                ac.wait_ge(outl_used, ck + 1)
                if ck:
                    ac.wait_ge(conv_done, 2 * ck)
                flat_samp = samp.rearrange("p k w n -> p (k w n)")
                for lo, hi in zip(SAMP_CUT[:-1], SAMP_CUT[1:]):
                    nc.scalar.activation(flat_samp[:, 128 * lo:128 * hi], acc[:, 128 * lo:128 * hi], ACT.Copy).then_inc(samp_done, 1)
                for oc in range(2):
                    ac.wait_ge(conv_done, 2 * ck + oc + 1)
                    nc.scalar.activation(convs[:, oc, ck, :], conv_ps[0:DC, 0:HT * 128], ACT.Copy).then_inc(conv_taken, 1)
                if ck == 0:
                    all_hats(2)
                    ac.wait_ge(ld_slots, 32)
                    nc.scalar.activation(slotn, slotv, ACT.Square, accum_out=slot_sq).then_inc(slot_sqd, 1)

            ac.wait_ge(slot_td, 1)
            nc.scalar.activation(slotT.rearrange("p j s -> p (j s)"), conv_ps[0:DC, 0:2 * SLOTS], ACT.Copy).then_inc(slot_td2, 1)
            for oc in range(2):
                ac.wait_ge(bn_affine, oc + 1)
                for hot in range(HT):
                    for hop in range(2):
                        src = convs[:, oc, hot, :].rearrange("p (wt hp wp b) -> p hp wt wp b", wt=HT, hp=2, wp=2)[:, hop]
                        dst = patch_tok[:, oc].rearrange("p b (hp ht wp wt) -> p hp ht wt wp b", hp=2, ht=HT, wp=2)[:, hop, hot]
                        last = nc.scalar.activation(dst, src, ACT.Gelu, bias=bn_t[:, oc:oc + 1], scale=bn_s[:, oc:oc + 1])
            last.then_inc(patches, 1)

            def take_patches(g):
                ac.wait_ge(s["tokT_done"], g + 1)
                nc.scalar.activation(h[0:PT * PT, 2 * g:2 * g + 2, :], tok_ps, ACT.Copy).then_inc(s["h_patches"], 1)

            def take_normed(g):
                ac.wait_ge(s["xlT_done"], g + 1)
                if g >= 3:
                    ac.wait_ge(s["score_done"], g - 2)
                nc.scalar.activation(xlT[0:DC, g % 3], tr_ps, ACT.Copy).then_inc(s["xlT_taken"], 1)

            def take_queries(g):
                ac.wait_ge(s["u_done"], g + 1)
                if g >= 2:
                    ac.wait_ge(s["score_done"], g - 1)
                for j in range(2):
                    last = nc.scalar.activation(uT[0:DC + j, g % 2, j, :], u_ps[0:DC + j, j, :], ACT.Identity, bias=gram0[0:DC + j, j:j + 1])
                last.then_inc(s["u_taken"], 1)

            def squares(g):
                ac.wait_ge(s["z_done"], g + 1)
                if g >= 4:
                    ac.wait_ge(s["f2_done"], g - 3)
                if g >= 2:
                    ac.wait_ge(s["tkT_done"], g - 1)
                for b in range(2):
                    last = nc.scalar.activation(tk[:, g % 2, b, :], z[:, g % ZR, b, :], ACT.Square, accum_out=ssq[:, g % 4, b:b + 1])
                last.then_inc(s["ssq_done"], 1)

            def take_directions(g):
                ac.wait_ge(s["tkT_done"], g + 1)
                if g >= 2:
                    ac.wait_ge(s["logits_done"], g - 1)
                nc.scalar.activation(tkT[:, g % 2], tr_ps, ACT.Copy).then_inc(s["tkT_taken"], 1)

            def exps(g):
                ac.wait_ge(s["max_done"], g + 1)
                if g >= 3:
                    ac.wait_ge(s["cT_done"], g - 2)
                for b in range(2):
                    last = nc.scalar.activation(e1[:, g % 3, b, :], l1_ps[:, b, :], ACT.Exp, bias=nmax1[:, g % 4, b:b + 1], accum_out=sum1[:, g % 4, b:b + 1])
                last.then_inc(s["exp1_done"], 1)
                if g >= 2:
                    ac.wait_ge(s["cT_done"], g - 1)
                for b in range(2):
                    last = nc.scalar.activation(e2[:, g % 2, b, :], l2_ps[:, b, :], ACT.Exp, bias=nmax2[:, g % 4, b:b + 1], accum_out=sum2[:, 2 * g + b:2 * g + b + 1])
                last.then_inc(s["exp2_done"], 1)

            def take_weights(g):
                ac.wait_ge(s["cT_done"], g + 1)
                if g >= 2:
                    ac.wait_ge(s["y_done"], g - 1)
                for b in range(2):
                    last = nc.scalar.activation(dT[:, g % 2, b, :], dT_ps[:, b, :], ACT.Copy, scale=a2[:, g, b:b + 1])
                last.then_inc(s["dT_taken"], 1)
                nc.scalar.activation(combT[half_of(2 * g), 2 * g % HB:2 * g % HB + 2, :], cT_ps, ACT.Copy).then_inc(s["cT_taken"], 1)

            def take_dispatched(g):
                ac.wait_ge(s["y_done"], g + 1)
                nc.scalar.activation(yT[0:DC, :, :, 2 * g:2 * g + 2].rearrange("p j s b -> p b j s"), y_ps, ACT.Copy).then_inc(s["y_taken"], 1)

            for stage, g in steps([(take_dispatched, 10), (take_weights, 9), (take_directions, 7), (squares, 6), (exps, 8),
                                   (take_queries, 3), (take_normed, 2), (take_patches, 0)]):
                stage(g)

            for q in range(MG + 1):
                if q < MG:
                    if q == 0:
                        ac.wait_ge(s["y_done"], NG)
                    if q < 2:
                        ac.dma_start(b2[:, q % 2, :], fc2_b[q]).then_inc(ld_b2[q % 2], 16)
                    ac.wait_ge(fc1_done, q + 1)
                    if q:
                        ac.wait_ge(h1T_done, q)
                    nc.scalar.activation(g1[:, 0].rearrange("p (a n) -> p a n", a=2), h1_ps[q % 2], ACT.Gelu).then_inc(gelu_done, 1)
                if q:
                    p = q - 1
                    ac.wait_ge(y2_done, p + 1)
                    for i in range(MS):
                        n = MS * p + i
                        ac.dma_start(ybuf[n:2 * SLOTS:SLOTS, :, :], y2[32 * i:32 * i + 32, p % 2, :]).then_inc(y_moved[p % 2], 16)
                    if p + 2 < MG:
                        ac.dma_start(b2[:, p % 2, :], fc2_b[p + 2]).then_inc(ld_b2[p % 2], 16)

            ac.wait_ge(rsum2_done, 1)
            for g in range(NG):
                ac.wait_ge(fin_done, g + 1)
                if g >= 4:
                    ac.wait_ge(out_added, g - 3)
                n = 2 * g + 1
                nc.scalar.activation(g1T[0:TOK, 0].rearrange("p a b -> p (a b)")[:, D * (g % 4):D * (g % 4) + D], fin_ps[g % 2][1], ACT.Copy,
                                     scale=rsum2[:, n:n + 1]).then_inc(out_scaled, 1)

        @block.gpsimd
        def _(gp):
            n_step = [0]

            def then(ins):
                n_step[0] += 1
                ins.then_inc(g_step, 1)
                gp.wait_ge(g_step, n_step[0])

            nc.gpsimd.memset(half_neg, -0.5)
            nc.gpsimd.memset(zeros, 0.0).then_inc(consts_made, 1)
            gp.wait_ge(consts_made, 1)

            ts, tt = nc.gpsimd.tensor_scalar, nc.gpsimd.tensor_tensor

            def floor(run, dst, ti, t):
                run(nc.gpsimd.tensor_copy(ti.bitcast(i32), dst))
                run(nc.gpsimd.tensor_copy(t, ti.bitcast(i32)))
                run(tt(dst, t, dst, ALU.subtract))
                run(ts(dst, dst, 0.0, None, ALU.is_gt))
                run(tt(dst, t, dst, ALU.subtract))

            def corner_weights(run, g, first_pixel):
                pos, low, ti, t, mask = g[:, 0:2], g[:, 2:4], g[:, 4:6], g[:, 6:8], g[:, 12:13]
                near_far = g[:, 8:12].rearrange("p (e a) n -> p e a n", e=2)
                n = g.shape[2]
                run(ts(low, pos, 0.0, float(IMG - 2), ALU.max, ALU.min))
                floor(run, low, ti, t)
                run(tt(pos, pos, low, ALU.subtract))
                for e, shift in ((0, 0.0), (1, 1.0)):
                    dst = near_far[:, e]
                    run(ts(dst, pos, -1.0, 1.0 + shift, ALU.mult, ALU.add))
                    run(ts(dst, dst, 0.0, 1.0, ALU.max, ALU.min))
                    run(ts(t, pos, 1.0 - shift, None, ALU.add))
                    run(ts(t, t, 0.0, 1.0, ALU.max, ALU.min))
                    run(tt(dst, dst, t, ALU.mult))
                for e in range(2):
                    run(tt(near_far[:, e, 0:1], near_far[:, e, 0:1], mask, ALU.mult))
                run(ts(ti[:, 0], low[:, 0], float(IMG), None, ALU.mult))
                run(tt(ti[:, 0], ti[:, 0], low[:, 1], ALU.add))
                run(tt(ti[:, 0], ti[:, 0], first_pixel.broadcast_to([128, n]), ALU.add))
                for e in range(2):
                    run(tt(g[:, 2 * e:2 * e + 2], near_far[:, e, 0:1].broadcast_to([128, 2, n]), near_far[:, :, 1], ALU.mult))

            def find_offsets(ck):
                g, at, row, got = far_gen[:, ck % 2], far_at[:, ck % 2], far_row[:, ck % 2], far_off[:, ck % 2]
                gp.wait_ge(far_found, ck + 1)
                if ck >= 2:
                    gp.wait_ge(far_out[ck - 2], 16 * FAR)
                then(nc.gpsimd.tensor_copy(at, far_idx[:, ck, 0:FAR].bitcast(u32)))
                then(tt(row, at, base[:, 0:1].broadcast_to([128, FAR]), ALU.add))
                then(nc.gpsimd.tensor_copy(row.bitcast(i32), row))
                gp.wait_ge(off_stored[ck], 16)
                for k in range(FAR):
                    gp.indirect_dma_start(got[:, k, :], None, off_d[ck].rearrange("p (n a) -> (p n) a", a=2),
                                          bass.IndirectOffsetOnAxis(ap=row.bitcast(u32)[:, k:k + 1], axis=0)).then_inc(far_off_in[ck], 16)
                rows, patch = g[:, 2], g[:, 3]
                then(ts(rows, at, 1.0 / PATCH, None, ALU.mult))
                then(ts(patch, at, 1.0 / KK, None, ALU.mult))
                floor(then, g[:, 2:4], g[:, 4:6], g[:, 6:8])
                then(ts(g[:, 2:4], g[:, 2:4], float(PATCH), None, ALU.mult))
                then(ts(g[:, 0], rows, 1.0 / PATCH, None, ALU.mult))
                then(tt(g[:, 1], at, rows, ALU.subtract))
                then(tt(g[:, 0], g[:, 0], patch, ALU.subtract))
                then(tt(g[:, 1], g[:, 1], patch, ALU.add))
                then(tt(g[:, 0:2], g[:, 0:2], base[:, 2 + 2 * ck:4 + 2 * ck].unsqueeze(2).broadcast_to([128, 2, FAR]), ALU.add))
                then(ts(g[:, 12], far_val[:, ck, 0:FAR], float(RAD), None, ALU.is_gt))

            def find_pixels(ck):
                g, got = far_gen[:, ck % 2], far_off[:, ck % 2]
                gp.wait_ge(far_off_in[ck], 16 * FAR)
                then(tt(g[:, 0:2], g[:, 0:2], got.rearrange("p k a -> p a k"), ALU.add))
                corner_weights(then, g, base[:, 1:2])
                then(nc.gpsimd.tensor_copy(far_pix.bitcast(i32), g[:, 4]))
                for k in range(FAR):
                    gp.indirect_dma_start(far_quad[:, k, :], None, x_quads,
                                          bass.IndirectOffsetOnAxis(ap=far_pix.bitcast(u32)[:, k:k + 1], axis=0)).then_inc(far_quad_in[ck], 16)

            def write_samples(ck):
                g, row = far_gen[:, ck % 2], far_row[:, ck % 2]
                then(nc.gpsimd.partition_all_reduce(off_all[:, ck:ck + 1], far_val[:, ck, FAR:BEST], 128, bass.bass_isa.ReduceOp.max))
                gp.wait_ge(far_quad_in[ck], 16 * FAR)
                for c in range(C):
                    then(tt(far_wv[:, :, c], far_quad[:, :, 4 * c:4 * c + 4], g[:, 0:4].rearrange("p k n -> p n k"), ALU.mult))
                if ck:
                    gp.wait_ge(far_out[ck - 1], 16 * FAR)
                then(tt(far_s, far_wv[:, :, :, 0:2], far_wv[:, :, :, 2:4], ALU.add))
                then(tt(far_sum, far_s[:, :, :, 0], far_s[:, :, :, 1], ALU.add))
                gp.wait_ge(far_cleared[ck], 16)
                for k in range(FAR):
                    gp.indirect_dma_start(far_d[ck].rearrange("p (n c) -> (p n) c", c=C), bass.IndirectOffsetOnAxis(ap=row.bitcast(u32)[:, k:k + 1], axis=0),
                                          far_sum[:, k, :], None).then_inc(far_out[ck], 16)

            def gather_all(ck):
                count = [0]
                gp.wait_ge(off_done, HT * HT)
                gp.wait_ge(outl_in[ck], 16)

                def run(ins):
                    count[0] += 1
                    ins.then_inc(exact_step[ck], 1)
                    gp.wait_ge(exact_step[ck], count[0])

                mask, t = gen[:, 12], gen[:, 6]
                for wt in range(HT):
                    gp.dma_start(gen[:, 0:2], grid_in[ck, :, :, KK * wt:KK * wt + KK]).then_inc(grid_in_sb[ck], 16)
                    gp.wait_ge(grid_in_sb[ck], 16 * (wt + 1))
                    for a in range(2):
                        d = off[:, ck, wt, :, a]
                        run(tt(gen[:, a], gen[:, a], d, ALU.add))
                        for n, (edge, op) in enumerate(((float(RAD), ALU.is_gt), (-float(RAD), ALU.is_lt))):
                            dst = mask if a + n == 0 else t
                            run(ts(dst, d, edge, None, op))
                            if a + n:
                                run(tt(mask, mask, t, ALU.add))
                    run(ts(mask, mask, 1.0, None, ALU.min))
                    corner_weights(run, gen, base[:, 1:2])
                    tile_gathered = gathered[HT * ck + wt]
                    with gp.Fori(0, KK) as q:
                        nc.gpsimd.tensor_copy(quad_at.bitcast(i32), gen[:, 4, bass.ds(q, 1)])
                        gp.drain()
                        gp.indirect_dma_start(quad_val, None, x_quads, bass.IndirectOffsetOnAxis(ap=quad_at.bitcast(u32), axis=0)).then_inc(tile_gathered, 16)
                        gp.wait_ge(tile_gathered, (q + 1) * 16)
                        tt(quad_wv, quad_val.rearrange("p (c k) -> p c k", k=4), gen[:, 0:4, bass.ds(q, 1)].rearrange("p k o -> p o k").broadcast_to([128, C, 4]), ALU.mult)
                        gp.drain()
                        tt(quad_s, quad_wv[:, :, 0:2], quad_wv[:, :, 2:4], ALU.add)
                        gp.drain()
                        tt(outl[:, wt, bass.ds(q, 1), :].rearrange("p o c -> p c o"), quad_s[:, :, 0:1], quad_s[:, :, 1:2], ALU.add)
                        gp.drain()

            gp.wait_ge(ld_base, 16)

            def check_all(ck):
                last_far = gp.value_load(off_all[0:1, ck:ck + 1].bitcast(i32))
                with gp.If(last_far > int(np.float32(RAD).view(np.int32))):
                    gather_all(ck)
                nc.gpsimd.nop().then_inc(off_checked, 1)

            for ck in range(HT):
                find_offsets(ck)
                find_pixels(ck)
                write_samples(ck)
                check_all(ck)
            gp.wait_ge(slot_sqd, 1)
            gp.wait_ge(ld_const, 16 * CONSTS)
            then(nc.gpsimd.tensor_scalar(slot_f, slot_sq, EPS * EPS, None, ALU.max))
            then(nc.gpsimd.tensor_tensor(slot_f, slot_f, half_neg[0:SLOTS, 0:1], ALU.pow))
            then(nc.gpsimd.tensor_tensor(slot_f, slot_f, slotsc, ALU.mult))
            nc.gpsimd.tensor_tensor(slotn, slotv, slot_f.broadcast_to([SLOTS, D]), ALU.mult).then_inc(slot_nd, 1)

            for oc in range(2):
                gp.wait_ge(bn_var, oc + 1)
                then(nc.gpsimd.tensor_scalar(bn_r[:, oc:oc + 1], bn2[:, oc, 1:2], EPS, None, ALU.add))
                nc.gpsimd.tensor_tensor(bn_r[:, oc:oc + 1], bn_r[:, oc:oc + 1], half_neg[0:DC, 0:1], ALU.pow).then_inc(bn_rstd, 1)
            gp.wait_ge(samp_done, PIECES * HT)
            nc.gpsimd.memset(xlT[DC:DC + 1, :, 1, :], 1.0)
            nc.gpsimd.memset(yT[DC:DC + 1, 0], 1.0).then_inc(consts_made, 1)
            gp.wait_ge(consts_made, 2)

            def first_rstd(g):
                gp.wait_ge(s["var1_done"], g + 1)
                if g >= 4:
                    gp.wait_ge(s["xl_done"], g - 3)
                then(nc.gpsimd.tensor_scalar(r1[:, g % 4, :], mv1[:, g % 4, :, 1], EPS, None, ALU.add))
                nc.gpsimd.tensor_tensor(r1[:, g % 4, :], r1[:, g % 4, :], half_neg[0:TOK, 0:2], ALU.pow).then_inc(s["rstd1_done"], 1)

            def second_factor(g):
                gp.wait_ge(s["var2_done"], g + 1)
                then(nc.gpsimd.tensor_scalar(a2[:, g, :], mv2[:, g, :, 1], 1.0 + EPS, EPS * EPS, ALU.mult, ALU.add))
                nc.gpsimd.tensor_tensor(a2[:, g, :], a2[:, g, :], half_neg[0:TOK, 0:2], ALU.pow).then_inc(s["a2_done"], 1)

            def unit_factor(g):
                gp.wait_ge(s["ssq_done"], g + 1)
                if g >= 4:
                    gp.wait_ge(s["tok_done"], g - 3)
                gp.wait_ge(s["a2_done"], g + 1)
                then(nc.gpsimd.tensor_tensor(tmp2[:, g % 4, :], a2[:, g, :], a2[:, g, :], ALU.mult))
                then(nc.gpsimd.tensor_tensor(tmp2[:, g % 4, :], tmp2[:, g % 4, :], ssq[:, g % 4, :], ALU.mult))
                then(nc.gpsimd.tensor_scalar(tmp2[:, g % 4, :], tmp2[:, g % 4, :], EPS * EPS, None, ALU.max))
                then(nc.gpsimd.tensor_tensor(tmp2[:, g % 4, :], tmp2[:, g % 4, :], half_neg[0:TOK, 0:2], ALU.pow))
                nc.gpsimd.tensor_tensor(f2[:, g % 4, :], tmp2[:, g % 4, :], a2[:, g, :], ALU.mult).then_inc(s["f2_done"], 1)

            for stage, g in steps([(unit_factor, 5), (second_factor, 4), (first_rstd, 0)]):
                stage(g)

            for g in range(NG):
                gp.wait_ge(out_scaled, g + 1)
                n = 2 * g + 1
                nc.gpsimd.tensor_tensor(h[:, n, :], g1T[0:TOK, 0].rearrange("p a b -> p (a b)")[:, D * (g % 4):D * (g % 4) + D], h[:, n, :], ALU.add).then_inc(out_added, 1)


_OUT = (B, TOK, D)


def kernel(x, txt, L0_tok_offset_w, L0_tok_offset_b, L0_tok_dconv_w, L0_tok_bn_gamma, L0_tok_bn_beta, L0_attn_W_qkv,
           L0_attn_b_qkv, L0_ffn_slots, L0_ffn_scale, L0_ffn_fc1_weight, L0_ffn_fc1_bias, L0_ffn_fc2_weight,
           L0_ffn_fc2_bias, L0_ffn_norm_weight):
    import concourse.bacc as bacc
    from concourse.bass_utils import run_bass_kernel_spmd

    x = np.asarray(x)
    halves = 2
    padded = np.zeros((B, C, IMG + 2 * RAD, IMG + 2 * RAD), x.dtype)
    padded[:, :, RAD:RAD + IMG, RAD:RAD + IMG] = x
    wide = PATCH + 2 * RAD
    halo = np.stack([np.stack([padded[:, :, QW * hp:QW * hp + HALO, QW * wp + PATCH * wt:QW * wp + PATCH * wt + wide] for wt in range(HT)], axis=2)
                     for hp in range(2) for wp in range(2)])
    cols = x.reshape(B, C, 2, HT, halves, 8, 2, HT, PATCH).transpose(3, 5, 8, 1, 4, 7, 2, 6, 0)
    w_off = np.asarray(L0_tok_offset_w).reshape(KK, 2, C, halves, 128).transpose(4, 2, 3, 1, 0)
    w_conv = np.asarray(L0_tok_dconv_w).reshape(D, C, halves, 128).transpose(3, 1, 2, 0)
    w_qkv, b_qkv = np.asarray(L0_attn_W_qkv), np.asarray(L0_attn_b_qkv)
    i = np.arange(TOK)
    gap = i[None, :] - i[:, None]
    decay = np.where(gap >= 0, np.float32(ALPHA) ** np.maximum(gap, 0).astype(np.float32), 0) / np.sqrt(np.float32(D))
    p = np.arange(128)
    hop, wop, b = p // 64, p // 32 % 2, p % 32
    r = np.arange(PATCH)
    wt = np.arange(HT)[None, :, None, None]
    grid = np.zeros((HT, 128, 2, HT, PATCH, PATCH), np.float32)
    for ck in range(HT):
        grid[ck, :, 0] = QW * hop[:, None, None, None] + PATCH * ck + r[None, None, :, None]
        grid[ck, :, 1] = QW * wop[:, None, None, None] + PATCH * wt + r[None, None, None, :]
    base = np.stack([p * NPOS, b * IMG * IMG] + [v for ck in range(HT) for v in (QW * hop + PATCH * ck, QW * wop)], axis=1)
    beyond = np.zeros((B, C, IMG + 1, IMG + 1), x.dtype)
    beyond[:, :, :IMG, :IMG] = x
    quads = np.stack([beyond[:, :, dy:dy + IMG, dx:dx + IMG] for dy in range(2) for dx in range(2)], axis=-1).transpose(0, 2, 3, 1, 4)
    arrays = {
        "x_halo": halo.reshape(128, C, HT, HALO, wide),
        "x_cols": cols.reshape(HT, 128, KC, HT, 128),
        "x_quads": quads.reshape(B * IMG * IMG, CORN),
        "w_off": w_off.reshape(128, KC, 2 * KK),
        "b_off": np.asarray(L0_tok_offset_b).reshape(KK, 2).T.reshape(2 * KK),
        "w_conv": w_conv.reshape(128, KC, D),
        "bn_g": np.asarray(L0_tok_bn_gamma).reshape(2, DC).T,
        "bn_b": np.asarray(L0_tok_bn_beta).reshape(2, DC).T,
        "txt": np.asarray(txt),
        "wq_t": w_qkv[:, 0:D].T.reshape(2, DC, D).transpose(1, 0, 2),
        "wk_t": np.concatenate([w_qkv[:, D:2 * D].T, b_qkv[D:2 * D, None]], axis=1).reshape(2, DC, D + 1).transpose(1, 0, 2),
        "b_q": b_qkv[:D].reshape(2, DC).T,
        "w_v": w_qkv[:, 2 * D:].reshape(2, DC, D).transpose(1, 0, 2),
        "b_v": b_qkv[2 * D:],
        "slots": np.asarray(L0_ffn_slots),
        "scale": np.asarray(L0_ffn_scale).reshape(SLOTS, 1),
        "fc1": np.asarray(L0_ffn_fc1_weight).reshape(SLOTS, 2, DC, FF).transpose(0, 2, 1, 3),
        "fc1_b": np.asarray(L0_ffn_fc1_bias),
        "fc2": np.asarray(L0_ffn_fc2_weight).reshape(SLOTS, FT, 128, D).transpose(0, 2, 1, 3),
        "fc2_b": np.repeat(np.asarray(L0_ffn_fc2_bias), B, axis=0).reshape(MG, MS * B, D),
        "norm_w": np.asarray(L0_ffn_norm_weight),
        "ident_in": np.eye(128, dtype=np.float32),
        "decay_in": decay.astype(np.float32),
        "grid_in": grid.reshape(HT, 128, 2, NPOS),
        "base_in": base.astype(np.float32),
    }
    arrays = {n: np.ascontiguousarray(a) for n, a in arrays.items()}
    nc = bacc.Bacc("TRN2", target_bir_lowering=False, num_devices=1)
    args = [nc.dram_tensor(n, a.shape, mybir.dt.from_np(a.dtype), kind="ExternalInput").ap() for n, a in arrays.items()]
    off_d = [nc.dram_tensor(f"off_d{ck}", (128, 2 * NPOS), mybir.dt.float32, kind="Internal").ap() for ck in range(HT)]
    far_d = [nc.dram_tensor(f"far_d{ck}", (128, C * NPOS), mybir.dt.float32, kind="Internal").ap() for ck in range(HT)]
    out = nc.dram_tensor("out", _OUT, mybir.dt.float32, kind="ExternalOutput").ap()
    fusion_program(nc, *args, off_d, far_d, out)
    return run_bass_kernel_spmd(nc, [arrays], core_ids=[0]).results[0]["out"]
```
